# Optimizing a Trainium2 kernel written in Bass

```python
import numpy as np
import jax
import jax.numpy as jnp

def _softmax(x, axis=-1):
    return jax.nn.softmax(x, axis=axis)

def _gelu(x):
    return jax.nn.gelu(x, approximate=True)

def _silu(x):
    return jax.nn.silu(x)

def _sigmoid(x):
    return jax.nn.sigmoid(x)

def _layernorm(x, axis=-1, eps=1e-05):
    m = jnp.mean(x, axis=axis, keepdims=True)
    v = jnp.var(x, axis=axis, keepdims=True)
    return (x - m) / jnp.sqrt(v + eps)

def _scatter_add(tgt, idx, src, axis=0):
    return tgt.at[idx].add(src)

def _segment_sum(src, seg, n):
    return jax.ops.segment_sum(src, seg, n)
kernel_name = 'mk_macaron_d2_jaxref_r4_19f759'

def setup_inputs(seed: int=0):
    np.random.seed(seed)
    _w = jnp.asarray

    def _L0_attn_setup():
        import jax, jax.numpy as jnp
        import numpy as np
        H = 16

        def _eff_if_sorted(poids, Z):
            if poids.ndim == Z.ndim + 1:
                Zb = Z[..., None]
            else:
                Zb = Z
            a = jnp.cumsum(poids, axis=2)
            b = jnp.cumsum(poids * Zb, axis=2)
            return a * Zb - b
        key = jax.random.key(seed)
        ks = jax.random.split(key, 11)
        E = 256
        B, T = (4, 1024)
        s = 1.0 / np.sqrt(E)
        return {'hidden_states': jax.random.normal(ks[0], (B, T, E), jnp.float32), 'Wq': jax.random.normal(ks[1], (E, E), jnp.float32) * s, 'bq': jax.random.normal(ks[2], (E,), jnp.float32) * 0.01, 'Wk': jax.random.normal(ks[3], (E, E), jnp.float32) * s, 'bk': jax.random.normal(ks[4], (E,), jnp.float32) * 0.01, 'Wv': jax.random.normal(ks[5], (E, E), jnp.float32) * s, 'bv': jax.random.normal(ks[6], (E,), jnp.float32) * 0.01, 'W1': jax.random.normal(ks[7], (E, E), jnp.float32) * s, 'b1': jax.random.normal(ks[8], (E,), jnp.float32) * 0.01, 'W2': jax.random.normal(ks[9], (E, H), jnp.float32) * s, 'b2': jax.random.normal(ks[10], (H,), jnp.float32) * 0.01}
    _L0_attn_in = _L0_attn_setup()

    def _L0_ffn_setup():
        import jax, jax.numpy as jnp
        import numpy as np
        H = 256
        E = 8
        B, S = (4, 512)
        key = jax.random.key(seed)
        k1, k2, k3, k4 = jax.random.split(key, 4)
        x = jax.random.normal(k1, (B, S, H), dtype=jnp.float32)
        wg = jax.random.normal(k2, (H, E), dtype=jnp.float32) * 0.02
        W = jax.random.normal(k3, (E, H, H), dtype=jnp.float32) * 0.02
        b = jax.random.normal(k4, (E, H), dtype=jnp.float32) * 0.02
        return {'x': x, 'wg': wg, 'W': W, 'b': b}
    _L0_ffn_in = _L0_ffn_setup()

    def _L1_attn_setup():
        import jax, jax.numpy as jnp
        import numpy as np
        DIM = 256
        BATCH = 4
        SEQ = 1024
        key = jax.random.key(seed)
        ks = jax.random.split(key, 5)
        s = 1.0 / np.sqrt(DIM)
        x = jax.random.normal(ks[0], (BATCH, SEQ, DIM), dtype=jnp.float32)
        W_in = jax.random.uniform(ks[1], (DIM, DIM), jnp.float32, -s, s)
        b_in = jax.random.uniform(ks[2], (DIM,), jnp.float32, -s, s)
        W_out = jax.random.uniform(ks[3], (DIM, DIM), jnp.float32, -s, s)
        b_out = jax.random.uniform(ks[4], (DIM,), jnp.float32, -s, s)
        decay = jnp.float32(0.25)
        mix = jnp.float32(0.5)
        return {'x': x, 'W_in': W_in, 'b_in': b_in, 'W_out': W_out, 'b_out': b_out, 'decay': decay, 'mix': mix}
    _L1_attn_in = _L1_attn_setup()

    def _L1_ffn_setup():
        import jax, jax.numpy as jnp
        import numpy as np
        H = 256
        I = 256
        E = 8
        key = jax.random.key(seed)
        ks = jax.random.split(key, 8)
        s = 0.02
        x = jax.random.normal(ks[0], (4, 512, H), dtype=jnp.float32)
        Wg = jax.random.normal(ks[1], (H, E), dtype=jnp.float32) * s
        bg = jnp.zeros((E,), dtype=jnp.float32)
        W1 = jax.random.normal(ks[2], (E, H, I), dtype=jnp.float32) * s
        b1 = jnp.zeros((E, I), dtype=jnp.float32)
        W2 = jax.random.normal(ks[3], (E, I, H), dtype=jnp.float32) * s
        b2 = jnp.zeros((E, H), dtype=jnp.float32)
        return {'x': x, 'Wg': Wg, 'bg': bg, 'W1': W1, 'b1': b1, 'W2': W2, 'b2': b2}
    _L1_ffn_in = _L1_ffn_setup()
    _d = {'L0_attn_hidden_states': _L0_attn_in['hidden_states'], 'L0_attn_Wq': _L0_attn_in['Wq'], 'L0_attn_bq': _L0_attn_in['bq'], 'L0_attn_Wk': _L0_attn_in['Wk'], 'L0_attn_bk': _L0_attn_in['bk'], 'L0_attn_Wv': _L0_attn_in['Wv'], 'L0_attn_bv': _L0_attn_in['bv'], 'L0_attn_W1': _L0_attn_in['W1'], 'L0_attn_b1': _L0_attn_in['b1'], 'L0_attn_W2': _L0_attn_in['W2'], 'L0_attn_b2': _L0_attn_in['b2'], 'L0_ffn_wg': _L0_ffn_in['wg'], 'L0_ffn_W': _L0_ffn_in['W'], 'L0_ffn_b': _L0_ffn_in['b'], 'L1_attn_W_in': _L1_attn_in['W_in'], 'L1_attn_b_in': _L1_attn_in['b_in'], 'L1_attn_W_out': _L1_attn_in['W_out'], 'L1_attn_b_out': _L1_attn_in['b_out'], 'L1_attn_decay': _L1_attn_in['decay'], 'L1_attn_mix': _L1_attn_in['mix'], 'L1_ffn_Wg': _L1_ffn_in['Wg'], 'L1_ffn_bg': _L1_ffn_in['bg'], 'L1_ffn_W1': _L1_ffn_in['W1'], 'L1_ffn_b1': _L1_ffn_in['b1'], 'L1_ffn_W2': _L1_ffn_in['W2'], 'L1_ffn_b2': _L1_ffn_in['b2']}
    _x0 = _d['L0_attn_hidden_states']
    _d['L0_attn_hidden_states'] = jax.random.normal(jax.random.fold_in(jax.random.key(seed), 1), (2, 2048, 256), dtype=_x0.dtype)
    del _x0
    return _d

def reference(L0_attn_hidden_states, L0_attn_Wq, L0_attn_bq, L0_attn_Wk, L0_attn_bk, L0_attn_Wv, L0_attn_bv, L0_attn_W1, L0_attn_b1, L0_attn_W2, L0_attn_b2, L0_ffn_wg, L0_ffn_W, L0_ffn_b, L1_attn_W_in, L1_attn_b_in, L1_attn_W_out, L1_attn_b_out, L1_attn_decay, L1_attn_mix, L1_ffn_Wg, L1_ffn_bg, L1_ffn_W1, L1_ffn_b1, L1_ffn_W2, L1_ffn_b2):

    def _L0_attn_ref(hidden_states, Wq, bq, Wk, bk, Wv, bv, W1, b1, W2, b2):
        import jax, jax.numpy as jnp
        import numpy as np
        H = 16

        def _eff_if_sorted(poids, Z):
            if poids.ndim == Z.ndim + 1:
                Zb = Z[..., None]
            else:
                Zb = Z
            a = jnp.cumsum(poids, axis=2)
            b = jnp.cumsum(poids * Zb, axis=2)
            return a * Zb - b
        B, T, E = hidden_states.shape
        D = E // H

        def heads(x):
            return x.reshape(B, T, H, D).transpose(0, 2, 1, 3)
        q = heads(hidden_states @ Wq + bq)
        k = heads(hidden_states @ Wk + bk)
        v = heads(hidden_states @ Wv + bv)

        def proj(x4):
            x = x4.reshape(B, T, H * D)
            m = jax.nn.gelu(x @ W1 + b1, approximate=False)
            return m @ W2 + b2
        q_proj = proj(q)
        k_proj = proj(k)
        eps = 1e-06
        mean_q = jnp.mean(q_proj, axis=1, keepdims=True)
        mean_k = jnp.mean(k_proj, axis=1, keepdims=True)
        qc = q_proj - mean_q
        kc = k_proj - mean_k
        var_q = jnp.mean(qc ** 2, axis=1, keepdims=True)
        var_k = jnp.mean(kc ** 2, axis=1, keepdims=True)
        std = jnp.sqrt(0.5 * (var_q + var_k) + eps)
        q_proj = qc / std
        k_proj = kc / std
        Z = jnp.concatenate([k_proj, q_proj], axis=1).transpose(0, 2, 1)
        idx = jnp.argsort(Z, axis=2)
        Z_sort = jnp.take_along_axis(Z, idx, axis=2)
        inv = jnp.argsort(idx, axis=2)
        vc = v - jnp.mean(v, axis=2, keepdims=True)
        v_exp = jnp.concatenate([vc, jnp.zeros_like(vc)], axis=2)
        v_sorted = jnp.take_along_axis(v_exp, idx[..., None], axis=2)
        context_s = _eff_if_sorted(v_sorted, Z_sort)
        context = jnp.take_along_axis(context_s, inv[..., None], axis=2)[:, :, T:]
        v_norm = jnp.concatenate([jnp.ones((B, H, T), Z.dtype), jnp.zeros((B, H, T), Z.dtype)], axis=2)
        vns = jnp.take_along_axis(v_norm, idx, axis=2)
        sum_relu = _eff_if_sorted(vns, Z_sort)
        total_v = jnp.sum(vns, axis=2, keepdims=True)
        total_vz = jnp.sum(vns * Z_sort, axis=2, keepdims=True)
        norm_sorted = 2.0 * sum_relu - (Z_sort * total_v - total_vz)
        norm = jnp.take_along_axis(norm_sorted, inv, axis=2)[:, :, T:]
        norm = jnp.maximum(norm, 0.0001)
        context = 2.0 * context / norm[..., None]
        return context.transpose(0, 2, 1, 3).reshape(B, T, H * D)

    def _L0_ffn_ref(x, wg, W, b):
        import jax, jax.numpy as jnp
        import numpy as np
        H = 256
        E = 8
        B, S = (4, 512)
        Bb, Ss, Hh = x.shape
        Ee = wg.shape[1]
        T = Bb * Ss
        C = T // Ee
        xt = x.reshape(T, Hh)
        logits = xt @ wg
        probs = jax.nn.softmax(logits, axis=-1)
        idx = jnp.argmax(probs, axis=-1)
        mask = jax.nn.one_hot(idx, Ee, dtype=xt.dtype)
        locations = jnp.cumsum(mask, axis=0) - mask
        mask = mask * (locations < C).astype(xt.dtype)
        gate = jnp.sum(probs * mask, axis=-1)
        loc_s = jnp.sum(locations * mask, axis=-1).astype(jnp.int32)
        loc_oh = jax.nn.one_hot(loc_s, C, dtype=xt.dtype)
        dispatch = mask[:, :, None] * loc_oh[:, None, :]
        combine = gate[:, None, None] * dispatch
        exp_in = jnp.einsum('tec,th->ech', dispatch, xt)
        exp_out = jnp.einsum('ech,efh->ecf', exp_in, W) + b[:, None, :]
        out = jnp.einsum('tec,ecf->tf', combine, exp_out)
        return out.reshape(Bb, Ss, Hh)

    def _L1_attn_ref(x, W_in, b_in, W_out, b_out, decay, mix):
        import jax, jax.numpy as jnp
        import numpy as np
        DIM = 256
        BATCH = 4
        SEQ = 1024
        shifted = jnp.pad(x, ((0, 0), (1, 0), (0, 0)))[:, :-1]
        inp = mix * x + (1.0 - mix) * shifted
        h = jax.nn.relu(jnp.einsum('bsd,ed->bse', inp, W_in) + b_in)

        def step(state, h_t):
            state = state * decay + h_t
            return (state, state)
        h_t_major = jnp.swapaxes(h, 0, 1)
        _, states = jax.lax.scan(step, jnp.zeros((x.shape[0], x.shape[2]), x.dtype), h_t_major)
        states = jnp.swapaxes(states, 0, 1)
        return jnp.einsum('bsd,ed->bse', states, W_out) + b_out

    def _L1_ffn_ref(x, Wg, bg, W1, b1, W2, b2):
        import jax, jax.numpy as jnp
        import numpy as np
        H = 256
        I = 256
        E = 8
        B, S, Hd = x.shape
        xf = x.reshape(-1, Hd)
        logits = xf @ Wg + bg
        gates = jax.nn.softmax(logits, axis=-1)
        idx = jnp.argmax(gates, axis=-1)
        h = jax.nn.gelu(jnp.einsum('th,ehi->tei', xf, W1) + b1, approximate=False)
        y = jnp.einsum('tei,eih->teh', h, W2) + b2
        out = jnp.take_along_axis(y, idx[:, None, None], axis=1)[:, 0, :]
        return out.reshape(B, S, Hd)
    x = L0_attn_hidden_states
    x = x + 0.5 * _L0_ffn_ref(_layernorm(x, axis=-1), L0_ffn_wg, L0_ffn_W, L0_ffn_b)
    x = x + _L0_attn_ref(_layernorm(x, axis=-1), L0_attn_Wq, L0_attn_bq, L0_attn_Wk, L0_attn_bk, L0_attn_Wv, L0_attn_bv, L0_attn_W1, L0_attn_b1, L0_attn_W2, L0_attn_b2)
    x = x + 0.5 * _L0_ffn_ref(_layernorm(x, axis=-1), L0_ffn_wg, L0_ffn_W, L0_ffn_b)
    x = x + 0.5 * _L1_ffn_ref(_layernorm(x, axis=-1), L1_ffn_Wg, L1_ffn_bg, L1_ffn_W1, L1_ffn_b1, L1_ffn_W2, L1_ffn_b2)
    x = x + _L1_attn_ref(_layernorm(x, axis=-1), L1_attn_W_in, L1_attn_b_in, L1_attn_W_out, L1_attn_b_out, L1_attn_decay, L1_attn_mix)
    x = x + 0.5 * _L1_ffn_ref(_layernorm(x, axis=-1), L1_ffn_Wg, L1_ffn_bg, L1_ffn_W1, L1_ffn_b1, L1_ffn_W2, L1_ffn_b2)
    return x

_drawn_inputs = setup_inputs


def setup_inputs(seed=0):
    import zlib

    import numpy as np

    out = dict(_drawn_inputs(seed))
    spreads = {'L1_ffn_bg': (0.0, 0.1), 'L1_ffn_b1': (0.0, 0.436), 'L1_ffn_b2': (0.0, 0.1)}
    factors = {'L0_attn_Wq': 41.541,
     'L0_attn_bq': 200.0,
     'L0_attn_bk': 200.0,
     'L0_attn_bv': 200.0,
     'L0_attn_b1': 200.0,
     'L0_attn_b2': 200.0,
     'L0_ffn_b': 8.0,
     'L1_attn_b_in': 2.905,
     'L0_attn_Wk': 3.493,
     'L0_attn_Wv': 3.199,
     'L0_attn_W1': 3.337,
     'L0_attn_W2': 3.232}
    for name, (base, spread) in spreads.items():
        noise = np.random.default_rng([zlib.crc32(name.encode()), seed]).standard_normal(out[name].shape)
        drawn = base * np.exp(spread * noise) if base else spread * noise
        out[name] = jnp.asarray(drawn.astype(out[name].dtype))
    for name, factor in factors.items():
        out[name] = (out[name] * factor).astype(out[name].dtype)
    return out
```

```python
from contextlib import ExitStack

import numpy as np

import concourse.bass as bass
from concourse import mybir

ALU = mybir.AluOpType
ACT = mybir.ActivationFunctionType
AX_X = mybir.AxisListType.X
F32 = mybir.dt.float32
BF16 = mybir.dt.bfloat16
I32 = mybir.dt.int32

P = 128
B, S = 2, 2048
D = 256
KD = D // P
T = B * S
NT = T // P
TB = S // P
E = 8
CAP = T // E
NJ0 = T // P
NJ1 = 40
H = 16
DH = D // H
BANK = 512
LN_EPS = 1e-5
STD_EPS = 1e-6
NORM_MIN = 1e-4
PHASES = ("moe0", "attn", "moe0", "moe1", "mixer", "moe1")

VC = 2 * DH + 2
VP = 3 * VC
RING = 6
AHEAD = 5
ACT_KT = (1, 4, 6, 9, 11, 14)


class Queue:

    def __init__(self, eng, sem):
        self.eng, self.sem, self.n, self.seen = eng, sem, 0, {}

    def wait(self, *ticks):
        for tick in ticks:
            if tick is None:
                continue
            if isinstance(tick, list):
                self.wait(*tick)
                continue
            sem, value = tick
            if self.seen.get(sem.name, 0) < value:
                self.eng.wait_ge(sem, value)
                self.seen[sem.name] = value

    def done(self, instruction):
        instruction.then_inc(self.sem, 1)
        self.n += 1
        return (self.sem, self.n)

    def last(self):
        return (self.sem, self.n) if self.n else None


class Transfers:

    def __init__(self, queue, sems):
        self.queue, self.sems, self.count, self.i = queue, sems, [0] * len(sems), 0

    def start(self, issue):
        k = self.i % len(self.sems)
        self.i += 1
        self.queue.wait((self.sems[k], self.count[k]) if self.count[k] else None)
        issue().then_inc(self.sems[k], 16)
        self.count[k] += 16
        return (self.sems[k], self.count[k])

    def all(self):
        return [(s, c) for s, c in zip(self.sems, self.count) if c]


def program(nc, a, out):
    with ExitStack() as ctx:
        build(nc, ctx, a, out)


def build(nc, ctx, a, out):
    def sb(name, shape, dt=F32):
        return ctx.enter_context(nc.sbuf_tensor(name, shape, dt))

    def sem(name):
        return ctx.enter_context(nc.semaphore(name))

    pe = Queue(nc.tensor, sem("pe_done"))
    dve = Queue(nc.vector, sem("dve_done"))
    act = Queue(nc.scalar, sem("act_done"))
    pool = Queue(nc.gpsimd, sem("pool_done"))
    sp = Queue(nc.sync, sem("sp_done"))
    loads = Transfers(sp, [sem(f"load{i}") for i in range(12)])
    stores = Transfers(sp, [sem(f"store{i}") for i in range(8)])
    scatters = Transfers(pool, [sem(f"scatter{i}") for i in range(8)])
    gathers = Transfers(pool, [sem(f"gather{i}") for i in range(8)])

    def load(dst, src, *after):
        sp.wait(*after)
        return loads.start(lambda: nc.sync.dma_start(dst, src))

    def store(dst, src, *after):
        sp.wait(*after)
        return stores.start(lambda: nc.sync.dma_start(dst, src))

    slots = nc.dram_tensor("slot_rows", [2 * T, D], F32, kind="Internal").ap()
    y0 = nc.dram_tensor("moe0_rows", [NJ0 * P, D], F32, kind="Internal").ap()
    y1 = nc.dram_tensor("moe1_rows", [NJ1 * P, D], F32, kind="Internal").ap()
    zq_rows = nc.dram_tensor("q_rows", [B * H, S], F32, kind="Internal").ap()

    X = sb("residual", [P, NT, D])
    XN = sb("normed", [P, NT, D])
    XTR = sb("normed_T", [P, 3, 2, KD, P])
    STATS = sb("ln_stats", [P, 8, 6])
    MV = sb("ln_mean_var", [P, NT, 2])
    SD = sb("ln_std", [P, NT])
    RSTD = sb("ln_rstd", [P, NT])
    LG = sb("logits", [P, E, NT])
    SC = sb("score", [P, E, NT])
    OHF = sb("onehot", [P, E, NT])
    OHB = sb("onehot_bf", [P, E, NT], BF16)
    POS = sb("position", [P, E, NT])
    CUM = sb("running", [P, E, NT])
    TMP = sb("route_tmp", [P, E, NT])
    sm = {n: sb("r_" + n, [P, NT]) for n in ("max", "rank", "den", "gate", "loc", "base", "keep", "slot")}
    SLOT_S = sb("slot_scatter", [P, NT], I32)
    SLOT_G = sb("slot_gather", [P, NT], I32)
    CE = sb("tile_counts", [P, 4, E])
    EXT = sb("expert_cmp", [P, NJ1, E])
    EXF = sb("expert_f", [P, NJ1])
    EXI = sb("expert_i", [P, NJ1], I32)
    IDENT = sb("identity", [P, P])
    UTRI = sb("upper_bf", [P, P], BF16)
    ONESB = sb("ones_bf", [P, P], BF16)
    ONESF = sb("ones_f", [P, P])
    HALF = sb("half_col", [P, 1])
    EPS = sb("eps", [P, 2])
    REV = sb("rank_of_expert", [P, E])
    ECOL = sb("expert_base", [P, E])
    RESET = sb("scan_reset", [P, E, NT])
    TRASH = sb("trash_slot", [P, NT])
    M128 = sb("tile_start", [P, NT])
    JCOL = sb("tile_index", [P, NJ1])
    SCH = sb("key_scale", [P, TB, H])
    WG0 = sb("wg0", [P, KD, E])
    WG1 = sb("wg1", [P, KD, E])
    BG1 = sb("bg1", [P, E])
    ARENA_N = 31400
    ARENA = sb("arena", [P, ARENA_N])
    ZERO = XN

    psum = [ctx.enter_context(nc.psum_tensor(f"bank{i}", [P, BANK], F32)) for i in range(8)]
    bank_free = [None] * 8
    turn = [0]

    def take_bank(choice=range(6)):
        choice = list(choice)
        b = choice[turn[0] % len(choice)]
        turn[0] += 1
        pe.wait(bank_free[b])
        return b

    def carve(start, n, parts=P):
        return ARENA[0:parts, start:start + n]

    nc.gpsimd.memset(ZERO[:, :, :], 0.0)
    zeroed = pool.done(nc.gpsimd.memset(IDENT[:, :], 0.0))
    nc.gpsimd.memset(UTRI[:, :], 1.0)
    nc.gpsimd.memset(ONESB[:, :], 1.0)
    nc.gpsimd.memset(ONESF[:, :], 1.0)
    nc.gpsimd.memset(HALF[:, :], 0.5)
    nc.gpsimd.memset(EPS[:, 0:1], LN_EPS)
    nc.gpsimd.memset(EPS[:, 1:2], STD_EPS)
    nc.gpsimd.memset(RESET[:, :, :], 1.0)
    pool.wait(pool.done(nc.gpsimd.memset(SCH[:, :, :], 2.0)))
    nc.gpsimd.affine_select(out=IDENT[:, :], in_=IDENT[:, :], compare_op=ALU.not_equal, fill=1.0, base=0,
                            pattern=[[-1, P]], channel_multiplier=1)
    nc.gpsimd.affine_select(out=UTRI[:, :], in_=UTRI[:, :], compare_op=ALU.is_ge, fill=0.0, base=-1,
                            pattern=[[1, P]], channel_multiplier=-1)
    nc.gpsimd.memset(RESET[:, :, 0:1], 0.0)
    for t in ACT_KT:
        nc.gpsimd.memset(SCH[:, t, :], 1.0)
    io = lambda ap, pat, base, cm: nc.gpsimd.iota(ap, pattern=pat, base=base, channel_multiplier=cm,
                                                  allow_small_or_imprecise_dtypes=True)
    io(REV[:, :], [[-1, E]], E, 0)
    io(ECOL[:, :], [[CAP, E]], 0, 0)
    io(TRASH[:, :], [[P, NT]], T, 1)
    io(M128[:, :], [[P, NT]], 0, 0)
    consts = pool.done(io(JCOL[:, :], [[1, NJ1]], 0, 0))

    slots_zeroed = [
        store(slots[0:T, :].rearrange("(t p) d -> p t d", p=P), ZERO[:, :, :], zeroed),
        store(slots[T:NJ1 * P, :].rearrange("(t p) d -> p t d", p=P), ZERO[:, 0:NJ1 - NT, :]),
    ]
    x_rows = a["x"].rearrange("(t p) d -> p t d", p=P)
    x_ready = [None] * NT
    for g in range(4):
        tick = load(X[:, 8 * g:8 * g + 8, :], x_rows[:, 8 * g:8 * g + 8, :])
        for t in range(8 * g, 8 * g + 8):
            x_ready[t] = tick
    wg_ready = [load(WG0[:, :, :], a["wg0"].rearrange("(k p) e -> p k e", p=P)),
                load(WG1[:, :, :], a["wg1"].rearrange("(k p) e -> p k e", p=P)),
                load(BG1[:, :], a["bg1"].partition_broadcast(P))]

    st = {
        "xn_free": list(slots_zeroed),
        "slots_written": list(slots_zeroed),
        "slots_read": [],
        "y_read": [],
        "arena_free": [],
        "xtr_free": [None] * 3,
    }

    def everything():
        return [q.last() for q in (pe, dve, act, pool)] + loads.all() + stores.all() + scatters.all() + gathers.all()

    def layernorm(tiles, dest, group=8):
        groups = [tiles[i:i + group] for i in range(0, len(tiles), group)]

        def statistics(g):
            ticks = []
            for t in g:
                dve.wait(x_ready[t], bn_free[t % 8])
                ticks.append(dve.done(nc.vector.bn_stats(STATS[:, t % 8, :], X[:, t, :])))
            for t, tick in zip(g, ticks):
                dve.wait(tick)
                bn_free[t % 8] = done = dve.done(nc.vector.bn_aggr(MV[:, t, :], STATS[:, t % 8, :]))
            act.wait(done, consts)
            lo, hi = g[0], g[-1] + 1
            root = act.done(nc.scalar.activation(SD[:, lo:hi], MV[:, lo:hi, 1], ACT.Sqrt, bias=EPS[:, 0:1]))
            return lo, hi, root

        pending = statistics(groups[0])
        for i, g in enumerate(groups):
            lo, hi, root = pending
            if i + 1 < len(groups):
                pending = statistics(groups[i + 1])
            dve.wait(root)
            dve.wait(dve.done(nc.vector.reciprocal(RSTD[:, lo:hi], SD[:, lo:hi])))
            for t in g:
                yield t, dve.done(nc.vector.tensor_scalar(dest(t), X[:, t, :], MV[:, t, 0:1], RSTD[:, t:t + 1],
                                                          ALU.subtract, ALU.mult))

    bn_free = [None] * 8

    def route(kind, WG):
        dve.wait(st["xn_free"])
        logit_bank = 7
        pe.wait(bank_free[logit_bank], wg_ready, consts)
        normed = [None] * NT
        evacuated = {}

        def logits(pair):
            slot = pair % 3
            pe.wait(evacuated[pair])
            for i in range(2):
                t = 2 * pair + i
                for k in range(KD):
                    ins = nc.tensor.matmul(psum[logit_bank][:, t * E:(t + 1) * E], XTR[:, slot, i, k, :], WG[:, k, :],
                                           start=(k == 0), stop=(k == KD - 1))
            st["xtr_free"][slot] = pe.done(ins)

        for t, tick in layernorm(list(range(NT)), lambda t: XN[:, t, :]):
            normed[t] = tick
            if t % 2 == 0:
                continue
            pair = t // 2
            b = take_bank()
            pe.wait(tick)
            for i in range(2):
                for k in range(KD):
                    ins = nc.tensor.transpose(psum[b][:, (2 * i + k) * P:(2 * i + k + 1) * P],
                                              XN[:, 2 * pair + i, k * P:(k + 1) * P], IDENT[:, :])
            turned = pe.done(ins)
            act.wait(turned, st["xtr_free"][pair % 3])
            evacuated[pair] = bank_free[b] = act.done(nc.scalar.activation(
                XTR[:, pair % 3, :, :, :].rearrange("p i k c -> p (i k c)"), psum[b][:, :], ACT.Copy))
            if pair >= 1:
                logits(pair - 1)
        logits(NT // 2 - 1)
        last_logits = pe.last()

        def step(ins):
            dve.wait(dve.done(ins))

        by_tile = lambda ap: ap.rearrange("p e t -> p t e")
        over_e = lambda ap: ap.unsqueeze(1).broadcast_to([P, E, NT])
        over_t = lambda ap: ap.unsqueeze(2).broadcast_to([P, E, NT])
        dve.wait(last_logits)
        raw = psum[logit_bank][:, 0:NT * E].rearrange("p (t e) -> p e t", e=E)
        if kind == "moe1":
            step(nc.vector.tensor_tensor(LG[:, :, :], raw, over_t(BG1[:, :]), ALU.add))
        else:
            step(nc.vector.tensor_copy(LG[:, :, :], raw))
        bank_free[logit_bank] = dve.last()
        step(nc.vector.tensor_reduce(sm["max"][:, :], by_tile(LG[:, :, :]), AX_X, ALU.max))
        step(nc.vector.tensor_tensor(TMP[:, :, :], LG[:, :, :], over_e(sm["max"][:, :]), ALU.is_equal))
        step(nc.vector.tensor_tensor(SC[:, :, :], TMP[:, :, :], over_t(REV[:, :]), ALU.mult))
        step(nc.vector.tensor_reduce(sm["rank"][:, :], by_tile(SC[:, :, :]), AX_X, ALU.max))
        step(nc.vector.tensor_tensor(OHB[:, :, :], SC[:, :, :], over_e(sm["rank"][:, :]), ALU.is_equal))
        pe.wait(dve.last())
        b = take_bank()
        flat = OHB[:, :, :].rearrange("p e t -> p (e t)")
        nc.tensor.matmul(psum[b][:, 0:E * NT], UTRI[:, :], flat, start=True, stop=True)
        counted = pe.done(nc.tensor.matmul(psum[b][:, E * NT:2 * E * NT], ONESB[:, :], flat, start=True, stop=True))
        step(nc.vector.tensor_copy(OHF[:, :, :], OHB[:, :, :]))
        if kind == "moe0":
            step(nc.vector.tensor_tensor(TMP[:, :, :], LG[:, :, :], over_e(sm["max"][:, :]), ALU.subtract))
            act.wait(dve.last())
            grown = act.done(nc.scalar.activation(SC[:, :, :], TMP[:, :, :], ACT.Exp))
        before, total = psum[b][:, 0:E * NT], psum[b][:, E * NT:2 * E * NT]
        line = lambda ap: ap[:, :, :].rearrange("p e t -> p (e t)")
        dve.wait(counted)
        step(nc.vector.tensor_tensor_scan(line(CUM), line(RESET), total, 0.0, ALU.mult, ALU.add))
        step(nc.vector.tensor_tensor(line(POS), line(CUM), total, ALU.subtract))
        step(nc.vector.tensor_tensor(line(POS), line(POS), before, ALU.add))
        bank_free[b] = dve.last()
        slots_ready = {}
        if kind == "moe0":
            dve.wait(grown)
            step(nc.vector.tensor_reduce(sm["den"][:, :], by_tile(SC[:, :, :]), AX_X, ALU.add))
            step(nc.vector.tensor_tensor(TMP[:, :, :], OHF[:, :, :], POS[:, :, :], ALU.mult))
            step(nc.vector.tensor_reduce(sm["loc"][:, :], by_tile(TMP[:, :, :]), AX_X, ALU.add))
            step(nc.vector.tensor_tensor(TMP[:, :, :], OHF[:, :, :], over_t(ECOL[:, :]), ALU.mult))
            step(nc.vector.tensor_reduce(sm["base"][:, :], by_tile(TMP[:, :, :]), AX_X, ALU.add))
            step(nc.vector.tensor_scalar(sm["keep"][:, :], sm["loc"][:, :], float(CAP), None, ALU.is_lt))
            step(nc.vector.tensor_tensor(sm["slot"][:, :], sm["loc"][:, :], sm["base"][:, :], ALU.add))
            step(nc.vector.tensor_tensor(sm["base"][:, :], sm["slot"][:, :], TRASH[:, :], ALU.subtract))
            step(nc.vector.tensor_tensor(sm["base"][:, :], sm["base"][:, :], sm["keep"][:, :], ALU.mult))
            step(nc.vector.tensor_tensor(SLOT_S[:, :], sm["base"][:, :], TRASH[:, :], ALU.add))
            step(nc.vector.tensor_tensor(SLOT_G[:, :], sm["slot"][:, :], sm["keep"][:, :], ALU.mult))
            slots_ready = dve.last()
            step(nc.vector.reciprocal(sm["gate"][:, :], sm["den"][:, :]))
            step(nc.vector.tensor_tensor(sm["gate"][:, :], sm["gate"][:, :], sm["keep"][:, :], ALU.mult))
            step(nc.vector.tensor_scalar(sm["gate"][:, :], sm["gate"][:, :], 0.5, None, ALU.mult))
            return normed, slots_ready, slots_ready, None
        cnt = CUM[:, :, NT - 1:NT].broadcast_to([P, E, NT])
        step(nc.vector.tensor_tensor(TMP[:, :, :], cnt, over_e(M128[:, :]), ALU.is_gt))
        step(nc.vector.tensor_reduce(CE[:, 0, :], TMP[:, :, :], AX_X, ALU.add))
        step(nc.vector.tensor_tensor_scan(CE[:, 1, :], ONESF[:, 0:E], CE[:, 0, :], 0.0, ALU.mult, ALU.add))
        step(nc.vector.tensor_tensor(CE[:, 2, :], CE[:, 1, :], CE[:, 0, :], ALU.subtract))
        step(nc.vector.tensor_scalar(CE[:, 3, :], CE[:, 2, :], float(P), None, ALU.mult))
        step(nc.vector.tensor_tensor(POS[:, :, :], POS[:, :, :], over_t(CE[:, 3, :]), ALU.add))
        step(nc.vector.tensor_tensor(TMP[:, :, :], OHF[:, :, :], POS[:, :, :], ALU.mult))
        step(nc.vector.tensor_reduce(sm["slot"][:, :], by_tile(TMP[:, :, :]), AX_X, ALU.add))
        step(nc.vector.tensor_copy(SLOT_S[:, :], sm["slot"][:, :]))
        slots_ready = dve.last()
        step(nc.vector.tensor_tensor(EXT[:, :, :], CE[:, 1, :].unsqueeze(1).broadcast_to([P, NJ1, E]),
                                     JCOL[:, :].unsqueeze(2).broadcast_to([P, NJ1, E]), ALU.is_le))
        step(nc.vector.tensor_reduce(EXF[:, :], EXT[:, :, :], AX_X, ALU.add))
        step(nc.vector.tensor_scalar(EXI[:, :], EXF[:, :], float(E - 1), None, ALU.min))
        return normed, slots_ready, slots_ready, dve.last()

    def scatter_rows(normed, slots_ready):
        pool.wait(slots_ready, st["slots_read"], st["slots_written"], consts)
        for t in range(NT):
            pool.wait(normed[t])
            scatters.start(lambda: nc.gpsimd.indirect_dma_start(
                out=slots, out_offset=bass.IndirectOffsetOnAxis(ap=SLOT_S[:, t:t + 1], axis=0),
                in_=XN[:, t, :], in_offset=None))
        st["slots_written"] = scatters.all()
        return scatters.all()

    def gather_rows(rows, index, stored, scattered, scale):
        pool.wait(stored, scattered)
        ticks = []
        for t in range(NT):
            ticks.append(gathers.start(lambda: nc.gpsimd.indirect_dma_start(
                out=XN[:, t, :], out_offset=None, in_=rows,
                in_offset=bass.IndirectOffsetOnAxis(ap=index[:, t:t + 1], axis=0))))
        for t in range(NT):
            dve.wait(ticks[t])
            x_ready[t] = dve.done(nc.vector.scalar_tensor_tensor(
                out=X[:, t, :], in0=XN[:, t, :], scalar=scale(t), in1=X[:, t, :], op0=ALU.mult, op1=ALU.add))
        st["y_read"] = gathers.all()
        st["xn_free"] = [x_ready[NT - 1]]

    def moe0():
        WT = carve(0, KD * E * D).rearrange("p (k e f) -> p k e f", k=KD, e=E)
        BB = carve(4096, E * D).rearrange("p (e f) -> p e f", e=E)
        ring = 3
        XS = carve(6144, ring * 2 * D).rearrange("p (r i d) -> p r i d", r=ring, i=2)
        XST = carve(6144 + 1536, ring * 2 * D).rearrange("p (r i k c) -> p r i k c", r=ring, i=2, k=KD)
        YS = carve(6144 + 3072, ring * 2 * D).rearrange("p (r i d) -> p r i d", r=ring, i=2)
        weights = [load(WT[:, k, :, :], a["w0t"][:, k * P:(k + 1) * P, :].rearrange("e p f -> p e f"), st["arena_free"])
                   for k in range(KD)]
        weights.append(load(BB[:, :, :], a["b0"].partition_broadcast(P)))
        normed, slots_ready, index_ready, _ = route("moe0", WG0)
        gate_ready = dve.last()
        scattered = scatter_rows(normed, slots_ready)
        xs_free, xst_free, ys_free = [None] * ring, [None] * ring, [None] * ring
        n_pairs = NJ0 // 2
        rows = lambda ap, j: ap[2 * j * P:2 * (j + 1) * P, :].rearrange("(i p) d -> p i d", p=P)
        xs_ready, xst_ready, stored = {}, {}, []

        def fetch(j):
            xs_ready[j] = load(XS[:, j % ring, :, :], rows(slots, j), scattered, xs_free[j % ring])

        def turn_pair(j):
            b = take_bank()
            pe.wait(xs_ready[j])
            for i in range(2):
                for k in range(KD):
                    ins = nc.tensor.transpose(psum[b][:, (2 * i + k) * P:(2 * i + k + 1) * P],
                                              XS[:, j % ring, i, k * P:(k + 1) * P], IDENT[:, :])
            xs_free[j % ring] = pe.done(ins)
            act.wait(pe.last(), xst_free[j % ring], st["arena_free"])
            xst_ready[j] = bank_free[b] = act.done(nc.scalar.activation(
                XST[:, j % ring, :, :, :].rearrange("p i k c -> p (i k c)"), psum[b][:, :], ACT.Copy))

        def expert_pair(j):
            e = (2 * j) // (CAP // P)
            b = take_bank()
            pe.wait(xst_ready[j], weights)
            for i in range(2):
                for k in range(KD):
                    ins = nc.tensor.matmul(psum[b][:, i * D:(i + 1) * D], XST[:, j % ring, i, k, :], WT[:, k, e, :],
                                           start=(k == 0), stop=(k == KD - 1))
            xst_free[j % ring] = pe.done(ins)
            dve.wait(pe.last(), ys_free[j % ring], weights, st["arena_free"])
            bank_free[b] = dve.done(nc.vector.tensor_tensor(
                YS[:, j % ring, :, :], psum[b][:, :].rearrange("p (i f) -> p i f", i=2),
                BB[:, e, :].unsqueeze(1).broadcast_to([P, 2, D]), ALU.add))
            ys_free[j % ring] = store(rows(y0, j), YS[:, j % ring, :, :], bank_free[b], st["y_read"])
            stored.append(ys_free[j % ring])

        for j in range(min(2, n_pairs)):
            fetch(j)
        turn_pair(0)
        for j in range(n_pairs):
            if j + 2 < n_pairs:
                fetch(j + 2)
            if j + 1 < n_pairs:
                turn_pair(j + 1)
            expert_pair(j)
        st["slots_read"] = list(xs_ready.values())[-12:]
        dve.wait(gate_ready)
        pool.wait(index_ready)
        gather_rows(y0, SLOT_G, stored[-8:], scattered, lambda t: sm["gate"][:, t:t + 1])

    L1 = 10752

    def moe1():
        at = [L1]

        def part(n, parts=P):
            at[0] += n
            assert at[0] <= ARENA_N
            return carve(at[0] - n, n, parts)

        ring = 3
        W1 = part(KD * E * D).rearrange("p (k n) -> p k n", k=KD)
        W2 = part(KD * E * D).rearrange("p (k n) -> p k n", k=KD)
        B3 = [part(E * D // 2, 3).bitcast(BF16) for _ in range(2)]
        XS = part(ring * 2 * D).rearrange("p (r i d) -> p r i d", r=ring, i=2)
        XST = part(ring * 2 * D).rearrange("p (r i k c) -> p r i k c", r=ring, i=2, k=KD)
        HS = part(ring * 2 * D).rearrange("p (r i d) -> p r i d", r=ring, i=2)
        HT = part(ring * 2 * D).rearrange("p (r i k c) -> p r i k c", r=ring, i=2, k=KD)
        YS = part(ring * 2 * D).rearrange("p (r i d) -> p r i d", r=ring, i=2)
        w_of = lambda name, k: a[name][:, k * P:(k + 1) * P, :].rearrange("e p f -> p e f")
        weights = [load(W[:, k, :].rearrange("p (e f) -> p e f", e=E), w_of(name, k), st["arena_free"])
                   for W, name in ((W1, "w1"), (W2, "w2")) for k in range(KD)]
        BR = carve(L1 + 2 * KD * E * D + E * D, E * D, 1)
        PART = carve(L1 + 2 * KD * E * D + 2 * E * D, E * D // 2, 1).bitcast(BF16)
        for n, name in enumerate(("b1", "b2")):
            got = load(BR, a[name], st["arena_free"], dve.last() if n else None)
            dve.wait(got, st["arena_free"])
            for i in range(3):
                dve.wait(dve.done(nc.vector.tensor_copy(PART, BR)))
                placed = load(B3[n][i:i + 1, :], PART, dve.last())
                if i < 2:
                    dve.wait(dve.done(nc.vector.tensor_tensor(BR, BR, PART, ALU.subtract)))
                dve.wait(placed)
                weights.append(placed)
        scratch_free = weights[-1]
        normed, slots_ready, index_ready, experts_ready = route("moe1", WG1)
        scattered = scatter_rows(normed, slots_ready)
        n_pairs = NJ1 // 2
        rows = lambda ap, j: ap[2 * j * P:2 * (j + 1) * P, :].rearrange("(i p) d -> p i d", p=P)
        free = {n: [None] * ring for n in ("xs", "xst", "hs", "ht", "ys")}
        ready = {n: {} for n in ("xs", "xst", "hs", "ht")}
        stored, column = [], {}
        act.wait(scratch_free)
        dve.wait(scratch_free)

        def fetch(j):
            ready["xs"][j] = load(XS[:, j % ring, :, :], rows(slots, j), scattered, free["xs"][j % ring], scratch_free)

        def turn_pair(j, src, dst, SRC, DST, copy):
            r = j % ring
            b = take_bank()
            pe.wait(ready[src][j])
            for i in range(2):
                for k in range(KD):
                    ins = nc.tensor.transpose(psum[b][:, (2 * i + k) * P:(2 * i + k + 1) * P],
                                              SRC[:, r, i, k * P:(k + 1) * P], IDENT[:, :])
            free[src][r] = pe.done(ins)
            ready[dst][j] = bank_free[b] = copy(DST[:, r, :, :, :].rearrange("p i k c -> p (i k c)"), psum[b][:, :],
                                                pe.last(), free[dst][r])

        def copy_act(o, i, *after):
            act.wait(*after)
            return act.done(nc.scalar.activation(o, i, ACT.Copy))

        def copy_dve(o, i, *after):
            dve.wait(*after)
            return dve.done(nc.vector.tensor_copy(o, i))

        def layer(j, SRC, W, bias, src):
            r = j % ring
            b = take_bank()
            pe.wait(ready[src][j], weights)
            for i in range(2):
                if (j, i) not in column:
                    pe.wait(experts_ready)
                    column[j, i] = nc.tensor.value_load(EXI[0:1, 2 * j + i:2 * j + i + 1], min_val=0, max_val=E - 1) * D
                where = bass.ds(column[j, i], D)
                for k in range(KD):
                    nc.tensor.matmul(psum[b][:, i * D:(i + 1) * D], SRC[:, r, i, k, :], W[:, k, where],
                                     start=(k == 0), stop=False)
                ins = nc.tensor.matmul(psum[b][:, i * D:(i + 1) * D], ONESB[0:3, :], bias[:, where],
                                       start=False, stop=True)
            free[src][r] = pe.done(ins)
            return b

        def first(j):
            b = layer(j, XST, W1, B3[0], "xst")
            act.wait(pe.last(), free["hs"][j % ring])
            ready["hs"][j] = bank_free[b] = act.done(nc.scalar.activation(
                HS[:, j % ring, :, :].rearrange("p i d -> p (i d)"), psum[b][:, :], ACT.Gelu))

        def second(j):
            b = layer(j, HT, W2, B3[1], "ht")
            dve.wait(pe.last(), free["ys"][j % ring])
            bank_free[b] = dve.done(nc.vector.tensor_copy(YS[:, j % ring, :, :].rearrange("p i d -> p (i d)"),
                                                          psum[b][:, :]))
            free["ys"][j % ring] = store(rows(y1, j), YS[:, j % ring, :, :], bank_free[b], st["y_read"])
            stored.append(free["ys"][j % ring])

        for j in range(n_pairs + 3):
            if j < n_pairs:
                fetch(j)
            if 0 <= j - 1 < n_pairs:
                turn_pair(j - 1, "xs", "xst", XS, XST, copy_act)
            if 0 <= j - 2 < n_pairs:
                first(j - 2)
            if 0 <= j - 3 < n_pairs:
                turn_pair(j - 3, "hs", "ht", HS, HT, copy_dve)
                second(j - 3)
        st["slots_read"] = list(ready["xs"].values())[-12:]
        pool.wait(index_ready)
        gather_rows(y1, SLOT_S, stored[-8:], scattered, lambda t: 0.5)

    def transposed(batch, XT, xt_free):
        LNR = XTR[:, :, :, :, :].rearrange("p r i k c -> p r i (k c)")
        ticks = [None] * TB
        act.wait(xt_free)
        dve.wait(st["xn_free"])

        def dest(t):
            pair = (t - batch * TB) // 2
            dve.wait(st["xtr_free"][pair % 3])
            return LNR[:, pair % 3, t % 2, :]

        for t, tick in layernorm(list(range(batch * TB, (batch + 1) * TB)), dest):
            if t % 2 == 0:
                continue
            pair = (t - batch * TB) // 2
            b = take_bank()
            pe.wait(tick, consts)
            for i in range(2):
                for k in range(KD):
                    ins = nc.tensor.transpose(psum[b][:, (2 * k + i) * P:(2 * k + i + 1) * P],
                                              LNR[:, pair % 3, i, k * P:(k + 1) * P], IDENT[:, :])
            st["xtr_free"][pair % 3] = pe.done(ins)
            act.wait(pe.last())
            bank_free[b] = act.done(nc.scalar.activation(
                XT[:, :, 2 * pair * P:2 * (pair + 1) * P], psum[b][:, :].rearrange("p (k c) -> p k c", k=KD), ACT.Copy))
            ticks[2 * pair] = ticks[2 * pair + 1] = bank_free[b]
        return ticks

    def attention():
        xn = XN[:, :, :].rearrange("p t d -> p (t d)")
        XT = xn[:, 0:4096].rearrange("p (k n) -> p k n", k=KD)
        PT = xn[:, 4096:6144].rearrange("p (r m n) -> p r m n", r=2, m=KD)
        GT = xn[:, 6144:8192].rearrange("p (r m n) -> p r m n", r=2, m=KD)
        at = [0]

        def part(n, parts=P):
            at[0] += n
            assert at[0] <= ARENA_N, at[0]
            return carve(at[0] - n, n, parts)

        VOP_F = part(TB * H * VP // 2)
        VOP = VOP_F.bitcast(BF16).rearrange("p (t h c) -> p t h c", t=TB, h=H)
        signs_flat = part(RING * S // 2)
        SG = signs_flat.bitcast(BF16).rearrange("p (r n) -> p r n", r=RING)
        U = signs_flat[:, 0:2 * 4 * H * VC].rearrange("p (r t h c) -> p r t h c", r=2, t=4, h=H)
        QB = part(2 * S).rearrange("p (r n) -> p r n", r=2)
        Z = QB[0:H, :, :]
        HM = VOP_F[:, 0:2 * H * D].rearrange("p (s h l d) -> p s h l d", s=2, h=H, l=S // P)
        OS = part(S)
        QTM = part(TB * H).rearrange("p (t h) -> p t h", t=TB)
        KTM = part(TB * H).rearrange("p (t h) -> p t h", t=TB)
        NKT = part(TB * H).rearrange("p (t h) -> p t h", t=TB)
        A = part(2 * TB * VC).rearrange("p (r t c) -> p r t c", r=2, t=TB)
        BQK = A[:, 0, :, :].rearrange("p t c -> p (t c)")[:, 0:2 * D].rearrange("p (s d) -> p s d", s=2)
        N1 = part(2 * TB).rearrange("p (r t) -> p r t", r=2)
        N2 = part(2 * TB).rearrange("p (r t) -> p r t", r=2)
        CT = part(TB * DH).rearrange("p (t d) -> p t d", t=TB)
        WATT = {n: part(KD * D).rearrange("p (k n) -> p k n", k=KD) for n in ("wq", "wk", "wv", "wp1")}
        WP2 = part(KD * H).rearrange("p (k n) -> p k n", k=KD)
        BP1 = part(KD)
        BP2 = part(1, H)
        BVB = part(D)
        ROW = part(2 * D).rearrange("p (s d) -> p s d", s=2)
        MEANS = part(KD)
        MB = part(KD * P).rearrange("p (k c) -> p k c", k=KD)
        ZST = part(2 * 4 * 6, H).rearrange("p (s c x) -> p s c x", s=2, c=4)
        ZMV = part(2 * 2, H).rearrange("p (s x) -> p s x", s=2)
        ZS = part(3, H)
        TOT = part(H * 2 * DH, 1)
        CB = part(H, VP)

        free = st["arena_free"]
        wt = []
        for n in ("wq", "wk", "wv", "wp1"):
            wt.append(load(WATT[n], a[n].rearrange("(k p) n -> p k n", p=P), free))
        wt.append(load(WP2, a["wp2"].rearrange("(k p) n -> p k n", p=P), free))
        wt.append(load(BP1, a["bp1"], free))
        wt.append(load(BP2, a["bp2"], free))
        wt.append(load(BVB, a["bv"].partition_broadcast(P), free))
        for q in (pe, dve, act):
            q.wait(wt, free)
        pool.wait(free)
        cb_zero = pool.done(nc.gpsimd.memset(CB, 0.0))

        qb_ready, head_done = {}, {}
        pe_tile = {}
        sign_made = {}
        bank_of = lambda hh, c: (4 * hh + c) % 6
        evac = {}
        os_free, a_free, ct_free = [None], [[None], [None]], [None]
        prep_done = [None]

        def prepare(batch):
            bias_rows = [load(BQK[:, n, :], a[name].partition_broadcast(P), free, pool.last())
                         for n, name in enumerate(("bq", "bk"))]
            xt = transposed(batch, XT, pe.last())
            dve.wait(xt[TB - 1])
            dve.wait(dve.done(nc.vector.tensor_reduce(MEANS, XT[:, :, :], AX_X, ALU.add)))
            for k in range(KD):
                mb = dve.done(nc.vector.tensor_scalar(MB[:, k, :], ONESF[:, :], MEANS[:, k:k + 1], 1.0 / S,
                                                      ALU.mult, ALU.mult))
            z_ready = {}
            nchunk = S // BANK
            pt_free, gt_free = [None, None], [None, None]
            steps = [(s, c) for s in range(2) for c in range(nchunk)]
            pt_ready, gt_ready = {}, {}
            vop_read = pe.last()
            z_free = [sign_made.get(k) for k in list(sign_made)[-16:]]

            by_head = {}

            def project(s):
                W = WATT["wq"] if s == 0 else WATT["wk"]
                dve.wait(bias_rows, vop_read)
                for l in range(0, S // P, 2):
                    b = take_bank()
                    for i in range(2):
                        for k in range(KD):
                            tokens = XT[:, k, :].rearrange("p (n l) -> p l n", l=S // P)[:, l + i, :]
                            ins = nc.tensor.matmul(psum[b][:, i * D:(i + 1) * D], tokens, W[:, k, :],
                                                   start=(k == 0), stop=(k == KD - 1))
                    dve.wait(pe.done(ins))
                    bank_free[b] = by_head[s] = dve.done(nc.vector.tensor_tensor(
                        HM[:, s, :, l:l + 2, :].rearrange("p h l d -> p l h d"),
                        psum[b][:, :].rearrange("p (l h d) -> p l h d", l=2, h=H),
                        BQK[:, s, :].rearrange("p (h d) -> p h d", h=H).unsqueeze(1).broadcast_to([P, 2, H, DH]), ALU.add))

            def turn_rows(i):
                s, c = steps[i]
                pe.wait(by_head[s])
                for half in range(2):
                    b = take_bank()
                    for j in range(2):
                        row = HM[:, s, 4 * c + 2 * half + j, :, :].rearrange("p l d -> p (l d)")
                        for k in range(KD):
                            ins = nc.tensor.transpose(psum[b][:, (2 * k + j) * P:(2 * k + j + 1) * P],
                                                      row[:, k * P:(k + 1) * P], IDENT[:, :])
                    act.wait(pe.done(ins), pt_free[i % 2])
                    bank_free[b] = pt_ready[i] = act.done(nc.scalar.activation(
                        PT[:, i % 2, :, half * 2 * P:(half + 1) * 2 * P],
                        psum[b][:, :].rearrange("p (k c) -> p k c", k=KD), ACT.Copy))

            def hidden(i):
                pe.wait(pt_ready[i])
                for m in range(KD):
                    b = take_bank()
                    for k in range(KD):
                        ins = nc.tensor.matmul(psum[b][:, :], WATT["wp1"][:, k, m * P:(m + 1) * P], PT[:, i % 2, k, :],
                                               start=(k == 0), stop=(k == KD - 1))
                    act.wait(pe.done(ins), gt_free[i % 2])
                    bank_free[b] = gt_ready[i] = act.done(nc.scalar.activation(
                        GT[:, i % 2, m, :], psum[b][:, :], ACT.Gelu, bias=BP1[:, m:m + 1]))
                pt_free[i % 2] = pe.last()

            def score(i):
                s, c = steps[i]
                pe.wait(gt_ready[i])
                b = take_bank()
                for k in range(KD):
                    ins = nc.tensor.matmul(psum[b][0:H, :], WP2[:, k, :], GT[:, i % 2, k, :],
                                           start=(k == 0), stop=(k == KD - 1))
                gt_free[i % 2] = pe.done(ins)
                dve.wait(pe.last(), z_free)
                bank_free[b] = dve.done(nc.vector.tensor_scalar(Z[:, s, c * BANK:(c + 1) * BANK], psum[b][0:H, :],
                                                                BP2[:, 0:1], None, ALU.add))
                dve.wait(bank_free[b])
                z_ready[s] = dve.done(nc.vector.bn_stats(ZST[:, s, c, :], Z[:, s, c * BANK:(c + 1) * BANK]))

            for i in range(len(steps) + 2):
                if i < len(steps):
                    if i == 0:
                        pe.wait(xt)
                        project(0)
                        project(1)
                    turn_rows(i)
                if 0 <= i - 1 < len(steps):
                    hidden(i - 1)
                if 0 <= i - 2 < len(steps):
                    score(i - 2)
            dve.wait(z_ready[0], z_ready[1])
            for s in range(2):
                mv = dve.done(nc.vector.bn_aggr(ZMV[:, s, :], ZST[:, s, :, :].rearrange("p c x -> p (c x)")))
            dve.wait(mv)
            both = dve.done(nc.vector.tensor_tensor(ZS[:, 0:1], ZMV[:, 0, 1:2], ZMV[:, 1, 1:2], ALU.add))
            act.wait(both)
            root = act.done(nc.scalar.activation(ZS[:, 1:2], ZS[:, 0:1], ACT.Sqrt, bias=EPS[0:H, 1:2], scale=0.5))
            dve.wait(root)
            dve.wait(dve.done(nc.vector.reciprocal(ZS[:, 2:3], ZS[:, 1:2])))
            for s in range(2):
                scaled = dve.done(nc.vector.tensor_scalar(Z[:, s, :], Z[:, s, :], ZMV[:, s, 0:1], ZS[:, 2:3],
                                                          ALU.subtract, ALU.mult))
                if s == 0:
                    q_stored = store(zq_rows[batch * H:(batch + 1) * H, :], Z[:, 0, :], scaled, loads.all())
            pe.wait(scaled)
            for s, M in ((0, QTM), (1, KTM)):
                b = take_bank()
                for t in range(TB):
                    ins = nc.tensor.transpose(psum[b][:, t * H:(t + 1) * H], Z[:, s, t * P:(t + 1) * P], IDENT[0:H, 0:H])
                dve.wait(pe.done(ins), pool.last())
                bank_free[b] = dve.done(nc.vector.tensor_copy(M.rearrange("p t h -> p (t h)"), psum[b][:, 0:TB * H]))
            dve.wait(bank_free[b])
            nkt = dve.done(nc.vector.tensor_scalar(NKT.rearrange("p t h -> p (t h)"), KTM.rearrange("p t h -> p (t h)"),
                                                   -1.0, None, ALU.mult))
            z_read = [pe.last(), q_stored]
            b = take_bank()
            pe.wait(mb)
            for k in range(KD):
                ins = nc.tensor.matmul(psum[b][:, 0:D], MB[:, k, :], WATT["wv"][:, k, :], start=(k == 0), stop=(k == KD - 1))
            dve.wait(pe.done(ins))
            bank_free[b] = dve.done(nc.vector.tensor_tensor(ROW[:, 1, :], psum[b][:, 0:D], BVB, ALU.add))
            dve.wait(bank_free[b])
            dve.wait(dve.done(nc.vector.tensor_tensor(ROW[:, 0, :], BVB, ROW[:, 1, :], ALU.subtract)))
            dve.wait(dve.done(nc.vector.tensor_scalar(ROW[:, 1, :], ROW[:, 0, :], 2.0, None, ALU.mult)))
            tot = 7
            pe.wait(bank_free[tot])
            u_free = [[None], [None]]
            vop_free = pe.last()
            parts_done = []
            for g in range(TB // 4):
                r = g % 2
                dve.wait(u_free[r])
                if g < 2:
                    dve.wait(pe.last())
                for half in range(2):
                    b = take_bank()
                    for i in range(2):
                        t = 4 * g + 2 * half + i
                        for k in range(KD):
                            ins = nc.tensor.matmul(psum[b][:, i * D:(i + 1) * D], XT[:, k, t * P:(t + 1) * P], WATT["wv"][:, k, :],
                                                   start=(k == 0), stop=(k == KD - 1))
                    dve.wait(pe.done(ins))
                    for i in range(2):
                        t = 4 * g + 2 * half + i
                        two = t not in ACT_KT
                        bank_free[b] = dve.done(nc.vector.scalar_tensor_tensor(
                            out=U[:, r, 2 * half + i, :, 0:DH],
                            in0=psum[b][:, i * D:(i + 1) * D].rearrange("p (h d) -> p h d", h=H),
                            scalar=2.0 if two else 1.0,
                            in1=ROW[:, int(two), :].rearrange("p (h d) -> p h d", h=H),
                            op0=ALU.mult, op1=ALU.add))
                dve.wait(bank_free[b])
                tt = slice(4 * g, 4 * g + 4)
                nc.vector.tensor_tensor(U[:, r, :, :, DH:2 * DH], U[:, r, :, :, 0:DH],
                                        KTM[:, tt, :].unsqueeze(3).broadcast_to([P, 4, H, DH]), ALU.mult)
                nc.vector.tensor_copy(U[:, r, :, :, 2 * DH], SCH[:, tt, :])
                whole = dve.done(nc.vector.tensor_tensor(U[:, r, :, :, 2 * DH + 1], KTM[:, tt, :], SCH[:, tt, :], ALU.mult))
                pe.wait(whole)
                for i in range(4):
                    t = 4 * g + i
                    weight = ONESF[:, 0:1] if t in ACT_KT else HALF[:, :]
                    ins = nc.tensor.matmul(psum[tot][0:1, :], weight, U[:, r, i, :, 0:2 * DH],
                                           start=(t == 0), stop=(t == TB - 1))
                summed = pe.done(ins)
                rows = lambda n: VOP[:, tt, :, n * VC:(n + 1) * VC].rearrange("p t h c -> p (t h) c")
                u = U[:, r, :, :, :].rearrange("p t h c -> p (t h) c")
                act.wait(whole, vop_free)
                hi = act.done(nc.scalar.activation(rows(0), u, ACT.Copy))
                dve.wait(hi, summed)
                rest = dve.done(nc.vector.tensor_tensor(u, u, rows(0), ALU.subtract))
                act.wait(rest)
                mid = act.done(nc.scalar.activation(rows(1), u, ACT.Copy))
                dve.wait(mid)
                lo = dve.done(nc.vector.tensor_tensor(rows(2), u, rows(1), ALU.subtract))
                u_free[r] = [lo]
                parts_done += [mid, lo]
            dve.wait(summed)
            bank_free[tot] = dve.done(nc.vector.tensor_copy(TOT, psum[tot][0:1, :]))
            b = take_bank()
            pe.wait(bank_free[tot])
            for h in range(H):
                ins = nc.tensor.matmul(psum[b][0:2 * DH, h:h + 1], TOT[:, h * 2 * DH:(h + 1) * 2 * DH], ONESF[0:1, 0:1],
                                       start=True, stop=True)
            dve.wait(pe.done(ins), cb_zero, act.last())
            bank_free[b] = dve.done(nc.vector.tensor_copy(CB[0:2 * DH, :], psum[b][0:2 * DH, 0:H]))
            return dict(q_stored=q_stored, z_read=z_read, nkt=nkt, parts=parts_done, cb=bank_free[b])

        def spread_q(hh, info):
            last = [sign_made[k] for k in sign_made if hh - 2 >= 0 and k // TB == hh - 2]
            act_dve = last + (info["z_read"] if hh % H < 2 else [])
            qb_ready[hh] = load(QB[:, hh % 2, :], zq_rows[hh, :].partition_broadcast(P), info["q_stored"], act_dve)

        def sign_tile(hh, kt, info):
            g = hh * TB + kt
            h = hh % H
            after = [qb_ready[hh], pe_tile.get(g - RING)]
            if kt in ACT_KT:
                act.wait(after, info["nkt"], info["parts"])
                sign_made[g] = act.done(nc.scalar.activation(SG[:, g % RING, :], QB[:, hh % 2, :], ACT.Sign,
                                                             bias=NKT[:, kt, h:h + 1]))
            else:
                dve.wait(after, info["nkt"], info["parts"])
                sign_made[g] = dve.done(nc.vector.tensor_scalar(SG[:, g % RING, :], QB[:, hh % 2, :], KTM[:, kt, h:h + 1],
                                                                0.5, ALU.is_gt, ALU.subtract))

        def accumulate(hh, kt, chunks, info):
            g = hh * TB + kt
            pe.wait(sign_made[g], info["parts"])
            for c in chunks:
                b = bank_of(hh, c)
                if kt == 0:
                    pe.wait(bank_free[b])
                ins = nc.tensor.matmul(psum[b][0:VP, :], VOP[:, kt, hh % H, :], SG[:, g % RING, c * BANK:(c + 1) * BANK],
                                       start=(kt == 0), stop=(kt == TB - 1))
            if chunks[-1] == 3:
                pe_tile[g] = pe.done(ins)

        def evacuate(hh, info):
            for c in range(4):
                b = bank_of(hh, c)
                act.wait(pe_tile[hh * TB + TB - 1], os_free[0], info["cb"])
                evac[hh, c] = bank_free[b] = act.done(nc.scalar.activation(
                    OS[0:VP, c * BANK:(c + 1) * BANK], psum[b][0:VP, :], ACT.Identity, bias=CB[:, hh % H:hh % H + 1]))

        turned, summed = {}, {}

        def turn_back(hh, c):
            b = 6 + c % 2
            pe.wait(evac[hh, c], bank_free[b])
            for i in range(4):
                ins = nc.tensor.transpose(psum[b][:, i * VP:(i + 1) * VP], OS[0:VP, (4 * c + i) * P:(4 * c + i + 1) * P],
                                          IDENT[0:VP, 0:VP])
            turned[hh, c] = pe.done(ins)
            if c == 3:
                os_free[0] = turned[hh, c]

        def sum_parts(hh, c):
            b = 6 + c % 2
            dve.wait(turned[hh, c], a_free[hh % 2])
            summed[hh, c] = bank_free[b] = dve.done(nc.vector.tensor_reduce(
                A[:, hh % 2, 4 * c:4 * c + 4, :],
                psum[b][:, 0:4 * VP].rearrange("p (i n c) -> p i c n", i=4, n=3), AX_X, ALU.add))

        norm = {}

        def norm_first(hh):
            r = hh % 2
            pool.wait(summed[hh, 3])
            q = QTM[:, :, hh % H]
            pool.wait(pool.done(nc.gpsimd.tensor_tensor(N1[:, r, :], A[:, r, :, 2 * DH], q, ALU.mult)))
            norm[hh] = pool.done(nc.gpsimd.tensor_tensor(N2[:, r, :], N1[:, r, :], A[:, r, :, 2 * DH + 1], ALU.subtract))
            pool.wait(pool.done(nc.gpsimd.tensor_tensor(CT, A[:, r, :, 0:DH], q.unsqueeze(2).broadcast_to([P, TB, DH]),
                                                        ALU.mult)))
            pool.wait(pool.done(nc.gpsimd.tensor_tensor(CT, CT, A[:, r, :, DH:2 * DH], ALU.subtract)))

        def norm_second(hh):
            r = hh % 2
            dve.wait(norm[hh])
            dve.wait(dve.done(nc.vector.tensor_scalar(N2[:, r, :], N2[:, r, :], NORM_MIN, None, ALU.max)))
            norm[hh] = dve.done(nc.vector.reciprocal(N1[:, r, :], N2[:, r, :]))

        def add_context(hh):
            r, batch, h = hh % 2, hh // H, hh % H
            pool.wait(norm[hh])
            pool.wait(pool.done(nc.gpsimd.tensor_tensor(CT, CT, N1[:, r, :].unsqueeze(2).broadcast_to([P, TB, DH]), ALU.mult)))
            x = X[:, batch * TB:(batch + 1) * TB, h * DH:(h + 1) * DH]
            a_free[r] = [pool.done(nc.gpsimd.tensor_tensor(x, x, CT, ALU.add))]
            pool.wait(a_free[r])

        def after_head(hh, kt):
            if kt in (6, 8, 10, 12):
                turn_back(hh, (kt - 6) // 2)
            if kt in (7, 9, 11, 13):
                sum_parts(hh, (kt - 7) // 2)
            if kt == 13:
                norm_first(hh)
            if kt == 15:
                norm_second(hh)
                add_context(hh)

        for batch in range(B):
            info = prepare(batch)
            heads = range(batch * H, (batch + 1) * H)
            spread_q(heads[0], info)
            for hh in heads:
                for kt in range(AHEAD):
                    sign_tile(hh, kt, info)
                if hh > heads[0]:
                    evacuate(hh - 1, info)
                if hh + 1 in heads:
                    spread_q(hh + 1, info)
                for chunks in ((0, 1), (2, 3)):
                    for kt in range(3):
                        accumulate(hh, kt, chunks, info)
                for kt in range(3, TB):
                    if kt - 3 + AHEAD < TB:
                        sign_tile(hh, kt - 3 + AHEAD, info)
                    accumulate(hh, kt, (0, 1, 2, 3), info)
                    if hh > heads[0]:
                        after_head(hh - 1, kt)
            evacuate(heads[-1], info)
            for kt in range(TB):
                after_head(heads[-1], kt)
            for t in range(batch * TB, (batch + 1) * TB):
                x_ready[t] = pool.last()
        st["xn_free"] = [pe.last(), act.last()]

    def mixer():
        xn = XN[:, :, :].rearrange("p t d -> p (t d)")
        XT = xn[:, 0:4096].rearrange("p (k n) -> p k n", k=KD)
        INP = xn[:, 4096:8192].rearrange("p (k n) -> p k n", k=KD)
        at = [0]

        def part(n, parts=P):
            at[0] += n
            assert at[0] <= ARENA_N, at[0]
            return carve(at[0] - n, n, parts)

        SHIFT = part(KD * (S + 1)).rearrange("p (k n) -> p k n", k=KD)
        HT = part(KD * S).rearrange("p (k n) -> p k n", k=KD)
        STATE = part(KD * S).rearrange("p (k n) -> p k n", k=KD)
        WIN = part(KD * D).rearrange("p (k n) -> p k n", k=KD)
        WOUT = part(KD * D).rearrange("p (k n) -> p k n", k=KD)
        BIN = part(KD)
        BOUT = part(D)
        SCAL = part(3)
        TMPO = part(4 * 2 * D).rearrange("p (r i d) -> p r i d", r=4, i=2)
        free = st["arena_free"]
        wt = [load(WIN, a["win_t"].rearrange("(k p) n -> p k n", p=P), free),
              load(WOUT, a["wout_t"].rearrange("(k p) n -> p k n", p=P), free),
              load(BIN, a["bin"], free),
              load(BOUT, a["bout"].partition_broadcast(P), free),
              load(SCAL[:, 0:1], a["decay"].partition_broadcast(P), free),
              load(SCAL[:, 1:2], a["mix"].partition_broadcast(P), free)]
        for q in (pe, dve, act):
            q.wait(wt, free)
        dve.wait(dve.done(nc.vector.tensor_scalar(SCAL[:, 2:3], SCAL[:, 1:2], -1.0, 1.0, ALU.mult, ALU.add)))
        dve.wait(dve.done(nc.vector.memset(SHIFT[:, :, 0:1], 0.0)))
        tmp_free = [None] * 4
        for batch in range(B):
            xt = transposed(batch, XT, dve.last())
            dve.wait(xt, pe.last())
            dve.wait(dve.done(nc.vector.tensor_scalar(SHIFT[:, :, 1:S + 1], XT[:, :, :], SCAL[:, 2:3], None, ALU.mult)))
            mixed = []
            for k in range(KD):
                mixed.append(dve.done(nc.vector.scalar_tensor_tensor(
                    out=INP[:, k, :], in0=XT[:, k, :], scalar=SCAL[:, 1:2], in1=SHIFT[:, k, 0:S], op0=ALU.mult, op1=ALU.add)))
            pe.wait(mixed)
            scan_ready = []
            for m in range(KD):
                for c in range(S // BANK):
                    b = take_bank()
                    for k in range(KD):
                        ins = nc.tensor.matmul(psum[b][:, :], WIN[:, k, m * P:(m + 1) * P], INP[:, k, c * BANK:(c + 1) * BANK],
                                               start=(k == 0), stop=(k == KD - 1))
                    act.wait(pe.done(ins), dve.last() if batch else None)
                    bank_free[b] = act.done(nc.scalar.activation(HT[:, m, c * BANK:(c + 1) * BANK], psum[b][:, :], ACT.Relu,
                                                                 bias=BIN[:, m:m + 1]))
                dve.wait(bank_free[b])
                scan_ready.append(dve.done(nc.vector.tensor_tensor_scan(
                    STATE[:, m, :], SCAL[:, 0:1].broadcast_to([P, S]), HT[:, m, :], 0.0, ALU.mult, ALU.add)))
            pe.wait(scan_ready)
            for pair in range(TB // 2):
                b = take_bank()
                for i in range(2):
                    t = 2 * pair + i
                    for k in range(KD):
                        ins = nc.tensor.matmul(psum[b][:, i * D:(i + 1) * D], STATE[:, k, t * P:(t + 1) * P], WOUT[:, k, :],
                                               start=(k == 0), stop=(k == KD - 1))
                r = pair % 4
                dve.wait(pe.done(ins), tmp_free[r])
                bank_free[b] = dve.done(nc.vector.tensor_tensor(
                    TMPO[:, r, :, :], psum[b][:, :].rearrange("p (i d) -> p i d", i=2),
                    BOUT.unsqueeze(1).broadcast_to([P, 2, D]), ALU.add))
                t = batch * TB + 2 * pair
                pool.wait(bank_free[b])
                tmp_free[r] = pool.done(nc.gpsimd.tensor_tensor(X[:, t:t + 2, :], X[:, t:t + 2, :], TMPO[:, r, :, :], ALU.add))
                x_ready[t] = x_ready[t + 1] = tmp_free[r]
        st["xn_free"] = [pe.last(), dve.last()]

    for phase in PHASES:
        {"moe0": moe0, "attn": attention, "moe1": moe1, "mixer": mixer}[phase]()
        st["arena_free"] = everything()

    o_rows = out.rearrange("(t p) d -> p t d", p=P)
    for g in range(4):
        store(o_rows[:, 8 * g:8 * g + 8, :], X[:, 8 * g:8 * g + 8, :], [x_ready[t] for t in range(8 * g, 8 * g + 8)])
    sp.wait(stores.all(), loads.all())


def kernel(**inputs):
    import concourse.bacc as bacc
    from concourse.bass_utils import run_bass_kernel_spmd

    given = {n: np.asarray(v) for n, v in inputs.items()}
    column = lambda v: np.ascontiguousarray(v.reshape(KD, P).T)
    arrays = {
        "x": given["L0_attn_hidden_states"].reshape(T, D),
        "wg0": given["L0_ffn_wg"], "w0t": np.ascontiguousarray(given["L0_ffn_W"].transpose(0, 2, 1)),
        "b0": given["L0_ffn_b"],
        "wq": given["L0_attn_Wq"], "wk": given["L0_attn_Wk"], "wv": given["L0_attn_Wv"], "wp1": given["L0_attn_W1"],
        "wp2": given["L0_attn_W2"], "bq": given["L0_attn_bq"], "bk": given["L0_attn_bk"],
        "bp1": column(given["L0_attn_b1"]), "bp2": given["L0_attn_b2"].reshape(H, 1), "bv": given["L0_attn_bv"],
        "wg1": given["L1_ffn_Wg"], "bg1": given["L1_ffn_bg"], "w1": given["L1_ffn_W1"], "w2": given["L1_ffn_W2"],
        "b1": given["L1_ffn_b1"].reshape(1, E * D), "b2": given["L1_ffn_b2"].reshape(1, E * D),
        "win_t": np.ascontiguousarray(given["L1_attn_W_in"].T), "bin": column(given["L1_attn_b_in"]),
        "wout_t": np.ascontiguousarray(given["L1_attn_W_out"].T), "bout": given["L1_attn_b_out"],
        "decay": given["L1_attn_decay"].reshape(1), "mix": given["L1_attn_mix"].reshape(1),
    }
    nc = bacc.Bacc("TRN2", target_bir_lowering=False, num_devices=1)
    arrays = {n: np.ascontiguousarray(v) for n, v in arrays.items()}
    aps = {n: nc.dram_tensor("in_" + n, v.shape, mybir.dt.from_np(v.dtype), kind="ExternalInput").ap()
           for n, v in arrays.items()}
    out = nc.dram_tensor("out_tokens", [T, D], F32, kind="ExternalOutput").ap()
    program(nc, aps, out)
    r = run_bass_kernel_spmd(nc, [{"in_" + n: v for n, v in arrays.items()}], core_ids=[0])
    return r.results[0]["out_tokens"].reshape(B, S, D)
```

```python
from contextlib import ExitStack

import numpy as np

import concourse.bass as bass
from concourse import mybir

ALU = mybir.AluOpType
ACT = mybir.ActivationFunctionType
AX_X = mybir.AxisListType.X
F32 = mybir.dt.float32
BF16 = mybir.dt.bfloat16
I32 = mybir.dt.int32

P = 128
B, S = 2, 2048
D = 256
KD = D // P
T = B * S
NT = T // P
TB = S // P
E = 8
CAP = T // E
NJ0 = T // P
NJ1 = 40
RW = D + 1
REGION = T + P
SPARE = E * REGION
GROUPS = ((0, 8), (8, 16), (16, 24), (24, 28), (28, 32))
H = 16
DH = D // H
BANK = 512
LN_EPS = 1e-5
STD_EPS = 1e-6
NORM_MIN = 1e-4
PHASES = ("moe0", "attn", "moe0", "moe1", "mixer", "moe1")

VC = 2 * DH + 2
VP = 3 * VC
RING = 6
LAG = 2
RING_X = 5
AHEAD = 5
ACT_KT = (1, 4, 6, 9, 11, 14)


class Queue:

    def __init__(self, eng, sem):
        self.eng, self.sem, self.n, self.seen = eng, sem, 0, {}

    def wait(self, *ticks):
        for tick in ticks:
            if tick is None:
                continue
            if isinstance(tick, list):
                self.wait(*tick)
                continue
            sem, value = tick
            if self.seen.get(sem.name, 0) < value:
                self.eng.wait_ge(sem, value)
                self.seen[sem.name] = value

    def done(self, instruction):
        instruction.then_inc(self.sem, 1)
        self.n += 1
        return (self.sem, self.n)

    def last(self):
        return (self.sem, self.n) if self.n else None


class Transfers:

    def __init__(self, queue, sems):
        self.queue, self.sems, self.count, self.i = queue, sems, [0] * len(sems), 0

    def start(self, issue):
        k = self.i % len(self.sems)
        self.i += 1
        self.queue.wait((self.sems[k], self.count[k]) if self.count[k] else None)
        issue().then_inc(self.sems[k], 16)
        self.count[k] += 16
        return (self.sems[k], self.count[k])

    def all(self):
        return [(s, c) for s, c in zip(self.sems, self.count) if c]


def program(nc, a, out):
    with ExitStack() as ctx:
        build(nc, ctx, a, out)


def build(nc, ctx, a, out):
    def sb(name, shape, dt=F32):
        return ctx.enter_context(nc.sbuf_tensor(name, shape, dt))

    def sem(name):
        return ctx.enter_context(nc.semaphore(name))

    pe = Queue(nc.tensor, sem("pe_done"))
    dve = Queue(nc.vector, sem("dve_done"))
    act = Queue(nc.scalar, sem("act_done"))
    pool = Queue(nc.gpsimd, sem("pool_done"))
    sp = Queue(nc.sync, sem("sp_done"))
    loads = Transfers(sp, [sem(f"load{i}") for i in range(12)])
    stores = Transfers(sp, [sem(f"store{i}") for i in range(8)])
    scatters = Transfers(pool, [sem(f"scatter{i}") for i in range(8)])
    gathers = Transfers(pool, [sem(f"gather{i}") for i in range(8)])

    def load(dst, src, *after):
        sp.wait(*after)
        return loads.start(lambda: nc.sync.dma_start(dst, src))

    def store(dst, src, *after):
        sp.wait(*after)
        return stores.start(lambda: nc.sync.dma_start(dst, src))

    dram = lambda name, rows, width: nc.dram_tensor(name, [rows, width], F32, kind="Internal").ap()
    empty0 = dram("moe0_empty_slots", T, RW)
    slots0 = dram("moe0_slots", 2 * T, RW)
    slots1 = dram("moe1_slots", SPARE + (NJ1 - NT) * P, RW)
    y_rows = dram("expert_rows", T + NJ1 * P, D)
    bias_parts = nc.dram_tensor("bias_parts", [2, 3, E * D], BF16, kind="Internal").ap()
    zq_rows = nc.dram_tensor("q_rows", [B * H, S], F32, kind="Internal").ap()

    X = sb("residual", [P, NT, D])
    XN = sb("normed", [P, NT, RW])
    XTR = sb("normed_T", [P, 3, 2, KD, P])
    STATS = sb("ln_stats", [P, 8, 6])
    MV = sb("ln_mean_var", [P, NT, 2])
    SD = sb("ln_std", [P, NT])
    RSTD = sb("ln_rstd", [P, NT])
    SHIFTS = sb("ln_shift", [P, NT])
    GM = 16
    LG, SC, OHF, POS, CUM, TMP = (sb(n, [P, E * GM]) for n in ("logits", "score", "onehot", "position", "running", "route_tmp"))
    OHB = sb("onehot_bf", [P, E * GM], BF16)
    CARRY = sb("routed_before", [P, E])
    sm = {n: sb("r_" + n, [P, NT]) for n in ("max", "rank", "den", "gate", "loc", "base", "keep", "slot")}
    SLOT = sb("slot_of_token", [P, NT], I32)
    CE = sb("tile_counts", [P, 4, E])
    LE = sb("tile_cmp", [P, 3, NJ1, E])
    GAPS = LE[:, :, :, :].rearrange("p i j e -> p (i j e)")[:, 0:NT * E].rearrange("p (t e) -> p t e", t=NT)
    TJ = sb("tile_f", [P, 4, NJ1])
    EXI = sb("tile_expert", [P, NJ1], I32)
    ROWI = sb("tile_row", [P, NJ1], I32)
    PADI = sb("pad_rows", [P, E], I32)
    PAD = sb("pad_source", [P, D + E])
    IDENT = sb("identity", [P, P])
    UTRI = sb("upper_bf", [P, P], BF16)
    ONESB = sb("ones_bf", [P, P], BF16)
    ONESF = sb("ones_f", [P, P])
    HALF = sb("half_col", [P, 1])
    EPS = sb("eps", [P, 2])
    REV = sb("rank_of_expert", [P, E])
    ECOL = sb("expert_base", [P, E])
    RESET = {n: sb(f"scan_reset{n}", [P, E, n]) for n in sorted({hi - lo for lo, hi in GROUPS})}
    TRASH = sb("trash_slot", [P, NT])
    REGCOL = sb("expert_region", [P, E])
    JROW = sb("tile_spare_row", [P, 2, NJ1])
    M128 = sb("tile_start", [P, NT])
    JCOL = sb("tile_index", [P, NJ1])
    SCH = sb("key_scale", [P, TB, H])
    WG0 = sb("wg0", [P, KD, E])
    WG1 = sb("wg1", [P, KD, E])
    BG1 = sb("bg1", [P, E])
    BIAS = sb("top1_biases", [P, 2, E * D // P])
    BIAS3 = sb("top1_bias_parts", [P, 2, 3, E * D // P], BF16)
    ARENA_N = 31232
    ARENA = sb("arena", [P, ARENA_N])

    psum = [ctx.enter_context(nc.psum_tensor(f"bank{i}", [P, BANK], F32)) for i in range(8)]
    bank_free = [None] * 8
    turn = [0]

    def take_bank(choice=range(6)):
        choice = list(choice)
        b = choice[turn[0] % len(choice)]
        turn[0] += 1
        pe.wait(bank_free[b])
        return b

    def carve(start, n, parts=P):
        return ARENA[0:parts, start:start + n]

    x_rows = a["x"].rearrange("(t p) d -> p t d", p=P)
    x_ready = [None] * NT
    for lo, hi in ((0, 4), (4, 8), (8, 16), (16, 24), (24, 32)):
        tick = load(X[:, lo:hi, :], x_rows[:, lo:hi, :])
        for t in range(lo, hi):
            x_ready[t] = tick
    wg_ready = [load(WG0[:, :, :], a["wg0"].rearrange("(k p) e -> p k e", p=P)),
                load(WG1[:, :, :], a["wg1"].rearrange("(k p) e -> p k e", p=P)),
                load(BG1[:, :], a["bg1"].partition_broadcast(P))]

    nc.gpsimd.memset(IDENT[:, :], 0.0)
    nc.gpsimd.memset(UTRI[:, :], 1.0)
    nc.gpsimd.memset(ONESB[:, :], 1.0)
    nc.gpsimd.memset(ONESF[:, :], 1.0)
    nc.gpsimd.memset(HALF[:, :], 0.5)
    nc.gpsimd.memset(EPS[:, 0:1], LN_EPS)
    nc.gpsimd.memset(EPS[:, 1:2], STD_EPS)
    nc.gpsimd.memset(PAD[:, :], 0.0)
    for n in RESET:
        nc.gpsimd.memset(RESET[n][:, :, :], 1.0)
    pool.wait(pool.done(nc.gpsimd.memset(SCH[:, :, :], 2.0)))
    nc.gpsimd.affine_select(out=IDENT[:, :], in_=IDENT[:, :], compare_op=ALU.not_equal, fill=1.0, base=0,
                            pattern=[[-1, P]], channel_multiplier=1)
    nc.gpsimd.affine_select(out=UTRI[:, :], in_=UTRI[:, :], compare_op=ALU.is_ge, fill=0.0, base=-1,
                            pattern=[[1, P]], channel_multiplier=-1)
    for n in RESET:
        nc.gpsimd.memset(RESET[n][:, :, 0:1], 0.0)
    for t in ACT_KT:
        nc.gpsimd.memset(SCH[:, t, :], 1.0)
    io = lambda ap, pat, base, cm: nc.gpsimd.iota(ap, pattern=pat, base=base, channel_multiplier=cm,
                                                  allow_small_or_imprecise_dtypes=True)
    io(REV[:, :], [[-1, E]], E, 0)
    io(ECOL[:, :], [[CAP, E]], 0, 0)
    io(TRASH[:, :], [[P, NT]], T, 1)
    io(M128[:, :], [[P, NT]], 0, 0)
    io(REGCOL[:, :], [[REGION, E]], 0, 0)
    number = lambda ap: ap[:, :, D:D + 1].bitcast(I32)[:, :, 0]
    io(PAD[:, D:D + E].bitcast(I32), [[P, E]], T, 1)
    io(JCOL[:, :], [[1, NJ1]], 0, 0)
    io(JROW[:, 1, :], [[P, NJ1]], SPARE - NT * P, 0)
    consts = pool.done(io(JROW[:, 0, :], [[P, NJ1]], 0, 0))

    biases_in = [load(BIAS[:, n, :], a[name].rearrange("o (p c) -> p (o c)", p=P)) for n, name in enumerate(("b1", "b2"))]
    bias_split = []

    tiles = lambda ap: ap.rearrange("(t p) d -> p t d", p=P)
    EMPTY = carve(ARENA_N - NT * RW, NT * RW).rearrange("p (t d) -> p t d", d=RW)
    pool.wait(pool.done(nc.gpsimd.memset(EMPTY, 0.0)))
    emptied = pool.done(io(number(EMPTY), [[P, NT]], T, 1))
    first_slots = store(tiles(slots0[0:T, :]), EMPTY, emptied)
    empty_made = []

    def fill_scratch():
        for n in range(2):
            pool.wait(biases_in[n])
            for i in range(3):
                pool.wait(pool.done(nc.gpsimd.tensor_copy(BIAS3[:, n, i, :], BIAS[:, n, :])))
                if i < 2:
                    pool.wait(pool.done(nc.gpsimd.tensor_tensor(BIAS[:, n, :], BIAS[:, n, :], BIAS3[:, n, i, :], ALU.subtract)))
            bias_split.append(store(bias_parts[n].rearrange("i (p c) -> p i c", p=P), BIAS3[:, n, :, :], pool.last()))
        spares = EMPTY[:, E:E + NJ1 - NT, :]
        empty_made.append(store(tiles(empty0), EMPTY))
        ready = [store(tiles(slots1[SPARE:SPARE + (NJ1 - NT) * P, :]), spares),
                 store(tiles(y_rows[0:T, :]), EMPTY[:, :, 0:D])]
        st["slots_free"] = ready[:1]
        st["y_free"] = ready

    st = {
        "xn_free": [],
        "empty0": first_slots,
        "slots_free": [],
        "y_free": [],
        "arena_free": [],
        "xtr_free": [None] * 3,
    }

    def everything():
        return [q.last() for q in (pe, dve, act, pool)] + loads.all() + stores.all() + scatters.all() + gathers.all()

    def empty_slots():
        sp.wait(st["slots_free"], empty_made)
        st["empty0"] = stores.start(lambda: nc.sync.dma_start(slots0[0:T, :], empty0))

    x_pending = [None] * NT

    def current(t):
        if x_pending[t] is not None:
            update, x_pending[t] = x_pending[t], None
            update()
        return x_ready[t]

    def layernorm(tiles, dest):
        cuts = [0] + list(range(4, len(tiles), 8)) + [len(tiles)]
        groups = [tiles[lo:hi] for lo, hi in zip(cuts, cuts[1:])]

        def statistics(g):
            ticks = []
            for t in g:
                dve.wait(current(t), bn_free[t % 8])
                ticks.append(dve.done(nc.vector.bn_stats(STATS[:, t % 8, :], X[:, t, :])))
            for t, tick in zip(g, ticks):
                dve.wait(tick)
                bn_free[t % 8] = done = dve.done(nc.vector.bn_aggr(MV[:, t, :], STATS[:, t % 8, :]))
            return done

        def scales(g, done):
            lo, hi = g[0], g[-1] + 1
            act.wait(done, consts)
            dve.wait(act.done(nc.scalar.activation(SD[:, lo:hi], MV[:, lo:hi, 1], ACT.Sqrt, bias=EPS[:, 0:1])))
            dve.wait(dve.done(nc.vector.reciprocal(RSTD[:, lo:hi], SD[:, lo:hi])))
            return dve.done(nc.vector.scalar_tensor_tensor(out=SHIFTS[:, lo:hi], in0=MV[:, lo:hi, 0], scalar=-1.0,
                                                           in1=RSTD[:, lo:hi], op0=ALU.mult, op1=ALU.mult))

        ready = scales(groups[0], statistics(groups[0]))
        for i, g in enumerate(groups):
            following = groups[i + 1] if i + 1 < len(groups) else None
            done = statistics(following) if following else None
            for n, t in enumerate(g):
                if n == len(g) - 2 and following:
                    next_ready = scales(following, done)
                act.wait(ready, x_ready[t])
                yield t, act.done(nc.scalar.activation(dest(t), X[:, t, :], ACT.Identity, bias=SHIFTS[:, t:t + 1],
                                                       scale=RSTD[:, t:t + 1]))
            ready = next_ready if following else None

    bn_free = [None] * 8
    exps_free = [None]

    def route(kind, WG):
        act.wait(st["xn_free"])
        pool.wait(st["xn_free"])
        numbered = pool.done(nc.gpsimd.iota(number(XN), pattern=[[P, NT]], base=0, channel_multiplier=1))
        pe.wait(bank_free[6], bank_free[7], wg_ready, consts)
        normed, evacuated, logits_made = [None] * NT, {}, {}
        slots = slots0 if kind == "moe0" else slots1
        dve.wait(dve.done(nc.vector.memset(CARRY[:, :], 0.0)), consts)

        def logits(pair):
            slot = pair % 3
            group = [i for i, (lo, hi) in enumerate(GROUPS) if lo <= 2 * pair < hi][0]
            bank = 6 + group % 2
            pe.wait(evacuated[pair], bank_free[bank])
            for i in range(2):
                t = 2 * pair + i - GROUPS[group][0]
                for k in range(KD):
                    ins = nc.tensor.matmul(psum[bank][:, t * E:(t + 1) * E], XTR[:, slot, i, k, :], WG[:, k, :],
                                           start=(k == 0), stop=(k == KD - 1))
            st["xtr_free"][slot] = logits_made[group] = pe.done(ins)

        def step(ins):
            dve.wait(dve.done(ins))

        def place(group):
            lo, hi = GROUPS[group]
            n = hi - lo
            view = lambda ap: ap[:, 0:E * n].rearrange("p (e t) -> p e t", e=E)
            line = lambda ap: ap[:, 0:E * n]
            by_tile = lambda ap: ap[:, 0:E * n].rearrange("p (e t) -> p t e", e=E)
            over_e = lambda ap: ap[:, lo:hi].unsqueeze(1).broadcast_to([P, E, n])
            over_t = lambda ap: ap.unsqueeze(2).broadcast_to([P, E, n])
            col = {name: ap[:, lo:hi] for name, ap in sm.items()}
            bank = 6 + group % 2
            dve.wait(logits_made[group])
            raw = psum[bank][:, 0:n * E].rearrange("p (t e) -> p e t", e=E)
            if kind == "moe1":
                step(nc.vector.tensor_tensor(view(LG), raw, over_t(BG1[:, :]), ALU.add))
            else:
                step(nc.vector.tensor_copy(view(LG), raw))
            bank_free[bank] = dve.last()
            step(nc.vector.tensor_reduce(col["max"], by_tile(LG), AX_X, ALU.max))
            step(nc.vector.tensor_tensor(view(TMP), view(LG), over_e(sm["max"]), ALU.is_equal))
            step(nc.vector.tensor_tensor(view(SC), view(TMP), over_t(REV[:, :]), ALU.mult))
            step(nc.vector.tensor_reduce(col["rank"], by_tile(SC), AX_X, ALU.max))
            step(nc.vector.tensor_tensor(view(OHB), view(SC), over_e(sm["rank"]), ALU.is_equal))
            pe.wait(dve.last())
            b = take_bank()
            before, total = psum[b][:, 0:E * n], psum[b][:, E * n:2 * E * n]
            nc.tensor.matmul(before, UTRI[:, :], line(OHB), start=True, stop=True)
            counted = pe.done(nc.tensor.matmul(total, ONESB[:, :], line(OHB), start=True, stop=True))
            step(nc.vector.tensor_copy(line(OHF), line(OHB)))
            if kind == "moe0":
                dve.wait(exps_free[0])
                step(nc.vector.tensor_tensor(GAPS[:, lo:hi, :].rearrange("p t e -> p e t"), view(LG), over_e(sm["max"]),
                                             ALU.subtract))
            dve.wait(counted)
            step(nc.vector.tensor_tensor_scan(line(CUM), RESET[n][:, :, :].rearrange("p e t -> p (e t)"), total, 0.0,
                                              ALU.mult, ALU.add))
            step(nc.vector.tensor_tensor(line(POS), line(CUM), total, ALU.subtract))
            step(nc.vector.tensor_tensor(line(POS), line(POS), before, ALU.add))
            bank_free[b] = dve.last()
            step(nc.vector.tensor_tensor(view(POS), view(POS), over_t(CARRY[:, :]), ALU.add))
            step(nc.vector.tensor_tensor(CARRY[:, :], CARRY[:, :], view(CUM)[:, :, n - 1], ALU.add))
            if kind == "moe1" and group == len(GROUPS) - 1:
                step(nc.vector.tensor_tensor(PADI[:, :], CARRY[:, :], REGCOL[:, :], ALU.add))
                pads_from.append(dve.last())
            if kind == "moe0":
                step(nc.vector.tensor_tensor(view(TMP), view(OHF), view(POS), ALU.mult))
                step(nc.vector.tensor_reduce(col["loc"], by_tile(TMP), AX_X, ALU.add))
                step(nc.vector.tensor_tensor(view(TMP), view(OHF), over_t(ECOL[:, :]), ALU.mult))
                step(nc.vector.tensor_reduce(col["base"], by_tile(TMP), AX_X, ALU.add))
                step(nc.vector.tensor_scalar(col["keep"], col["loc"], float(CAP), None, ALU.is_lt))
                step(nc.vector.tensor_tensor(col["slot"], col["loc"], col["base"], ALU.add))
                step(nc.vector.tensor_tensor(col["base"], col["slot"], TRASH[:, lo:hi], ALU.subtract))
                step(nc.vector.tensor_tensor(col["base"], col["base"], col["keep"], ALU.mult))
                step(nc.vector.tensor_tensor(SLOT[:, lo:hi], col["base"], TRASH[:, lo:hi], ALU.add))
                slots_ready = dve.last()
            else:
                step(nc.vector.tensor_tensor(view(POS), view(POS), over_t(REGCOL[:, :]), ALU.add))
                step(nc.vector.tensor_tensor(view(TMP), view(OHF), view(POS), ALU.mult))
                step(nc.vector.tensor_reduce(col["slot"], by_tile(TMP), AX_X, ALU.add))
                step(nc.vector.tensor_copy(SLOT[:, lo:hi], col["slot"]))
                slots_ready = dve.last()
            pool.wait(slots_ready, numbered, st["slots_free"], st["empty0"] if kind == "moe0" else None)
            for t in range(lo, hi):
                pool.wait(normed[t])
                scatters.start(lambda: nc.gpsimd.indirect_dma_start(
                    out=slots, out_offset=bass.IndirectOffsetOnAxis(ap=SLOT[:, t:t + 1], axis=0),
                    in_=XN[:, t, :], in_offset=None))

        def turn(pair):
            b = turned_bank[pair] = take_bank()
            pe.wait(normed[2 * pair + 1])
            for i in range(2):
                for k in range(KD):
                    ins = nc.tensor.transpose(psum[b][:, (2 * i + k) * P:(2 * i + k + 1) * P],
                                              XN[:, 2 * pair + i, k * P:(k + 1) * P], IDENT[:, :])
            turned[pair] = pe.done(ins)

        def take_turned(pair):
            b = turned_bank[pair]
            act.wait(turned[pair], st["xtr_free"][pair % 3])
            evacuated[pair] = bank_free[b] = act.done(nc.scalar.activation(
                XTR[:, pair % 3, :, :, :].rearrange("p i k c -> p (i k c)"), psum[b][:, :], ACT.Copy))

        def after_pair(pair):
            if 0 <= pair - LAG < NT // 2:
                take_turned(pair - LAG)
            if 0 <= pair - LAG - 1 < NT // 2:
                logits(pair - LAG - 1)
                if 2 * (pair - LAG) >= GROUPS[pending[0]][1]:
                    place(pending.pop(0))

        pads_from = []
        turned, turned_bank = {}, {}
        pending = list(range(len(GROUPS)))
        for t, tick in layernorm(list(range(NT)), lambda t: XN[:, t, 0:D]):
            normed[t] = tick
            if t % 2:
                turn(t // 2)
                after_pair(t // 2)
        for pair in range(NT // 2, NT // 2 + LAG + 1):
            after_pair(pair)
        if kind == "moe0":
            act.wait(dve.last())
            dve.wait(act.done(nc.scalar.activation(GAPS[:, :, :], GAPS[:, :, :], ACT.Exp)))
            step(nc.vector.tensor_reduce(sm["den"][:, :], GAPS[:, :, :], AX_X, ALU.add))
            exps_free[0] = dve.last()
            step(nc.vector.reciprocal(sm["gate"][:, :], sm["den"][:, :]))
            step(nc.vector.tensor_tensor(sm["gate"][:, :], sm["gate"][:, :], sm["keep"][:, :], ALU.mult))
            step(nc.vector.tensor_scalar(sm["gate"][:, :], sm["gate"][:, :], 0.5, None, ALU.mult))
            return scatters.all(), dve.last()
        over_j = lambda ap: ap.unsqueeze(1).broadcast_to([P, NJ1, E])
        tile_j = JCOL[:, :].unsqueeze(2).broadcast_to([P, NJ1, E])
        cnt = CARRY[:, :]
        counts = LE[:, 0, 0:NT, :].rearrange("p t e -> p e t")
        sp.wait(pads_from, st["slots_free"], consts)
        padded = []
        for e in range(E):
            row = nc.sync.value_load(PADI[0:1, e:e + 1], min_val=0, max_val=SPARE - P)
            padded.append(store(slots[bass.ds(row, P), :], PAD[:, e:e + RW]))
        step(nc.vector.tensor_tensor(counts, cnt.unsqueeze(2).broadcast_to([P, E, NT]),
                                     M128[:, :].unsqueeze(1).broadcast_to([P, E, NT]), ALU.is_gt))
        step(nc.vector.tensor_reduce(CE[:, 0, :], counts, AX_X, ALU.add))
        step(nc.vector.tensor_tensor_scan(CE[:, 1, :], ONESF[:, 0:E], CE[:, 0, :], 0.0, ALU.mult, ALU.add))
        step(nc.vector.tensor_tensor(CE[:, 2, :], CE[:, 1, :], CE[:, 0, :], ALU.subtract))
        step(nc.vector.tensor_tensor(LE[:, 1, :, :], over_j(CE[:, 1, :]), tile_j, ALU.is_le))
        step(nc.vector.tensor_reduce(TJ[:, 0, :], LE[:, 1, :, :], AX_X, ALU.add))
        step(nc.vector.tensor_scalar(EXI[:, :], TJ[:, 0, :], float(E - 1), None, ALU.min))
        step(nc.vector.tensor_scalar(CE[:, 3, :], CE[:, 2, :], -float(P), None, ALU.mult))
        step(nc.vector.tensor_tensor(CE[:, 3, :], CE[:, 3, :], REGCOL[:, :], ALU.add))
        step(nc.vector.tensor_tensor(LE[:, 2, :, :], over_j(CE[:, 2, :]), tile_j, ALU.is_le))
        step(nc.vector.tensor_tensor(LE[:, 0, :, :], LE[:, 2, :, :], LE[:, 1, :, :], ALU.subtract))
        step(nc.vector.tensor_reduce(TJ[:, 1, :], LE[:, 0, :, :], AX_X, ALU.add))
        step(nc.vector.tensor_tensor(LE[:, 2, :, :], LE[:, 0, :, :], over_j(CE[:, 3, :]), ALU.mult))
        step(nc.vector.tensor_reduce(TJ[:, 2, :], LE[:, 2, :, :], AX_X, ALU.add))
        step(nc.vector.tensor_tensor(TJ[:, 3, :], JROW[:, 0, :], JROW[:, 1, :], ALU.subtract))
        step(nc.vector.tensor_tensor(TJ[:, 3, :], TJ[:, 3, :], TJ[:, 1, :], ALU.mult))
        step(nc.vector.tensor_tensor(TJ[:, 3, :], TJ[:, 3, :], JROW[:, 1, :], ALU.add))
        step(nc.vector.tensor_tensor(ROWI[:, :], TJ[:, 3, :], TJ[:, 2, :], ALU.add))
        return scatters.all() + padded, dve.last()

    def return_rows(YS_tile, number_of, *after):
        pool.wait(*after, st["y_free"])
        return gathers.start(lambda: nc.gpsimd.indirect_dma_start(
            out=y_rows, out_offset=bass.IndirectOffsetOnAxis(ap=number_of, axis=0), in_=YS_tile, in_offset=None))

    def add_rows(scale):
        back = gathers.all()
        last = []
        for g in range(4):
            got = load(XN[:, 8 * g:8 * g + 8, 0:D], tiles(y_rows[8 * g * P:8 * (g + 1) * P, :]), back)
            last.append(got)
            for t in range(8 * g, 8 * g + 8):
                def update(t=t, got=got):
                    dve.wait(got)
                    x_ready[t] = dve.done(nc.vector.scalar_tensor_tensor(
                        out=X[:, t, :], in0=XN[:, t, 0:D], scalar=scale(t), in1=X[:, t, :], op0=ALU.mult, op1=ALU.add))
                x_pending[t] = update
        st["y_free"] = last
        st["xn_free"] = []

    def add_everything():
        for t in range(NT):
            current(t)

    def moe0(before_moe1):
        WT = carve(0, KD * E * D).rearrange("p (k e f) -> p k e f", k=KD, e=E)
        BB = carve(4096, E * D).rearrange("p (e f) -> p e f", e=E)
        ring = 3
        XS = carve(9216, RING_X * 2 * RW).rearrange("p (r i d) -> p r i d", r=RING_X, i=2)
        XST = carve(6144, ring * 2 * D).rearrange("p (r i k c) -> p r i k c", r=ring, i=2, k=KD)
        YS = carve(6144 + 1536, ring * 2 * D).rearrange("p (r i d) -> p r i d", r=ring, i=2)
        weights = [load(WT[:, k, :, :], a["w0t"][:, k * P:(k + 1) * P, :].rearrange("e p f -> p e f"), st["arena_free"])
                   for k in range(KD)]
        weights.append(load(BB[:, :, :], a["b0"].partition_broadcast(P)))
        if st["empty0"] is None:
            empty_slots()
        if not empty_made:
            fill_scratch()
        scattered, gate_ready = route("moe0", WG0)
        st["empty0"] = None
        xs_free, xst_free, ys_free = [None] * RING_X, [None] * ring, [None] * ring
        n_pairs = NJ0 // 2
        xs_ready, xst_ready = {}, {}

        def fetch(j):
            xs_ready[j] = load(XS[:, j % RING_X, :, :], tiles(slots0[2 * j * P:2 * (j + 1) * P, :]), scattered,
                               xs_free[j % RING_X])

        def turn_pair(j):
            b = take_bank()
            pe.wait(xs_ready[j])
            for i in range(2):
                for k in range(KD):
                    ins = nc.tensor.transpose(psum[b][:, (2 * i + k) * P:(2 * i + k + 1) * P],
                                              XS[:, j % RING_X, i, k * P:(k + 1) * P], IDENT[:, :])
            pe.done(ins)
            act.wait(pe.last(), xst_free[j % ring], st["arena_free"])
            xst_ready[j] = bank_free[b] = act.done(nc.scalar.activation(
                XST[:, j % ring, :, :, :].rearrange("p i k c -> p (i k c)"), psum[b][:, :], ACT.Copy))

        def expert_pair(j):
            e = (2 * j) // (CAP // P)
            b = take_bank()
            pe.wait(xst_ready[j], weights)
            for i in range(2):
                for k in range(KD):
                    ins = nc.tensor.matmul(psum[b][:, i * D:(i + 1) * D], XST[:, j % ring, i, k, :], WT[:, k, e, :],
                                           start=(k == 0), stop=(k == KD - 1))
            xst_free[j % ring] = pe.done(ins)
            dve.wait(pe.last(), ys_free[j % ring], weights, st["arena_free"])
            bank_free[b] = dve.done(nc.vector.tensor_tensor(
                YS[:, j % ring, :, :], psum[b][:, :].rearrange("p (i f) -> p i f", i=2),
                BB[:, e, :].unsqueeze(1).broadcast_to([P, 2, D]), ALU.add))
            ys_free[j % ring] = [return_rows(YS[:, j % ring, i, :], XS[:, j % RING_X, i, D:D + 1].bitcast(I32),
                                             bank_free[b], xs_ready[j]) for i in range(2)]
            xs_free[j % RING_X] = ys_free[j % ring]

        for j in range(2):
            fetch(j)
        if before_moe1:
            load_weights1()
        turn_pair(0)
        for j in range(n_pairs):
            if j + 2 < n_pairs:
                fetch(j + 2)
            if j + 1 < n_pairs:
                turn_pair(j + 1)
            expert_pair(j)
        st["slots_free"] = scattered + list(xs_ready.values())[-12:]
        add_rows(lambda t: sm["gate"][:, t:t + 1])

    L1 = 9216 + RING_X * 2 * RW
    WEIGHTS1 = ARENA_N - (2 * KD + 1) * E * D
    W1, W2 = (carve(WEIGHTS1 + n * KD * E * D, KD * E * D).rearrange("p (k n) -> p k n", k=KD) for n in range(2))
    B3 = [carve(WEIGHTS1 + (4 * KD + n) * E * D // 2, E * D // 2, 3).bitcast(BF16) for n in range(2)]
    weights1 = []

    def load_weights1():
        for W, name in ((W1, "w1"), (W2, "w2")):
            for k in range(KD):
                weights1.append(load(W[:, k, :].rearrange("p (e f) -> p e f", e=E),
                                     a[name][:, k * P:(k + 1) * P, :].rearrange("e p f -> p e f"), st["arena_free"]))
        for n in range(2):
            weights1.append(load(B3[n], bias_parts[n], bias_split, st["arena_free"]))

    def moe1():
        at = [L1]

        def part(n, parts=P):
            at[0] += n
            assert at[0] <= WEIGHTS1
            return carve(at[0] - n, n, parts)

        ring = 3
        XS = part(RING_X * 2 * RW).rearrange("p (r i d) -> p r i d", r=RING_X, i=2)
        XST = part(ring * 2 * D).rearrange("p (r i k c) -> p r i k c", r=ring, i=2, k=KD)
        HS = part(ring * 2 * D).rearrange("p (r i d) -> p r i d", r=ring, i=2)
        HT = part(ring * 2 * D).rearrange("p (r i k c) -> p r i k c", r=ring, i=2, k=KD)
        YS = part(ring * 2 * D).rearrange("p (r i d) -> p r i d", r=ring, i=2)
        if not weights1:
            load_weights1()
        weights = weights1
        rings_free = st["arena_free"]
        if not empty_made:
            fill_scratch()
        scattered, tiles_ready = route("moe1", WG1)
        n_pairs = NJ1 // 2
        free = {n: [None] * RING_X for n in ("xs", "xst", "hs", "ht", "ys")}
        ready = {n: {} for n in ("xs", "xst", "hs", "ht")}
        column = {}
        act.wait(rings_free)
        dve.wait(rings_free)

        def fetch(j):
            sp.wait(tiles_ready)
            ready["xs"][j] = []
            for i in range(2):
                row = nc.sync.value_load(ROWI[0:1, 2 * j + i:2 * j + i + 1], min_val=0, max_val=SPARE + (NJ1 - NT - 1) * P)
                ready["xs"][j].append(load(XS[:, j % RING_X, i, :], slots1[bass.ds(row, P), :], scattered,
                                           free["xs"][j % RING_X], rings_free))

        def turn_pair(j, src, dst, SRC, DST, copy):
            r, rs = j % ring, j % (RING_X if src == "xs" else ring)
            b = take_bank()
            pe.wait(ready[src][j])
            for i in range(2):
                for k in range(KD):
                    ins = nc.tensor.transpose(psum[b][:, (2 * i + k) * P:(2 * i + k + 1) * P],
                                              SRC[:, rs, i, k * P:(k + 1) * P], IDENT[:, :])
            turned = pe.done(ins)
            if src != "xs":
                free[src][r] = turned
            ready[dst][j] = bank_free[b] = copy(DST[:, r, :, :, :].rearrange("p i k c -> p (i k c)"), psum[b][:, :],
                                                pe.last(), free[dst][r])

        def copy_act(o, i, *after):
            act.wait(*after)
            return act.done(nc.scalar.activation(o, i, ACT.Copy))

        def copy_dve(o, i, *after):
            dve.wait(*after)
            return dve.done(nc.vector.tensor_copy(o, i))

        def layer(j, SRC, W, bias, src):
            r = j % ring
            b = take_bank()
            pe.wait(ready[src][j], weights)
            for i in range(2):
                if (j, i) not in column:
                    pe.wait(tiles_ready)
                    column[j, i] = nc.tensor.value_load(EXI[0:1, 2 * j + i:2 * j + i + 1], min_val=0, max_val=E - 1) * D
                where = bass.ds(column[j, i], D)
                for k in range(KD):
                    nc.tensor.matmul(psum[b][:, i * D:(i + 1) * D], SRC[:, r, i, k, :], W[:, k, where],
                                     start=(k == 0), stop=False)
                ins = nc.tensor.matmul(psum[b][:, i * D:(i + 1) * D], ONESB[0:3, :], bias[:, where],
                                       start=False, stop=True)
            free[src][r] = pe.done(ins)
            return b

        def first(j):
            b = layer(j, XST, W1, B3[0], "xst")
            act.wait(pe.last(), free["hs"][j % ring])
            ready["hs"][j] = bank_free[b] = act.done(nc.scalar.activation(
                HS[:, j % ring, :, :].rearrange("p i d -> p (i d)"), psum[b][:, :], ACT.Gelu))

        def second(j):
            b = layer(j, HT, W2, B3[1], "ht")
            dve.wait(pe.last(), free["ys"][j % ring])
            bank_free[b] = dve.done(nc.vector.tensor_copy(YS[:, j % ring, :, :].rearrange("p i d -> p (i d)"),
                                                          psum[b][:, :]))
            free["ys"][j % ring] = free["xs"][j % RING_X] = [
                return_rows(YS[:, j % ring, i, :], XS[:, j % RING_X, i, D:D + 1].bitcast(I32),
                            bank_free[b], ready["xs"][j]) for i in range(2)]

        for j in range(n_pairs + 3):
            if j < n_pairs:
                fetch(j)
            if 0 <= j - 1 < n_pairs:
                turn_pair(j - 1, "xs", "xst", XS, XST, copy_act)
            if 0 <= j - 2 < n_pairs:
                first(j - 2)
            if 0 <= j - 3 < n_pairs:
                turn_pair(j - 3, "hs", "ht", HS, HT, copy_dve)
                second(j - 3)
        st["slots_free"] = scattered + [x for j in range(n_pairs - 6, n_pairs) for x in ready["xs"][j]]
        add_rows(lambda t: 0.5)

    def transposed(batch, XT, xt_free):
        act.wait([x_ready[t] for t in range(NT)])
        LNR = XTR[:, :, :, :, :].rearrange("p r i k c -> p r i (k c)")
        ticks = [None] * TB
        act.wait(xt_free)
        dve.wait(st["xn_free"])

        def dest(t):
            pair = (t - batch * TB) // 2
            act.wait(st["xtr_free"][pair % 3])
            return LNR[:, pair % 3, t % 2, :]

        turned = {}

        def take_turned(pair):
            b, tick = turned[pair]
            act.wait(tick)
            ticks[2 * pair] = ticks[2 * pair + 1] = bank_free[b] = act.done(nc.scalar.activation(
                XT[:, :, 2 * pair * P:2 * (pair + 1) * P], psum[b][:, :].rearrange("p (k c) -> p k c", k=KD), ACT.Copy))

        for t, tick in layernorm(list(range(batch * TB, (batch + 1) * TB)), dest):
            if t % 2 == 0:
                continue
            pair = (t - batch * TB) // 2
            b = take_bank()
            pe.wait(tick, consts)
            for i in range(2):
                for k in range(KD):
                    ins = nc.tensor.transpose(psum[b][:, (2 * k + i) * P:(2 * k + i + 1) * P],
                                              LNR[:, pair % 3, i, k * P:(k + 1) * P], IDENT[:, :])
            st["xtr_free"][pair % 3] = pe.done(ins)
            turned[pair] = b, pe.last()
            if pair >= LAG:
                take_turned(pair - LAG)
        for pair in range(TB // 2 - LAG, TB // 2):
            take_turned(pair)
        return ticks

    def attention():
        xn = XN[:, :, :].rearrange("p t d -> p (t d)")
        add_everything()
        if "moe0" in PHASES[PHASES.index("attn"):]:
            empty_slots()
        XT = xn[:, 0:4096].rearrange("p (k n) -> p k n", k=KD)
        PT = xn[:, 4096:6144].rearrange("p (r m n) -> p r m n", r=2, m=KD)
        GT = xn[:, 6144:8192].rearrange("p (r m n) -> p r m n", r=2, m=KD)
        at = [0]

        def part(n, parts=P):
            at[0] += n
            assert at[0] <= ARENA_N, at[0]
            return carve(at[0] - n, n, parts)

        VOP_F = part(TB * H * VP // 2)
        VOP = VOP_F.bitcast(BF16).rearrange("p (t h c) -> p t h c", t=TB, h=H)
        signs_flat = part(RING * S // 2)
        SG = signs_flat.bitcast(BF16).rearrange("p (r n) -> p r n", r=RING)
        U = signs_flat[:, 0:2 * 4 * H * VC].rearrange("p (r t h c) -> p r t h c", r=2, t=4, h=H)
        QB = part(2 * S).rearrange("p (r n) -> p r n", r=2)
        Z = QB[0:H, :, :]
        HM = VOP_F[:, 0:2 * H * D].rearrange("p (s h l d) -> p s h l d", s=2, h=H, l=S // P)
        OS = part(S)
        QTM = part(TB * H).rearrange("p (t h) -> p t h", t=TB)
        KTM = part(TB * H).rearrange("p (t h) -> p t h", t=TB)
        NKT = part(TB * H).rearrange("p (t h) -> p t h", t=TB)
        A = part(2 * TB * VC).rearrange("p (r t c) -> p r t c", r=2, t=TB)
        BQK = A[:, 0, :, :].rearrange("p t c -> p (t c)")[:, 0:2 * D].rearrange("p (s d) -> p s d", s=2)
        N1 = part(2 * TB).rearrange("p (r t) -> p r t", r=2)
        N2 = part(2 * TB).rearrange("p (r t) -> p r t", r=2)
        CT = part(TB * DH).rearrange("p (t d) -> p t d", t=TB)
        WATT = {n: part(KD * D).rearrange("p (k n) -> p k n", k=KD) for n in ("wq", "wk", "wv", "wp1")}
        WP2 = part(KD * H).rearrange("p (k n) -> p k n", k=KD)
        BP1 = part(KD)
        BP2 = part(1, H)
        BVB = part(D)
        ROW = part(2 * D).rearrange("p (s d) -> p s d", s=2)
        MEANS = part(KD)
        MB = part(KD * P).rearrange("p (k c) -> p k c", k=KD)
        ZST = part(2 * 4 * 6, H).rearrange("p (s c x) -> p s c x", s=2, c=4)
        ZMV = part(2 * 2, H).rearrange("p (s x) -> p s x", s=2)
        ZS = part(3, H)
        TOT = part(H * 2 * DH, 1)
        CB = part(H, VP)

        free = st["arena_free"]
        wt = []
        for n in ("wq", "wk", "wv", "wp1"):
            wt.append(load(WATT[n], a[n].rearrange("(k p) n -> p k n", p=P), free))
        wt.append(load(WP2, a["wp2"].rearrange("(k p) n -> p k n", p=P), free))
        wt.append(load(BP1, a["bp1"], free))
        wt.append(load(BP2, a["bp2"], free))
        wt.append(load(BVB, a["bv"].partition_broadcast(P), free))
        for q in (pe, dve, act):
            q.wait(wt, free)
        pool.wait(free)
        cb_zero = pool.done(nc.gpsimd.memset(CB, 0.0))

        qb_ready, head_done = {}, {}
        pe_tile = {}
        sign_made = {}
        bank_of = lambda hh, c: (4 * hh + c) % 6
        evac = {}
        os_free, a_free, ct_free = [None], [[None], [None]], [None]
        prep_done = [None]

        def prepare(batch):
            bias_rows = [load(BQK[:, n, :], a[name].partition_broadcast(P), free, pool.last())
                         for n, name in enumerate(("bq", "bk"))]
            xt = transposed(batch, XT, pe.last())
            dve.wait(xt[TB - 1])
            dve.wait(dve.done(nc.vector.tensor_reduce(MEANS, XT[:, :, :], AX_X, ALU.add)))
            for k in range(KD):
                mb = dve.done(nc.vector.tensor_scalar(MB[:, k, :], ONESF[:, :], MEANS[:, k:k + 1], 1.0 / S,
                                                      ALU.mult, ALU.mult))
            z_ready = {}
            nchunk = S // BANK
            pt_free, gt_free = [None, None], [None, None]
            steps = [(s, c) for s in range(2) for c in range(nchunk)]
            pt_ready, gt_ready = {}, {}
            vop_read = pe.last()
            z_free = [sign_made.get(k) for k in list(sign_made)[-16:]]

            by_head = {}

            def project(s):
                W = WATT["wq"] if s == 0 else WATT["wk"]
                dve.wait(bias_rows, vop_read)
                for l in range(0, S // P, 2):
                    b = take_bank()
                    for i in range(2):
                        for k in range(KD):
                            tokens = XT[:, k, :].rearrange("p (n l) -> p l n", l=S // P)[:, l + i, :]
                            ins = nc.tensor.matmul(psum[b][:, i * D:(i + 1) * D], tokens, W[:, k, :],
                                                   start=(k == 0), stop=(k == KD - 1))
                    dve.wait(pe.done(ins))
                    bank_free[b] = by_head[s] = dve.done(nc.vector.tensor_tensor(
                        HM[:, s, :, l:l + 2, :].rearrange("p h l d -> p l h d"),
                        psum[b][:, :].rearrange("p (l h d) -> p l h d", l=2, h=H),
                        BQK[:, s, :].rearrange("p (h d) -> p h d", h=H).unsqueeze(1).broadcast_to([P, 2, H, DH]), ALU.add))

            def turn_rows(i):
                s, c = steps[i]
                pe.wait(by_head[s])
                for half in range(2):
                    b = take_bank()
                    for j in range(2):
                        row = HM[:, s, 4 * c + 2 * half + j, :, :].rearrange("p l d -> p (l d)")
                        for k in range(KD):
                            ins = nc.tensor.transpose(psum[b][:, (2 * k + j) * P:(2 * k + j + 1) * P],
                                                      row[:, k * P:(k + 1) * P], IDENT[:, :])
                    act.wait(pe.done(ins), pt_free[i % 2])
                    bank_free[b] = pt_ready[i] = act.done(nc.scalar.activation(
                        PT[:, i % 2, :, half * 2 * P:(half + 1) * 2 * P],
                        psum[b][:, :].rearrange("p (k c) -> p k c", k=KD), ACT.Copy))

            def hidden(i):
                pe.wait(pt_ready[i])
                for m in range(KD):
                    b = take_bank()
                    for k in range(KD):
                        ins = nc.tensor.matmul(psum[b][:, :], WATT["wp1"][:, k, m * P:(m + 1) * P], PT[:, i % 2, k, :],
                                               start=(k == 0), stop=(k == KD - 1))
                    act.wait(pe.done(ins), gt_free[i % 2])
                    bank_free[b] = gt_ready[i] = act.done(nc.scalar.activation(
                        GT[:, i % 2, m, :], psum[b][:, :], ACT.Gelu, bias=BP1[:, m:m + 1]))
                pt_free[i % 2] = pe.last()

            def score(i):
                s, c = steps[i]
                pe.wait(gt_ready[i])
                b = take_bank()
                for k in range(KD):
                    ins = nc.tensor.matmul(psum[b][0:H, :], WP2[:, k, :], GT[:, i % 2, k, :],
                                           start=(k == 0), stop=(k == KD - 1))
                gt_free[i % 2] = pe.done(ins)
                dve.wait(pe.last(), z_free)
                bank_free[b] = dve.done(nc.vector.tensor_scalar(Z[:, s, c * BANK:(c + 1) * BANK], psum[b][0:H, :],
                                                                BP2[:, 0:1], None, ALU.add))
                dve.wait(bank_free[b])
                z_ready[s] = dve.done(nc.vector.bn_stats(ZST[:, s, c, :], Z[:, s, c * BANK:(c + 1) * BANK]))

            for i in range(len(steps) + 2):
                if i < len(steps):
                    if i == 0:
                        pe.wait(xt)
                        project(0)
                        project(1)
                    turn_rows(i)
                if 0 <= i - 1 < len(steps):
                    hidden(i - 1)
                if 0 <= i - 2 < len(steps):
                    score(i - 2)
            dve.wait(z_ready[0], z_ready[1])
            for s in range(2):
                mv = dve.done(nc.vector.bn_aggr(ZMV[:, s, :], ZST[:, s, :, :].rearrange("p c x -> p (c x)")))
            dve.wait(mv)
            both = dve.done(nc.vector.tensor_tensor(ZS[:, 0:1], ZMV[:, 0, 1:2], ZMV[:, 1, 1:2], ALU.add))
            act.wait(both)
            root = act.done(nc.scalar.activation(ZS[:, 1:2], ZS[:, 0:1], ACT.Sqrt, bias=EPS[0:H, 1:2], scale=0.5))
            dve.wait(root)
            dve.wait(dve.done(nc.vector.reciprocal(ZS[:, 2:3], ZS[:, 1:2])))
            for s in range(2):
                scaled = dve.done(nc.vector.tensor_scalar(Z[:, s, :], Z[:, s, :], ZMV[:, s, 0:1], ZS[:, 2:3],
                                                          ALU.subtract, ALU.mult))
                if s == 0:
                    q_stored = store(zq_rows[batch * H:(batch + 1) * H, :], Z[:, 0, :], scaled, loads.all())
            pe.wait(scaled)
            for s, M in ((0, QTM), (1, KTM)):
                b = take_bank()
                for t in range(TB):
                    ins = nc.tensor.transpose(psum[b][:, t * H:(t + 1) * H], Z[:, s, t * P:(t + 1) * P], IDENT[0:H, 0:H])
                dve.wait(pe.done(ins), pool.last())
                bank_free[b] = dve.done(nc.vector.tensor_copy(M.rearrange("p t h -> p (t h)"), psum[b][:, 0:TB * H]))
            dve.wait(bank_free[b])
            nkt = dve.done(nc.vector.tensor_scalar(NKT.rearrange("p t h -> p (t h)"), KTM.rearrange("p t h -> p (t h)"),
                                                   -1.0, None, ALU.mult))
            z_read = [pe.last(), q_stored]
            b = take_bank()
            pe.wait(mb)
            for k in range(KD):
                ins = nc.tensor.matmul(psum[b][:, 0:D], MB[:, k, :], WATT["wv"][:, k, :], start=(k == 0), stop=(k == KD - 1))
            dve.wait(pe.done(ins))
            bank_free[b] = dve.done(nc.vector.tensor_tensor(ROW[:, 1, :], psum[b][:, 0:D], BVB, ALU.add))
            dve.wait(bank_free[b])
            dve.wait(dve.done(nc.vector.tensor_tensor(ROW[:, 0, :], BVB, ROW[:, 1, :], ALU.subtract)))
            dve.wait(dve.done(nc.vector.tensor_scalar(ROW[:, 1, :], ROW[:, 0, :], 2.0, None, ALU.mult)))
            tot = 7
            pe.wait(bank_free[tot])
            u_free = [[None], [None]]
            vop_free = pe.last()
            parts_done = []
            for g in range(TB // 4):
                r = g % 2
                dve.wait(u_free[r])
                if g < 2:
                    dve.wait(pe.last())
                for half in range(2):
                    b = take_bank()
                    for i in range(2):
                        t = 4 * g + 2 * half + i
                        for k in range(KD):
                            ins = nc.tensor.matmul(psum[b][:, i * D:(i + 1) * D], XT[:, k, t * P:(t + 1) * P], WATT["wv"][:, k, :],
                                                   start=(k == 0), stop=(k == KD - 1))
                    dve.wait(pe.done(ins))
                    for i in range(2):
                        t = 4 * g + 2 * half + i
                        two = t not in ACT_KT
                        bank_free[b] = dve.done(nc.vector.scalar_tensor_tensor(
                            out=U[:, r, 2 * half + i, :, 0:DH],
                            in0=psum[b][:, i * D:(i + 1) * D].rearrange("p (h d) -> p h d", h=H),
                            scalar=2.0 if two else 1.0,
                            in1=ROW[:, int(two), :].rearrange("p (h d) -> p h d", h=H),
                            op0=ALU.mult, op1=ALU.add))
                dve.wait(bank_free[b])
                tt = slice(4 * g, 4 * g + 4)
                nc.vector.tensor_tensor(U[:, r, :, :, DH:2 * DH], U[:, r, :, :, 0:DH],
                                        KTM[:, tt, :].unsqueeze(3).broadcast_to([P, 4, H, DH]), ALU.mult)
                nc.vector.tensor_copy(U[:, r, :, :, 2 * DH], SCH[:, tt, :])
                whole = dve.done(nc.vector.tensor_tensor(U[:, r, :, :, 2 * DH + 1], KTM[:, tt, :], SCH[:, tt, :], ALU.mult))
                pe.wait(whole)
                for i in range(4):
                    t = 4 * g + i
                    weight = ONESF[:, 0:1] if t in ACT_KT else HALF[:, :]
                    ins = nc.tensor.matmul(psum[tot][0:1, :], weight, U[:, r, i, :, 0:2 * DH],
                                           start=(t == 0), stop=(t == TB - 1))
                summed = pe.done(ins)
                rows = lambda n: VOP[:, tt, :, n * VC:(n + 1) * VC].rearrange("p t h c -> p (t h) c")
                u = U[:, r, :, :, :].rearrange("p t h c -> p (t h) c")
                act.wait(whole, vop_free)
                hi = act.done(nc.scalar.activation(rows(0), u, ACT.Copy))
                dve.wait(hi, summed)
                rest = dve.done(nc.vector.tensor_tensor(u, u, rows(0), ALU.subtract))
                act.wait(rest)
                mid = act.done(nc.scalar.activation(rows(1), u, ACT.Copy))
                dve.wait(mid)
                lo = dve.done(nc.vector.tensor_tensor(rows(2), u, rows(1), ALU.subtract))
                u_free[r] = [lo]
                parts_done += [mid, lo]
            dve.wait(summed)
            bank_free[tot] = dve.done(nc.vector.tensor_copy(TOT, psum[tot][0:1, :]))
            b = take_bank()
            pe.wait(bank_free[tot])
            for h in range(H):
                ins = nc.tensor.matmul(psum[b][0:2 * DH, h:h + 1], TOT[:, h * 2 * DH:(h + 1) * 2 * DH], ONESF[0:1, 0:1],
                                       start=True, stop=True)
            dve.wait(pe.done(ins), cb_zero, act.last())
            bank_free[b] = dve.done(nc.vector.tensor_copy(CB[0:2 * DH, :], psum[b][0:2 * DH, 0:H]))
            return dict(q_stored=q_stored, z_read=z_read, nkt=nkt, parts=parts_done, cb=bank_free[b])

        def spread_q(hh, info):
            last = [sign_made[k] for k in sign_made if hh - 2 >= 0 and k // TB == hh - 2]
            act_dve = last + (info["z_read"] if hh % H < 2 else [])
            qb_ready[hh] = load(QB[:, hh % 2, :], zq_rows[hh, :].partition_broadcast(P), info["q_stored"], act_dve)

        def sign_tile(hh, kt, info):
            g = hh * TB + kt
            h = hh % H
            after = [qb_ready[hh], pe_tile.get(g - RING)]
            if kt in ACT_KT:
                act.wait(after, info["nkt"], info["parts"])
                sign_made[g] = act.done(nc.scalar.activation(SG[:, g % RING, :], QB[:, hh % 2, :], ACT.Sign,
                                                             bias=NKT[:, kt, h:h + 1]))
            else:
                dve.wait(after, info["nkt"], info["parts"])
                sign_made[g] = dve.done(nc.vector.tensor_scalar(SG[:, g % RING, :], QB[:, hh % 2, :], KTM[:, kt, h:h + 1],
                                                                0.5, ALU.is_gt, ALU.subtract))

        def accumulate(hh, kt, chunks, info):
            g = hh * TB + kt
            pe.wait(sign_made[g], info["parts"])
            for c in chunks:
                b = bank_of(hh, c)
                if kt == 0:
                    pe.wait(bank_free[b])
                ins = nc.tensor.matmul(psum[b][0:VP, :], VOP[:, kt, hh % H, :], SG[:, g % RING, c * BANK:(c + 1) * BANK],
                                       start=(kt == 0), stop=(kt == TB - 1))
            if chunks[-1] == 3:
                pe_tile[g] = pe.done(ins)

        def evacuate(hh, info):
            for c in range(4):
                b = bank_of(hh, c)
                act.wait(pe_tile[hh * TB + TB - 1], os_free[0], info["cb"])
                evac[hh, c] = bank_free[b] = act.done(nc.scalar.activation(
                    OS[0:VP, c * BANK:(c + 1) * BANK], psum[b][0:VP, :], ACT.Identity, bias=CB[:, hh % H:hh % H + 1]))

        turned, summed = {}, {}

        def turn_back(hh, c):
            b = 6 + c % 2
            pe.wait(evac[hh, c], bank_free[b])
            for i in range(4):
                ins = nc.tensor.transpose(psum[b][:, i * VP:(i + 1) * VP], OS[0:VP, (4 * c + i) * P:(4 * c + i + 1) * P],
                                          IDENT[0:VP, 0:VP])
            turned[hh, c] = pe.done(ins)
            if c == 3:
                os_free[0] = turned[hh, c]

        def sum_parts(hh, c):
            b = 6 + c % 2
            dve.wait(turned[hh, c], a_free[hh % 2])
            summed[hh, c] = bank_free[b] = dve.done(nc.vector.tensor_reduce(
                A[:, hh % 2, 4 * c:4 * c + 4, :],
                psum[b][:, 0:4 * VP].rearrange("p (i n c) -> p i c n", i=4, n=3), AX_X, ALU.add))

        norm = {}

        def norm_first(hh):
            r = hh % 2
            pool.wait(summed[hh, 3])
            q = QTM[:, :, hh % H]
            pool.wait(pool.done(nc.gpsimd.tensor_tensor(N1[:, r, :], A[:, r, :, 2 * DH], q, ALU.mult)))
            norm[hh] = pool.done(nc.gpsimd.tensor_tensor(N2[:, r, :], N1[:, r, :], A[:, r, :, 2 * DH + 1], ALU.subtract))
            pool.wait(pool.done(nc.gpsimd.tensor_tensor(CT, A[:, r, :, 0:DH], q.unsqueeze(2).broadcast_to([P, TB, DH]),
                                                        ALU.mult)))
            pool.wait(pool.done(nc.gpsimd.tensor_tensor(CT, CT, A[:, r, :, DH:2 * DH], ALU.subtract)))

        def norm_second(hh):
            r = hh % 2
            dve.wait(norm[hh])
            dve.wait(dve.done(nc.vector.tensor_scalar(N2[:, r, :], N2[:, r, :], NORM_MIN, None, ALU.max)))
            norm[hh] = dve.done(nc.vector.reciprocal(N1[:, r, :], N2[:, r, :]))

        def add_context(hh):
            r, batch, h = hh % 2, hh // H, hh % H
            pool.wait(norm[hh])
            pool.wait(pool.done(nc.gpsimd.tensor_tensor(CT, CT, N1[:, r, :].unsqueeze(2).broadcast_to([P, TB, DH]), ALU.mult)))
            x = X[:, batch * TB:(batch + 1) * TB, h * DH:(h + 1) * DH]
            a_free[r] = [pool.done(nc.gpsimd.tensor_tensor(x, x, CT, ALU.add))]
            pool.wait(a_free[r])

        def after_head(hh, kt):
            if kt in (6, 8, 10, 12):
                turn_back(hh, (kt - 6) // 2)
            if kt in (7, 9, 11, 13):
                sum_parts(hh, (kt - 7) // 2)
            if kt == 13:
                norm_first(hh)
            if kt == 15:
                norm_second(hh)
                add_context(hh)

        for batch in range(B):
            info = prepare(batch)
            heads = range(batch * H, (batch + 1) * H)
            spread_q(heads[0], info)
            for hh in heads:
                for kt in range(AHEAD):
                    sign_tile(hh, kt, info)
                if hh > heads[0]:
                    evacuate(hh - 1, info)
                if hh + 1 in heads:
                    spread_q(hh + 1, info)
                for chunks in ((0, 1), (2, 3)):
                    for kt in range(3):
                        accumulate(hh, kt, chunks, info)
                for kt in range(3, TB):
                    if kt - 3 + AHEAD < TB:
                        sign_tile(hh, kt - 3 + AHEAD, info)
                    accumulate(hh, kt, (0, 1, 2, 3), info)
                    if hh > heads[0]:
                        after_head(hh - 1, kt)
            evacuate(heads[-1], info)
            for kt in range(TB):
                after_head(heads[-1], kt)
            for t in range(batch * TB, (batch + 1) * TB):
                x_ready[t] = pool.last()
        st["xn_free"] = [pe.last(), act.last()]

    def mixer():
        xn = XN[:, :, :].rearrange("p t d -> p (t d)")
        add_everything()
        XT = xn[:, 0:4096].rearrange("p (k n) -> p k n", k=KD)
        INP = xn[:, 4096:8192].rearrange("p (k n) -> p k n", k=KD)
        at = [0]

        def part(n, parts=P):
            at[0] += n
            assert at[0] <= ARENA_N, at[0]
            return carve(at[0] - n, n, parts)

        SHIFT = part(KD * (S + 1)).rearrange("p (k n) -> p k n", k=KD)
        HT = part(KD * S).rearrange("p (k n) -> p k n", k=KD)
        STATE = part(KD * S).rearrange("p (k n) -> p k n", k=KD)
        WIN = part(KD * D).rearrange("p (k n) -> p k n", k=KD)
        WOUT = part(KD * D).rearrange("p (k n) -> p k n", k=KD)
        BIN = part(KD)
        BOUT = part(D)
        SCAL = part(3)
        TMPO = part(4 * 2 * D).rearrange("p (r i d) -> p r i d", r=4, i=2)
        free = st["arena_free"]
        wt = [load(WIN, a["win_t"].rearrange("(k p) n -> p k n", p=P), free),
              load(WOUT, a["wout_t"].rearrange("(k p) n -> p k n", p=P), free),
              load(BIN, a["bin"], free),
              load(BOUT, a["bout"].partition_broadcast(P), free),
              load(SCAL[:, 0:1], a["decay"].partition_broadcast(P), free),
              load(SCAL[:, 1:2], a["mix"].partition_broadcast(P), free)]
        for q in (pe, dve, act):
            q.wait(wt, free)
        dve.wait(dve.done(nc.vector.tensor_scalar(SCAL[:, 2:3], SCAL[:, 1:2], -1.0, 1.0, ALU.mult, ALU.add)))
        dve.wait(dve.done(nc.vector.memset(SHIFT[:, :, 0:1], 0.0)))
        tmp_free = [None] * 4
        for batch in range(B):
            xt = transposed(batch, XT, dve.last())
            dve.wait(xt, pe.last())
            dve.wait(dve.done(nc.vector.tensor_scalar(SHIFT[:, :, 1:S + 1], XT[:, :, :], SCAL[:, 2:3], None, ALU.mult)))
            mixed = []
            for k in range(KD):
                mixed.append(dve.done(nc.vector.scalar_tensor_tensor(
                    out=INP[:, k, :], in0=XT[:, k, :], scalar=SCAL[:, 1:2], in1=SHIFT[:, k, 0:S], op0=ALU.mult, op1=ALU.add)))
            pe.wait(mixed)
            scan_ready = []
            for m in range(KD):
                for c in range(S // BANK):
                    b = take_bank()
                    for k in range(KD):
                        ins = nc.tensor.matmul(psum[b][:, :], WIN[:, k, m * P:(m + 1) * P], INP[:, k, c * BANK:(c + 1) * BANK],
                                               start=(k == 0), stop=(k == KD - 1))
                    act.wait(pe.done(ins), dve.last() if batch else None)
                    bank_free[b] = act.done(nc.scalar.activation(HT[:, m, c * BANK:(c + 1) * BANK], psum[b][:, :], ACT.Relu,
                                                                 bias=BIN[:, m:m + 1]))
                dve.wait(bank_free[b])
                scan_ready.append(dve.done(nc.vector.tensor_tensor_scan(
                    STATE[:, m, :], SCAL[:, 0:1].broadcast_to([P, S]), HT[:, m, :], 0.0, ALU.mult, ALU.add)))
            pe.wait(scan_ready)
            for pair in range(TB // 2):
                b = take_bank()
                for i in range(2):
                    t = 2 * pair + i
                    for k in range(KD):
                        ins = nc.tensor.matmul(psum[b][:, i * D:(i + 1) * D], STATE[:, k, t * P:(t + 1) * P], WOUT[:, k, :],
                                               start=(k == 0), stop=(k == KD - 1))
                r = pair % 4
                dve.wait(pe.done(ins), tmp_free[r])
                bank_free[b] = dve.done(nc.vector.tensor_tensor(
                    TMPO[:, r, :, :], psum[b][:, :].rearrange("p (i d) -> p i d", i=2),
                    BOUT.unsqueeze(1).broadcast_to([P, 2, D]), ALU.add))
                t = batch * TB + 2 * pair
                pool.wait(bank_free[b])
                tmp_free[r] = pool.done(nc.gpsimd.tensor_tensor(X[:, t:t + 2, :], X[:, t:t + 2, :], TMPO[:, r, :, :], ALU.add))
                x_ready[t] = x_ready[t + 1] = tmp_free[r]
        st["xn_free"] = [pe.last(), dve.last()]

    for n, phase in enumerate(PHASES):
        if phase == "moe0":
            moe0(PHASES[n + 1:n + 2] == ("moe1",))
        else:
            {"attn": attention, "moe1": moe1, "mixer": mixer}[phase]()
        st["arena_free"] = everything()

    add_everything()
    o_rows = out.rearrange("(t p) d -> p t d", p=P)
    for g in range(4):
        store(o_rows[:, 8 * g:8 * g + 8, :], X[:, 8 * g:8 * g + 8, :], [x_ready[t] for t in range(8 * g, 8 * g + 8)])
    sp.wait(stores.all(), loads.all())


def kernel(**inputs):
    import concourse.bacc as bacc
    from concourse.bass_utils import run_bass_kernel_spmd

    given = {n: np.asarray(v) for n, v in inputs.items()}
    column = lambda v: np.ascontiguousarray(v.reshape(KD, P).T)
    arrays = {
        "x": given["L0_attn_hidden_states"].reshape(T, D),
        "wg0": given["L0_ffn_wg"], "w0t": np.ascontiguousarray(given["L0_ffn_W"].transpose(0, 2, 1)),
        "b0": given["L0_ffn_b"],
        "wq": given["L0_attn_Wq"], "wk": given["L0_attn_Wk"], "wv": given["L0_attn_Wv"], "wp1": given["L0_attn_W1"],
        "wp2": given["L0_attn_W2"], "bq": given["L0_attn_bq"], "bk": given["L0_attn_bk"],
        "bp1": column(given["L0_attn_b1"]), "bp2": given["L0_attn_b2"].reshape(H, 1), "bv": given["L0_attn_bv"],
        "wg1": given["L1_ffn_Wg"], "bg1": given["L1_ffn_bg"], "w1": given["L1_ffn_W1"], "w2": given["L1_ffn_W2"],
        "b1": given["L1_ffn_b1"].reshape(1, E * D), "b2": given["L1_ffn_b2"].reshape(1, E * D),
        "win_t": np.ascontiguousarray(given["L1_attn_W_in"].T), "bin": column(given["L1_attn_b_in"]),
        "wout_t": np.ascontiguousarray(given["L1_attn_W_out"].T), "bout": given["L1_attn_b_out"],
        "decay": given["L1_attn_decay"].reshape(1), "mix": given["L1_attn_mix"].reshape(1),
    }
    nc = bacc.Bacc("TRN2", target_bir_lowering=False, num_devices=1)
    arrays = {n: np.ascontiguousarray(v) for n, v in arrays.items()}
    aps = {n: nc.dram_tensor("in_" + n, v.shape, mybir.dt.from_np(v.dtype), kind="ExternalInput").ap()
           for n, v in arrays.items()}
    out = nc.dram_tensor("out_tokens", [T, D], F32, kind="ExternalOutput").ap()
    program(nc, aps, out)
    r = run_bass_kernel_spmd(nc, [{"in_" + n: v for n, v in arrays.items()}], core_ids=[0])
    return r.results[0]["out_tokens"].reshape(B, S, D)
```

```python
from contextlib import ExitStack

import numpy as np

import concourse.bass as bass
from concourse import mybir

ALU = mybir.AluOpType
ACT = mybir.ActivationFunctionType
AX_X = mybir.AxisListType.X
F32 = mybir.dt.float32
BF16 = mybir.dt.bfloat16
I32 = mybir.dt.int32
F32R = mybir.dt.float32r

P = 128
B, S = 2, 2048
D = 256
KD = D // P
T = B * S
NT = T // P
TB = S // P
E = 8
CAP = T // E
NJ0 = T // P
NJ1 = 40
RW = D + 3
REGION = T + P
SPARE = E * REGION
GROUP = 8
TOKEN_CUTS = ((0, 4), (4, 8), (8, 16), (16, 24), (24, 32))
H = 16
DH = D // H
BANK = 512
LN_EPS = 1e-5
STD_EPS = 1e-6
NORM_MIN = 1e-4
PHASES = ("moe0", "attn", "moe0", "moe1", "mixer", "moe1")

VC = 2 * DH + 2
VP = 3 * VC
RING = 6
LAG = 2
STAGE_FLOATS = 31744
KEPT = (4 * KD + 1) * E * D
ROUNDED = 3 * 2 * D
COLUMNS = 4
RING_X = 5
AHEAD = 5
ACT_KT = (1, 4, 6, 9, 11, 14)


class Queue:

    def __init__(self, eng, sem):
        self.eng, self.sem, self.n, self.seen = eng, sem, 0, {}

    def wait(self, *ticks):
        for tick in ticks:
            if tick is None:
                continue
            if isinstance(tick, list):
                self.wait(*tick)
                continue
            sem, value = tick
            if self.seen.get(sem.name, 0) < value:
                self.eng.wait_ge(sem, value)
                self.seen[sem.name] = value

    def done(self, instruction):
        instruction.then_inc(self.sem, 1)
        self.n += 1
        return (self.sem, self.n)

    def last(self):
        return (self.sem, self.n) if self.n else None


class Transfers:

    def __init__(self, queue, sems):
        self.queue, self.sems, self.count, self.i = queue, sems, [0] * len(sems), 0

    def start(self, issue):
        k = self.i % len(self.sems)
        self.i += 1
        self.queue.wait((self.sems[k], self.count[k]) if self.count[k] else None)
        issue().then_inc(self.sems[k], 16)
        self.count[k] += 16
        return (self.sems[k], self.count[k])

    def all(self):
        return [(s, c) for s, c in zip(self.sems, self.count) if c]


def program(nc, a, out):
    with ExitStack() as ctx:
        build(nc, ctx, a, out)


def build(nc, ctx, a, out):
    def sb(name, shape, dt=F32):
        return ctx.enter_context(nc.sbuf_tensor(name, shape, dt))

    def sem(name):
        return ctx.enter_context(nc.semaphore(name))

    pe = Queue(nc.tensor, sem("pe_done"))
    dve = Queue(nc.vector, sem("dve_done"))
    act = Queue(nc.scalar, sem("act_done"))
    pool = Queue(nc.gpsimd, sem("pool_done"))
    sp = Queue(nc.sync, sem("sp_done"))
    loads = Transfers(sp, [sem(f"load{i}") for i in range(12)])
    stores = Transfers(sp, [sem(f"store{i}") for i in range(8)])
    scatters = Transfers(pool, [sem(f"scatter{i}") for i in range(16)])
    gathers = Transfers(pool, [sem(f"gather{i}") for i in range(8)])

    def load(dst, src, *after):
        sp.wait(*after)
        return loads.start(lambda: nc.sync.dma_start(dst, src))

    def store(dst, src, *after):
        sp.wait(*after)
        return stores.start(lambda: nc.sync.dma_start(dst, src))

    dram = lambda name, rows, width: nc.dram_tensor(name, [rows, width], F32, kind="Internal").ap()
    empty0 = dram("moe0_empty_slots", T, RW)
    slots0 = dram("moe0_slots", SPARE, RW)
    slots1 = dram("moe1_slots", SPARE + (NJ1 - NT) * P, RW)
    y_rows = dram("expert_rows", T + NJ1 * P, D)
    bias_parts = nc.dram_tensor("bias_parts", [2, 3, E * D], BF16, kind="Internal").ap()
    zq_rows = nc.dram_tensor("q_rows", [B * H, S], F32, kind="Internal").ap()

    X = sb("residual", [P, NT, D])
    XN = sb("normed", [P, NT, RW])
    XTR = sb("normed_T", [P, 3, 2, KD, P])
    STATS = sb("ln_stats", [P, 8, 6])
    MV = sb("ln_mean_var", [P, NT, 2])
    SD = sb("ln_std", [P, NT])
    RSTD = sb("ln_rstd", [P, NT])
    SHIFTS = sb("ln_shift", [P, NT])
    LG, SC, TMP = (sb(n, [P, E, GROUP]) for n in ("logits", "score", "route_tmp"))
    CHOSEN = sb("chosen_bf", [P, E, GROUP + 1], BF16)
    POS = sb("position", [P, 2, E, GROUP + 1])
    sm = {n: sb("r_" + n, [P, NT]) for n in ("max", "rank", "den", "gate", "keep", "slot")}
    SLOT = sb("slot_of_token", [P, NT], I32)
    CE = sb("tile_counts", [P, 4, E])
    LE = sb("tile_cmp", [P, 3, NJ1, E])
    GAPS = LE[:, :, :, :].rearrange("p i j e -> p (i j e)")[:, 0:NT * E].rearrange("p (t e) -> p t e", t=NT)
    TJ = sb("tile_f", [P, 4, NJ1])
    EXI = sb("tile_columns", [P, NJ1], I32)
    ROWI = sb("tile_row", [P, NJ1], I32)
    PADI = sb("pad_rows", [P, E], I32)
    PAD = sb("pad_source", [P, RW - 1 + E])
    IDENT = sb("identity", [P, P])
    UTRI = sb("upper_bf", [P, P], BF16)
    ONESB = sb("ones_bf", [P, P], BF16)
    ONESF = sb("ones_f", [P, P])
    HALF = sb("half_col", [P, 1])
    EPS = sb("eps", [P, 2])
    REV = sb("rank_of_expert", [P, E])
    REGCOL = sb("expert_region", [P, E])
    JROW = sb("tile_spare_row", [P, 2, NJ1])
    M128 = sb("tile_start", [P, NT])
    JCOL = sb("tile_index", [P, NJ1])
    SCH = sb("key_scale", [P, TB, H])
    WG0 = sb("wg0", [P, KD, E])
    WG1 = sb("wg1", [P, KD, E])
    BG1 = sb("bg1", [P, E])
    BIAS = sb("top1_biases", [P, 2, E * D // P])
    BIAS3 = sb("top1_bias_parts", [P, 2, 3, E * D // P], BF16)

    psum = [ctx.enter_context(nc.psum_tensor(f"bank{i}", [P, BANK], F32)) for i in range(8)]
    bank_free = [None] * 8
    turn = [0]

    def take_bank(choice=range(6)):
        choice = list(choice)
        b = choice[turn[0] % len(choice)]
        turn[0] += 1
        pe.wait(bank_free[b])
        return b

    stage_memory = ExitStack()
    stage_count = [0]

    def renew(floats):
        stage_memory.close()
        stage_count[0] += 1
        whole = stage_memory.enter_context(nc.sbuf_tensor(f"stage{stage_count[0]}", [P, floats], F32))
        used = [0]

        def part(n, parts=P):
            used[0] += n
            assert used[0] <= floats, (used[0], floats)
            return whole[0:parts, used[0] - n:used[0]]

        return part

    x_rows = a["x"].rearrange("(t p) d -> p t d", p=P)
    x_ready = [None] * NT
    for lo, hi in TOKEN_CUTS:
        tick = load(X[:, lo:hi, :], x_rows[:, lo:hi, :])
        for t in range(lo, hi):
            x_ready[t] = tick
    wg_ready = [load(WG0[:, :, :], a["wg0"].rearrange("(k p) e -> p k e", p=P)),
                load(WG1[:, :, :], a["wg1"].rearrange("(k p) e -> p k e", p=P)),
                load(BG1[:, :], a["bg1"].partition_broadcast(P))]

    nc.gpsimd.memset(IDENT[:, :], 0.0)
    nc.gpsimd.memset(UTRI[:, :], 1.0)
    nc.gpsimd.memset(ONESB[:, :], 1.0)
    nc.gpsimd.memset(ONESF[:, :], 1.0)
    nc.gpsimd.memset(HALF[:, :], 0.5)
    nc.gpsimd.memset(EPS[:, 0:1], LN_EPS)
    nc.gpsimd.memset(EPS[:, 1:2], STD_EPS)
    nc.gpsimd.memset(PAD[:, :], 0.0)
    nc.gpsimd.memset(CHOSEN[:, :, :], 0.0)
    pool.wait(pool.done(nc.gpsimd.memset(SCH[:, :, :], 2.0)))
    nc.gpsimd.affine_select(out=IDENT[:, :], in_=IDENT[:, :], compare_op=ALU.not_equal, fill=1.0, base=0,
                            pattern=[[-1, P]], channel_multiplier=1)
    nc.gpsimd.affine_select(out=UTRI[:, :], in_=UTRI[:, :], compare_op=ALU.is_ge, fill=0.0, base=-1,
                            pattern=[[1, P]], channel_multiplier=-1)
    for t in ACT_KT:
        nc.gpsimd.memset(SCH[:, t, :], 1.0)
    io = lambda ap, pat, base, cm: nc.gpsimd.iota(ap, pattern=pat, base=base, channel_multiplier=cm,
                                                  allow_small_or_imprecise_dtypes=True)
    io(REV[:, :], [[-1, E]], E, 0)
    io(M128[:, :], [[P, NT]], 0, 0)
    io(REGCOL[:, :], [[REGION, E]], 0, 0)
    number = lambda ap: ap[:, :, D:D + 1].bitcast(I32)[:, :, 0]
    io(PAD[:, D:D + E].bitcast(I32), [[P, E]], T, 1)
    io(JCOL[:, :], [[1, NJ1]], 0, 0)
    io(JROW[:, 1, :], [[P, NJ1]], SPARE - NT * P, 0)
    consts = pool.done(io(JROW[:, 0, :], [[P, NJ1]], 0, 0))

    biases_in = [load(BIAS[:, n, :], a[name].rearrange("o (p c) -> p (o c)", p=P)) for n, name in enumerate(("b1", "b2"))]
    bias_split = []

    tiles = lambda ap: ap.rearrange("(t p) d -> p t d", p=P)
    by_slot = slots0.rearrange("(e r) d -> e r d", r=REGION)[:, 0:CAP, :]

    def make_empty(EMPTY):
        pool.wait(pool.done(nc.gpsimd.memset(EMPTY, 0.0)))
        emptied = pool.done(io(number(EMPTY), [[P, NT]], T, 1))
        st["empty0"] = [store(tiles(by_slot[e]), EMPTY[:, e * CAP // P:(e + 1) * CAP // P, :], emptied) for e in range(E)]

    empty_made, spares_made = [], []

    def fill_scratch(EMPTY, *after):
        st["y_free"] = [store(tiles(y_rows[0:T, :]), EMPTY[:, :, 0:D], *after)]
        for n in range(2):
            pool.wait(biases_in[n])
            for i in range(3):
                pool.wait(pool.done(nc.gpsimd.tensor_copy(BIAS3[:, n, i, :], BIAS[:, n, :])))
                if i < 2:
                    pool.wait(pool.done(nc.gpsimd.tensor_tensor(BIAS[:, n, :], BIAS[:, n, :], BIAS3[:, n, i, :], ALU.subtract)))
            bias_split.append(store(bias_parts[n].rearrange("i (p c) -> p i c", p=P), BIAS3[:, n, :, :], pool.last()))

    def fill_spares(EMPTY, part, parts):
        cut = slice(part * NT // parts, (part + 1) * NT // parts)
        empty_made.append(store(tiles(empty0)[:, cut, :], EMPTY[:, cut, :]))
        if part:
            return
        spares = EMPTY[:, E:E + NJ1 - NT, :]
        spares_made.append(store(tiles(slots1[SPARE:SPARE + (NJ1 - NT) * P, :]), spares))

    st = {
        "xn_free": [],
        "empty0": None,
        "slots_free": [],
        "y_free": [],
        "arena_free": [],
        "xtr_free": [None] * 3,
    }

    def everything():
        return [q.last() for q in (pe, dve, act, pool)] + loads.all() + stores.all() + scatters.all() + gathers.all()

    def empty_slots():
        sp.wait(st["slots_free"], empty_made)
        st["empty0"] = stores.start(lambda: nc.sync.dma_start(by_slot, empty0.rearrange("(e r) d -> e r d", e=E)))

    x_pending = [None] * NT

    def current(t):
        if x_pending[t] is not None:
            update, x_pending[t] = x_pending[t], None
            update()
        return x_ready[t]

    def statistics(g):
        ticks = []
        for t in g:
            dve.wait(current(t), bn_free[t % 8])
            ticks.append(dve.done(nc.vector.bn_stats(STATS[:, t % 8, :], X[:, t, :])))
            if len(ticks) == 8 or t == g[-1]:
                for u, tick in zip(g[g.index(t) + 1 - len(ticks):], ticks):
                    dve.wait(tick)
                    bn_free[u % 8] = done = dve.done(nc.vector.bn_aggr(MV[:, u, :], STATS[:, u % 8, :]))
                ticks = []
        return done

    def scales(g, done):
        lo, hi = g[0], g[-1] + 1
        act.wait(done, consts)
        dve.wait(act.done(nc.scalar.activation(SD[:, lo:hi], MV[:, lo:hi, 1], ACT.Sqrt, bias=EPS[:, 0:1])))
        dve.wait(dve.done(nc.vector.reciprocal(RSTD[:, lo:hi], SD[:, lo:hi])))
        return dve.done(nc.vector.scalar_tensor_tensor(out=SHIFTS[:, lo:hi], in0=MV[:, lo:hi, 0], scalar=-1.0,
                                                       in1=RSTD[:, lo:hi], op0=ALU.mult, op1=ALU.mult))

    def normalise(t, dst, ready):
        act.wait(ready, x_ready[t])
        return act.done(nc.scalar.activation(dst, X[:, t, :], ACT.Identity, bias=SHIFTS[:, t:t + 1],
                                             scale=RSTD[:, t:t + 1]))

    def layernorm(tiles, dest):
        cuts = [0] + list(range(4, len(tiles), 8)) + [len(tiles)]
        groups = [tiles[lo:hi] for lo, hi in zip(cuts, cuts[1:])]
        ready = scales(groups[0], statistics(groups[0]))
        for i, g in enumerate(groups):
            following = groups[i + 1] if i + 1 < len(groups) else None
            done = statistics(following) if following else None
            for n, t in enumerate(g):
                if n == len(g) - 2 and following:
                    next_ready = scales(following, done)
                yield t, normalise(t, dest(t), ready)
            ready = next_ready if following else None

    bn_free = [None] * 8
    exps_free = [None]

    def route(kind, WG, part):
        act.wait(st["xn_free"])
        pool.wait(st["xn_free"])
        numbered = pool.done(nc.gpsimd.iota(number(XN), pattern=[[P, NT]], base=0, channel_multiplier=1))
        pe.wait(bank_free[6], bank_free[7], wg_ready, consts)
        normed, evacuated, logits_made = [None] * NT, {}, {}
        slots = slots0 if kind == "moe0" else slots1
        dve.wait(consts)

        LT = part(3 * 2 * P, E).rearrange("e (r n) -> e r n", r=3)
        by_expert, lt_ready, lt_free = {}, {}, [None] * 3

        def logits(pair):
            slot = pair % 3
            b = by_expert[pair] = take_bank()
            pe.wait(evacuated[pair])
            for k in range(KD):
                ins = nc.tensor.matmul(psum[b][0:E, 0:2 * P], WG[:, k, :],
                                       XTR[:, slot, :, :, :].rearrange("p i k c -> p (i k c)")[:, k * 2 * P:(k + 1) * 2 * P],
                                       start=(k == 0), stop=(k == KD - 1))
            st["xtr_free"][slot] = lt_ready[pair] = pe.done(ins)

        def turn_logits(pair):
            slot, b = pair % 3, by_expert[pair]
            act.wait(lt_ready[pair], lt_free[slot], st["arena_free"])
            bank_free[b] = act.done(nc.scalar.activation(LT[:, slot, :], psum[b][0:E, 0:2 * P], ACT.Copy))
            group = 2 * pair // GROUP
            bank = 6 + group % 2
            pe.wait(bank_free[b], bank_free[bank])
            for i in range(2):
                t = (2 * pair + i) % GROUP
                ins = nc.tensor.transpose(psum[bank][:, t * E:(t + 1) * E], LT[:, slot, i * P:(i + 1) * P], IDENT[0:E, 0:E])
            lt_free[slot] = logits_made[group] = pe.done(ins)

        def step(ins):
            dve.wait(dve.done(ins))

        def place(group):
            lo, hi = group * GROUP, (group + 1) * GROUP
            by_tile = lambda ap: ap.rearrange("p e t -> p t e")
            over_e = lambda ap: ap[:, lo:hi].unsqueeze(1).broadcast_to([P, E, GROUP])
            over_t = lambda ap, n=GROUP: ap.unsqueeze(2).broadcast_to([P, E, n])
            col = {name: ap[:, lo:hi] for name, ap in sm.items()}
            bank = 6 + group % 2
            lg = psum[bank][:, 0:GROUP * E].rearrange("p (t e) -> p e t", e=E)
            dve.wait(logits_made[group])
            if kind == "moe1":
                step(nc.vector.tensor_tensor(LG[:, :, :], lg, over_t(BG1[:, :]), ALU.add))
                lg = LG[:, :, :]
            step(nc.vector.tensor_reduce(col["max"], by_tile(lg), AX_X, ALU.max))
            step(nc.vector.tensor_tensor(TMP[:, :, :], lg, over_e(sm["max"]), ALU.is_equal))
            step(nc.vector.tensor_tensor(SC[:, :, :], TMP[:, :, :], over_t(REV[:, :]), ALU.mult))
            step(nc.vector.tensor_reduce(col["rank"], by_tile(SC[:, :, :]), AX_X, ALU.max))
            step(nc.vector.tensor_tensor(CHOSEN[:, :, 0:GROUP], SC[:, :, :], over_e(sm["rank"]), ALU.is_equal))
            pe.wait(dve.last())
            b = take_bank()
            before = psum[b][:, 0:E * (GROUP + 1)].rearrange("p (e t) -> p e t", e=E)
            nc.tensor.matmul(before, UTRI[:, :], CHOSEN[:, :, :], start=True, stop=False)
            for s in range(1, GROUP + 1):
                counted = nc.tensor.matmul(before[:, :, s:GROUP + 1], ONESB[:, :], CHOSEN[:, :, 0:GROUP + 1 - s],
                                           start=False, stop=(s == GROUP))
            counted = pe.done(counted)
            if kind == "moe0":
                dve.wait(exps_free[0])
                step(nc.vector.tensor_tensor(GAPS[:, lo:hi, :].rearrange("p t e -> p e t"), lg, over_e(sm["max"]),
                                             ALU.subtract))
            bank_free[bank] = dve.last()
            start = POS[:, (group - 1) % 2, :, GROUP] if group else REGCOL[:, :]
            pos = POS[:, group % 2, :, :]
            dve.wait(counted)
            step(nc.vector.tensor_tensor(pos, before, over_t(start, GROUP + 1), ALU.add))
            bank_free[b] = dve.last()
            if kind == "moe1" and group == NT // GROUP - 1:
                step(nc.vector.tensor_copy(PADI[:, :], pos[:, :, GROUP]))
                pads_from.append(dve.last())
            step(nc.vector.tensor_tensor(TMP[:, :, :], CHOSEN[:, :, 0:GROUP], pos[:, :, 0:GROUP], ALU.mult))
            step(nc.vector.tensor_reduce(col["slot"], by_tile(TMP[:, :, :]), AX_X, ALU.add))
            step(nc.vector.tensor_copy(SLOT[:, lo:hi], col["slot"]))
            slots_ready = dve.last()
            pool.wait(slots_ready, numbered, st["slots_free"], st["empty0"] if kind == "moe0" else None)
            pool.wait(normed[hi - 1])
            nc.gpsimd.tensor_copy(XN[:, lo:hi, D + 1], MV[:, lo:hi, 0])
            pool.wait(pool.done(nc.gpsimd.tensor_copy(XN[:, lo:hi, D + 2], SD[:, lo:hi])))
            for t in range(lo, hi):
                pool.wait(normed[t])
                scatters.start(lambda: nc.gpsimd.indirect_dma_start(
                    out=slots, out_offset=bass.IndirectOffsetOnAxis(ap=SLOT[:, t:t + 1], axis=0),
                    in_=XN[:, t, :], in_offset=None))

        def turn(pair):
            b = turned_bank[pair] = take_bank()
            pe.wait(normed[2 * pair + 1])
            for i in range(2):
                for k in range(KD):
                    ins = nc.tensor.transpose(psum[b][:, (2 * k + i) * P:(2 * k + i + 1) * P],
                                              XN[:, 2 * pair + i, k * P:(k + 1) * P], IDENT[:, :])
            turned[pair] = pe.done(ins)

        def take_turned(pair):
            b = turned_bank[pair]
            act.wait(turned[pair], st["xtr_free"][pair % 3])
            evacuated[pair] = bank_free[b] = act.done(nc.scalar.activation(
                XTR[:, pair % 3, :, :, :].rearrange("p i k c -> p (i k c)"), psum[b][:, :], ACT.Copy))

        def after_pair(pair):
            if 0 <= pair - LAG < NT // 2:
                take_turned(pair - LAG)
            if 0 <= pair - LAG - 1 < NT // 2:
                logits(pair - LAG - 1)
            if 0 <= pair - LAG - 2 < NT // 2:
                turn_logits(pair - LAG - 2)
                if 2 * (pair - LAG - 1) % GROUP == 0:
                    place(2 * (pair - LAG - 1) // GROUP - 1)

        pads_from = []
        turned, turned_bank = {}, {}
        for t, tick in layernorm(list(range(NT)), lambda t: XN[:, t, 0:D]):
            normed[t] = tick
            if t % 2:
                turn(t // 2)
                after_pair(t // 2)
        for pair in range(NT // 2, NT // 2 + LAG + 2):
            after_pair(pair)
        if kind == "moe0":
            act.wait(dve.last())
            dve.wait(act.done(nc.scalar.activation(GAPS[:, :, :], GAPS[:, :, :], ACT.Exp)))
            step(nc.vector.tensor_reduce(sm["den"][:, :], GAPS[:, :, :], AX_X, ALU.add))
            exps_free[0] = dve.last()
            step(nc.vector.reciprocal(sm["gate"][:, :], sm["den"][:, :]))
            step(nc.vector.scalar_tensor_tensor(out=sm["slot"][:, :], in0=sm["rank"][:, :], scalar=float(REGION),
                                                in1=sm["slot"][:, :], op0=ALU.mult, op1=ALU.add))
            step(nc.vector.tensor_scalar(sm["keep"][:, :], sm["slot"][:, :], float(E * REGION + CAP), None, ALU.is_lt))
            step(nc.vector.tensor_tensor(sm["gate"][:, :], sm["gate"][:, :], sm["keep"][:, :], ALU.mult))
            step(nc.vector.tensor_scalar(sm["gate"][:, :], sm["gate"][:, :], 0.5, None, ALU.mult))
            return scatters.all(), dve.last()
        over_j = lambda ap: ap.unsqueeze(1).broadcast_to([P, NJ1, E])
        tile_j = JCOL[:, :].unsqueeze(2).broadcast_to([P, NJ1, E])
        cnt = CE[:, 3, :]
        step(nc.vector.tensor_tensor(cnt, POS[:, (NT // GROUP - 1) % 2, :, GROUP], REGCOL[:, :], ALU.subtract))
        counts = LE[:, 0, 0:NT, :].rearrange("p t e -> p e t")
        sp.wait(pads_from, st["slots_free"], consts)
        padded = []
        for e in range(E):
            row = nc.sync.value_load(PADI[0:1, e:e + 1], min_val=0, max_val=SPARE - P)
            padded.append(store(slots[bass.ds(row, P), :], PAD[:, e:e + RW]))
        step(nc.vector.tensor_tensor(counts, cnt.unsqueeze(2).broadcast_to([P, E, NT]),
                                     M128[:, :].unsqueeze(1).broadcast_to([P, E, NT]), ALU.is_gt))
        step(nc.vector.tensor_reduce(CE[:, 0, :], counts, AX_X, ALU.add))
        step(nc.vector.tensor_tensor_scan(CE[:, 1, :], ONESF[:, 0:E], CE[:, 0, :], 0.0, ALU.mult, ALU.add))
        step(nc.vector.tensor_tensor(CE[:, 2, :], CE[:, 1, :], CE[:, 0, :], ALU.subtract))
        step(nc.vector.tensor_tensor(LE[:, 1, :, :], over_j(CE[:, 1, :]), tile_j, ALU.is_le))
        step(nc.vector.tensor_reduce(TJ[:, 0, :], LE[:, 1, :, :], AX_X, ALU.add))
        step(nc.vector.tensor_scalar(EXI[:, :], TJ[:, 0, :], float(E - 1), float(D), ALU.min, ALU.mult))
        step(nc.vector.tensor_scalar(CE[:, 3, :], CE[:, 2, :], -float(P), None, ALU.mult))
        step(nc.vector.tensor_tensor(CE[:, 3, :], CE[:, 3, :], REGCOL[:, :], ALU.add))
        step(nc.vector.tensor_tensor(LE[:, 2, :, :], over_j(CE[:, 2, :]), tile_j, ALU.is_le))
        step(nc.vector.tensor_tensor(LE[:, 0, :, :], LE[:, 2, :, :], LE[:, 1, :, :], ALU.subtract))
        step(nc.vector.tensor_reduce(TJ[:, 1, :], LE[:, 0, :, :], AX_X, ALU.add))
        step(nc.vector.tensor_tensor(LE[:, 2, :, :], LE[:, 0, :, :], over_j(CE[:, 3, :]), ALU.mult))
        step(nc.vector.tensor_reduce(TJ[:, 2, :], LE[:, 2, :, :], AX_X, ALU.add))
        step(nc.vector.tensor_tensor(TJ[:, 3, :], JROW[:, 0, :], JROW[:, 1, :], ALU.subtract))
        step(nc.vector.tensor_tensor(TJ[:, 3, :], TJ[:, 3, :], TJ[:, 1, :], ALU.mult))
        step(nc.vector.tensor_tensor(TJ[:, 3, :], TJ[:, 3, :], JROW[:, 1, :], ALU.add))
        step(nc.vector.tensor_tensor(ROWI[:, :], TJ[:, 3, :], TJ[:, 2, :], ALU.add))
        return scatters.all() + padded, dve.last()

    def return_rows(YS_tile, number_of, *after, to=y_rows):
        pool.wait(*after, st["y_free"])
        return gathers.start(lambda: nc.gpsimd.indirect_dma_start(
            out=to, out_offset=bass.IndirectOffsetOnAxis(ap=number_of, axis=0), in_=YS_tile, in_offset=None))

    def add_rows(scale):
        back = gathers.all() + weights1
        last = []
        for lo, hi in TOKEN_CUTS:
            got = load(XN[:, lo:hi, 0:D], tiles(y_rows[lo * P:hi * P, :]), back)
            last.append(got)
            for t in range(lo, hi):
                def update(t=t, got=got):
                    dve.wait(got)
                    x_ready[t] = dve.done(nc.vector.scalar_tensor_tensor(
                        out=X[:, t, :], in0=XN[:, t, 0:D], scalar=scale(t), in1=X[:, t, :], op0=ALU.mult, op1=ALU.add))
                x_pending[t] = update
        st["y_free"] = last
        st["xn_free"] = []

    def add_all(tiles=range(NT)):
        for t in tiles:
            current(t)

    def moe0(before_moe1):
        first_time = not empty_made
        part = renew(STAGE_FLOATS if first_time else STAGE_FLOATS - KEPT)
        ring = 3
        WT = part(KD * E * D).rearrange("p (k e f) -> p k e f", k=KD, e=E)
        BB = part(E * D).rearrange("p (e f) -> p e f", e=E)
        XS = part(RING_X * 2 * RW).rearrange("p (r i d) -> p r i d", r=RING_X, i=2)
        XST = part(ring * 2 * D).rearrange("p (r i k c) -> p r i k c", r=ring, i=2, k=KD)
        YS = part(ring * 2 * D).rearrange("p (r i d) -> p r i d", r=ring, i=2)
        if first_time:
            EMPTY = part(NT * RW).rearrange("p (t d) -> p t d", d=RW)
            make_empty(EMPTY)
        weights = [load(WT[:, k, :, :], a["w0t"][:, k * P:(k + 1) * P, :].rearrange("e p f -> p e f"), st["arena_free"])
                   for k in range(KD)]
        weights.append(load(BB[:, :, :], a["b0"].partition_broadcast(P)))
        scattered, gate_ready = route("moe0", WG0, part)
        if first_time:
            fill_scratch(EMPTY, act.last())
        st["empty0"] = None
        xs_free, xst_free, ys_free = [None] * RING_X, [None] * ring, [None] * ring
        n_pairs = NJ0 // 2
        xs_ready, xst_ready = {}, {}

        def fetch(j):
            xs_ready[j] = load(XS[:, j % RING_X, :, :], tiles(by_slot[2 * j * P // CAP, 2 * j * P % CAP:2 * j * P % CAP + 2 * P, :]), scattered,
                               xs_free[j % RING_X])

        def turn_pair(j):
            b = take_bank()
            pe.wait(xs_ready[j])
            for i in range(2):
                for k in range(KD):
                    ins = nc.tensor.transpose(psum[b][:, (2 * i + k) * P:(2 * i + k + 1) * P],
                                              XS[:, j % RING_X, i, k * P:(k + 1) * P], IDENT[:, :])
            pe.done(ins)
            act.wait(pe.last(), xst_free[j % ring], st["arena_free"])
            xst_ready[j] = bank_free[b] = act.done(nc.scalar.activation(
                XST[:, j % ring, :, :, :].rearrange("p i k c -> p (i k c)"), psum[b][:, :], ACT.Copy))

        def expert_pair(j):
            e = (2 * j) // (CAP // P)
            b = take_bank()
            pe.wait(xst_ready[j], weights)
            for i in range(2):
                for k in range(KD):
                    ins = nc.tensor.matmul(psum[b][:, i * D:(i + 1) * D], XST[:, j % ring, i, k, :], WT[:, k, e, :],
                                           start=(k == 0), stop=(k == KD - 1))
            xst_free[j % ring] = pe.done(ins)
            dve.wait(pe.last(), ys_free[j % ring], weights, st["arena_free"])
            bank_free[b] = dve.done(nc.vector.tensor_tensor(
                YS[:, j % ring, :, :], psum[b][:, :].rearrange("p (i f) -> p i f", i=2),
                BB[:, e, :].unsqueeze(1).broadcast_to([P, 2, D]), ALU.add))
            ys_free[j % ring] = [return_rows(YS[:, j % ring, i, :], XS[:, j % RING_X, i, D:D + 1].bitcast(I32),
                                             bank_free[b], xs_ready[j]) for i in range(2)]
            xs_free[j % RING_X] = ys_free[j % ring]

        for j in range(3):
            fetch(j)
        turn_pair(0)
        for j in range(n_pairs):
            if j + 3 < n_pairs:
                fetch(j + 3)
            if j + 1 < n_pairs:
                turn_pair(j + 1)
            expert_pair(j)
            if before_moe1 and j % 3 == 1:
                if j // 3 < len(WEIGHT_PARTS):
                    load_weights1(*WEIGHT_PARTS[j // 3], scattered)
                if j // 3 > 0:
                    split_weights1(*WEIGHT_PARTS[j // 3 - 1])
            if first_time and j % 2:
                fill_spares(EMPTY, j // 2, n_pairs // 2)
        st["slots_free"] = scattered + list(xs_ready.values())[-12:]
        add_rows(lambda t: sm["gate"][:, t:t + 1])

    kept = {}
    weights1, weights1_in = [], {}
    WEIGHT_PARTS = [(n, k) for n in range(2) for k in range(KD)]

    def keep_weights1():
        stage_memory.close()
        for name in ("hi", "lo"):
            for n in range(2):
                kept[name, n] = sb(f"w{n + 1}_{name}", [P, KD, E * D], F32R)
        for n in range(2):
            kept["bias", n] = sb(f"b{n + 1}_parts", [3, E * D], BF16)
        ctx.callback(stage_memory.close)

    weights1_raw = lambda n, k: XN[:, :, :].rearrange("p t d -> p (t d)")[:, (KD * n + k) * E * D:(KD * n + k + 1) * E * D]

    def load_weights1(n, k, scattered):
        weights1_in[n, k] = load(weights1_raw(n, k).rearrange("p (e f) -> p e f", e=E),
                                 a["w1" if n == 0 else "w2"][:, k * P:(k + 1) * P, :].rearrange("e p f -> p e f"),
                                 scattered)
        if k == 0:
            weights1.append(load(kept["bias", n][:, :], bias_parts[n], bias_split, st["arena_free"]))

    def split_weights1(n, k):
        raw, hi, lo = weights1_raw(n, k), kept["hi", n][:, k, :], kept["lo", n][:, k, :]
        act.wait(weights1_in[n, k], st["arena_free"])
        dve.wait(act.done(nc.scalar.activation(hi, raw, ACT.Copy)), st["arena_free"])
        weights1.append(dve.done(nc.vector.tensor_tensor(lo, raw, hi.bitcast(F32), ALU.subtract)))

    def moe1(to_out):
        part = renew(STAGE_FLOATS - KEPT - 4 * ROUNDED)
        ring = 3
        stage_sb = lambda name: stage_memory.enter_context(
            nc.sbuf_tensor(f"{name}{stage_count[0]}", [P, 2, ring, 2, KD, P], F32R))
        XS = part(RING_X * 2 * RW).rearrange("p (r i d) -> p r i d", r=RING_X, i=2)
        XST, HT = stage_sb("rows_T"), stage_sb("hidden_T")
        HS = part(ring * 2 * D).rearrange("p (r i d) -> p r i d", r=ring, i=2)
        YS = part(ring * 2 * D).rearrange("p (r i d) -> p r i d", r=ring, i=2)
        weights = weights1
        rings_free = st["arena_free"]
        scattered, tiles_ready = route("moe1", WG1, part)
        n_pairs = NJ1 // 2
        free = {n: [None] * RING_X for n in ("xs", "xst", "hs", "ht", "ys")}
        ready = {n: {} for n in ("xs", "xst", "hs", "ht")}
        column = {}
        act.wait(rings_free)
        dve.wait(rings_free)

        def fetch(j):
            sp.wait(tiles_ready)
            ready["xs"][j] = []
            for i in range(2):
                row = nc.sync.value_load(ROWI[0:1, 2 * j + i:2 * j + i + 1], min_val=0, max_val=SPARE + (NJ1 - NT - 1) * P)
                ready["xs"][j].append(load(XS[:, j % RING_X, i, :], slots1[bass.ds(row, P), :], scattered, spares_made,
                                           free["xs"][j % RING_X], rings_free))

        def turn_pair(j, src, dst, SRC, DST):
            r, rs = j % ring, j % (RING_X if src == "xs" else ring)
            b = take_bank()
            pe.wait(ready[src][j])
            for i in range(2):
                for k in range(KD):
                    ins = nc.tensor.transpose(psum[b][:, (2 * i + k) * P:(2 * i + k + 1) * P],
                                              SRC[:, rs, i, k * P:(k + 1) * P], IDENT[:, :])
            turned = pe.done(ins)
            if src != "xs":
                free[src][r] = turned
            act.wait(turned, free[dst][r])
            hi, lo = (DST[:, n, r, :, :, :].rearrange("p i k c -> p (i k c)") for n in range(2))
            rounded = act.done(nc.scalar.activation(hi, psum[b][:, :], ACT.Copy))
            dve.wait(rounded, free[dst][r])
            ready[dst][j] = bank_free[b] = dve.done(nc.vector.tensor_tensor(lo, psum[b][:, :], hi.bitcast(F32), ALU.subtract))

        def read_columns(t):
            pe.wait(tiles_ready)
            _, columns = nc.values_load_multi_w_load_instructions(
                EXI[0:1, t:t + COLUMNS], engines=(mybir.EngineType.PE,), min_val=0, max_val=(E - 1) * D,
                skip_runtime_bounds_check_because="route() takes the smaller of it and E - 1 before it multiplies by D")
            column.update(zip(range(t, t + COLUMNS), columns))

        def layer(j, SRC, n, src):
            r = j % ring
            b = take_bank()
            pe.wait(ready[src][j], weights)
            for i in range(2):
                where = bass.ds(column[2 * j + i], D)
                for k in range(KD):
                    x_hi, x_lo = (SRC[:, s, r, i, k, :] for s in range(2))
                    w_hi, w_lo = (kept[s, n][:, k, where] for s in ("hi", "lo"))
                    for x, w in ((x_hi, w_hi), (x_hi, w_lo), (x_lo, w_hi)):
                        nc.tensor.matmul(psum[b][:, i * D:(i + 1) * D], x, w, start=(k == 0 and x is x_hi and w is w_hi),
                                         stop=False)
                ins = nc.tensor.matmul(psum[b][:, i * D:(i + 1) * D], ONESB[0:3, :], kept["bias", n][:, where],
                                       start=False, stop=True)
            free[src][r] = pe.done(ins)
            return b

        def first(j):
            b = layer(j, XST, 0, "xst")
            act.wait(pe.last(), free["hs"][j % ring])
            ready["hs"][j] = bank_free[b] = act.done(nc.scalar.activation(
                HS[:, j % ring, :, :].rearrange("p i d -> p (i d)"), psum[b][:, :], ACT.Gelu))

        def second(j):
            b = layer(j, HT, 1, "ht")
            ys = YS[:, j % ring, :, :]
            if to_out:
                dve.wait(ready["xs"][j], free["ys"][j % ring])
                for i in range(2):
                    xs = XS[:, j % RING_X, i, :]
                    x = dve.done(nc.vector.tensor_scalar(ys[:, i, :], xs[:, 0:D], xs[:, D + 2:D + 3], xs[:, D + 1:D + 2],
                                                         ALU.mult, ALU.add))
                dve.wait(pe.last(), x)
                bank_free[b] = dve.done(nc.vector.scalar_tensor_tensor(
                    out=ys, in0=psum[b][:, :].rearrange("p (i d) -> p i d", i=2), scalar=0.5, in1=ys, op0=ALU.mult, op1=ALU.add))
            else:
                dve.wait(pe.last(), free["ys"][j % ring])
                bank_free[b] = dve.done(nc.vector.tensor_copy(ys.rearrange("p i d -> p (i d)"), psum[b][:, :]))
            free["ys"][j % ring] = free["xs"][j % RING_X] = [
                return_rows(ys[:, i, :], XS[:, j % RING_X, i, D:D + 1].bitcast(I32),
                            bank_free[b], ready["xs"][j], to=out if to_out else y_rows) for i in range(2)]

        for j in range(n_pairs + 4):
            if 0 <= j - 4 < n_pairs:
                second(j - 4)
            if j < n_pairs:
                fetch(j)
            if 0 <= j - 3 < n_pairs:
                turn_pair(j - 3, "hs", "ht", HS, HT)
            if 0 <= j - 2 < n_pairs:
                first(j - 2)
            if 2 * j % COLUMNS == 0 and j < n_pairs:
                read_columns(2 * j)
            if 0 <= j - 1 < n_pairs:
                turn_pair(j - 1, "xs", "xst", XS, XST)
        if to_out:
            return
        st["slots_free"] = scattered + [x for j in range(n_pairs - 6, n_pairs) for x in ready["xs"][j]]
        add_rows(lambda t: 0.5)

    LNR = XTR[:, :, :, :, :].rearrange("p r i k c -> p r i (k c)")

    def turn_pair_of(pair, normed):
        slot = pair % 3
        act.wait(st["xtr_free"][slot])
        tick = [normed(i) for i in range(2)][-1]
        b = take_bank() if pair < TB // 2 else 6 + pair % 2
        pe.wait(tick, consts, bank_free[b])
        for i in range(2):
            for k in range(KD):
                ins = nc.tensor.transpose(psum[b][:, (2 * k + i) * P:(2 * k + i + 1) * P],
                                          LNR[:, slot, i, k * P:(k + 1) * P], IDENT[:, :])
        st["xtr_free"][slot] = pe.done(ins)
        return b, pe.last()

    def take_pair(pair, turned, XT):
        b, tick = turned
        at = 2 * (pair % (TB // 2)) * P
        act.wait(tick)
        bank_free[b] = act.done(nc.scalar.activation(
            XT[:, :, at:at + 2 * P], psum[b][:, :].rearrange("p (k c) -> p k c", k=KD), ACT.Copy))
        return bank_free[b]

    def transposed(XT, xt_free):
        act.wait(xt_free, st["xn_free"])
        normed = layernorm(list(range(TB)), lambda t: LNR[:, t // 2 % 3, t % 2, :])
        turned = {}
        for pair in range(TB // 2 + LAG):
            if pair < TB // 2:
                turned[pair] = turn_pair_of(pair, lambda i: next(normed)[1])
            if pair >= LAG:
                reached = range(((KD - 1) * S + 2 * (pair - LAG + 1) * P) // RW + 1)
                add_all(reached)
                act.wait([x_ready[t] for t in reached])
                tick = take_pair(pair - LAG, turned[pair - LAG], XT)
        add_all()
        act.wait([x_ready[t] for t in range(NT)])
        return tick

    def attention():
        xn = XN[:, :, :].rearrange("p t d -> p (t d)")
        XT = xn[:, 0:4096].rearrange("p (k n) -> p k n", k=KD)
        OS = xn[:, KD * S:(KD + 1) * S]
        upper = [(KD + 1) * S]

        def beside(n, parts=P):
            upper[0] += n
            assert upper[0] <= NT * RW
            return xn[0:parts, upper[0] - n:upper[0]]

        part = renew(STAGE_FLOATS - 2 * KD * D - 4 * KD * BANK)
        W1R = stage_memory.enter_context(nc.sbuf_tensor("hidden_weights", [P, 2, KD, D], F32R))
        PT = stage_memory.enter_context(nc.sbuf_tensor("q_or_k_T", [P, 2, 2, KD, BANK], F32R))
        VOP_F = part(TB * H * VP // 2)
        VOP = VOP_F.bitcast(BF16).rearrange("p (t h c) -> p t h c", t=TB, h=H)
        signs_flat = part(RING * S // 2)
        SG = signs_flat.bitcast(BF16).rearrange("p (r n) -> p r n", r=RING)
        GT = signs_flat[:, 2 * S:3 * S].rearrange("p (r m n) -> p r m n", r=2, m=KD)
        U = signs_flat[:, 0:2 * 4 * H * VC].rearrange("p (r t h c) -> p r t h c", r=2, t=4, h=H)
        QB = part(2 * S).rearrange("p (r n) -> p r n", r=2)
        Z = QB[0:H, :, :]
        HM = VOP_F[:, 0:2 * H * D].rearrange("p (s h l d) -> p s h l d", s=2, h=H, l=S // P)
        QTM = beside(TB * H).rearrange("p (t h) -> p t h", t=TB)
        KTM = beside(TB * H).rearrange("p (t h) -> p t h", t=TB)
        NKT = beside(TB * H).rearrange("p (t h) -> p t h", t=TB)
        A = part(2 * TB * VC).rearrange("p (r t c) -> p r t c", r=2, t=TB)
        BQK = A[:, 0, :, :].rearrange("p t c -> p (t c)")[:, 0:2 * D].rearrange("p (s d) -> p s d", s=2)
        N1 = beside(2 * TB).rearrange("p (r t) -> p r t", r=2)
        N2 = beside(2 * TB).rearrange("p (r t) -> p r t", r=2)
        CT = beside(TB * DH).rearrange("p (t d) -> p t d", t=TB)
        WATT = {n: part(KD * D).rearrange("p (k n) -> p k n", k=KD) for n in ("wq", "wk", "wv")}
        WATT["wp1"] = QB[:, 0, 0:KD * D].rearrange("p (k n) -> p k n", k=KD)
        WP2 = part(KD * H).rearrange("p (k n) -> p k n", k=KD)
        BP1 = part(KD)
        BP2 = part(1, H)
        BVB = part(D)
        ROW = beside(2 * D).rearrange("p (s d) -> p s d", s=2)
        MEANS = part(KD)
        MB = part(KD * P).rearrange("p (k c) -> p k c", k=KD)
        ZST = part(2 * 4 * 6, H).rearrange("p (s c x) -> p s c x", s=2, c=4)
        ZMV = part(2 * 2, H).rearrange("p (s x) -> p s x", s=2)
        ZS = part(3, H)
        TOT = beside(H * 2 * DH, 1)
        CB = part(H, VP)

        free = st["arena_free"]
        wt = []
        for n in ("wq", "wk", "wv", "wp1"):
            wt.append(load(WATT[n], a[n].rearrange("(k p) n -> p k n", p=P), free))
        wt.append(load(WP2, a["wp2"].rearrange("(k p) n -> p k n", p=P), free))
        wt.append(load(BP1, a["bp1"], free))
        wt.append(load(BP2, a["bp2"], free))
        wt.append(load(BVB, a["bv"].partition_broadcast(P), free))
        pool.wait(free)
        cb_zero = pool.done(nc.gpsimd.memset(CB, 0.0))

        qb_ready = {}
        pe_tile = {}
        sign_made = {}
        bank_of = lambda hh, c: (4 * hh + c) % 6
        evac = {}
        os_free, a_free = [None], [[None], [None]]

        next_turned = {}

        def turn_next(step, hh):
            pair = hh - (H - 1 - TB // 2) + TB // 2
            if hh >= H or not TB // 2 <= pair < TB:
                return
            if step == 0:
                act.wait(next_turned["xt_free"])
                next_turned["at"] = turn_pair_of(pair, lambda i: normalise(2 * pair + i, LNR[:, pair % 3, i, :], next_turned["ready"]))
            if step == 1:
                next_turned["tick"] = take_pair(pair, next_turned["at"], XT)

        def prepare(batch):
            bias_rows = [load(BQK[:, n, :], a[name].partition_broadcast(P), free, pool.last())
                         for n, name in enumerate(("bq", "bk"))]
            if batch == 0:
                xt = transposed(XT, pe.last())
                act.wait(wt, free)
                hi = act.done(nc.scalar.activation(W1R[:, 0, :, :], WATT["wp1"], ACT.Copy))
                dve.wait(hi)
                pe.wait(dve.done(nc.vector.tensor_tensor(W1R[:, 1, :, :], WATT["wp1"], W1R[:, 0, :, :].bitcast(F32), ALU.subtract)))
            else:
                xt = next_turned["tick"]
            for q in (pe, dve, act):
                q.wait(wt, free)
            dve.wait(xt)
            dve.wait(dve.done(nc.vector.tensor_reduce(MEANS, XT[:, :, :], AX_X, ALU.add)))
            for k in range(KD):
                mb = dve.done(nc.vector.tensor_scalar(MB[:, k, :], ONESF[:, :], MEANS[:, k:k + 1], 1.0 / S,
                                                      ALU.mult, ALU.mult))
            z_ready = {}
            nchunk = S // BANK
            pt_free, gt_free = [None, None], [None, None]
            steps = [(s, c) for s in range(2) for c in range(nchunk)]
            pt_ready, gt_ready = {}, {}
            vop_read = pe.last()
            z_free = [sign_made.get(k) for k in list(sign_made)[-16:]]

            by_head = {}

            def project(s):
                W = WATT["wq"] if s == 0 else WATT["wk"]
                dve.wait(bias_rows, vop_read)
                for l in range(0, S // P, 2):
                    b = take_bank()
                    for i in range(2):
                        for k in range(KD):
                            tokens = XT[:, k, :].rearrange("p (n l) -> p l n", l=S // P)[:, l + i, :]
                            ins = nc.tensor.matmul(psum[b][:, i * D:(i + 1) * D], tokens, W[:, k, :],
                                                   start=(k == 0), stop=(k == KD - 1))
                    dve.wait(pe.done(ins))
                    bank_free[b] = by_head[s] = dve.done(nc.vector.tensor_tensor(
                        HM[:, s, :, l:l + 2, :].rearrange("p h l d -> p l h d"),
                        psum[b][:, :].rearrange("p (l h d) -> p l h d", l=2, h=H),
                        BQK[:, s, :].rearrange("p (h d) -> p h d", h=H).unsqueeze(1).broadcast_to([P, 2, H, DH]), ALU.add))

            turned = {}

            def turn_rows(i):
                s, c = steps[i]
                pe.wait(by_head[s])
                for half in range(2):
                    b = take_bank()
                    for j in range(2):
                        row = HM[:, s, 4 * c + 2 * half + j, :, :].rearrange("p l d -> p (l d)")
                        for k in range(KD):
                            ins = nc.tensor.transpose(psum[b][:, (2 * k + j) * P:(2 * k + j + 1) * P],
                                                      row[:, k * P:(k + 1) * P], IDENT[:, :])
                    turned[half] = b, pe.done(ins)

            def take_rows(i):
                for half in range(2):
                    b, tick = turned[half]
                    rows = psum[b][:, :].rearrange("p (k c) -> p k c", k=KD)
                    hi, lo = (PT[:, i % 2, n, :, half * 2 * P:(half + 1) * 2 * P] for n in range(2))
                    act.wait(tick, pt_free[i % 2])
                    dve.wait(act.done(nc.scalar.activation(hi, rows, ACT.Copy)))
                    bank_free[b] = pt_ready[i] = dve.done(nc.vector.tensor_tensor(lo, rows, hi.bitcast(F32), ALU.subtract))

            def hidden(i):
                pe.wait(pt_ready[i])
                for m in range(KD):
                    b = take_bank()
                    for k in range(KD):
                        for n, (w, x) in enumerate(((0, 0), (0, 1), (1, 0))):
                            ins = nc.tensor.matmul(psum[b][:, :], W1R[:, w, k, m * P:(m + 1) * P], PT[:, i % 2, x, k, :],
                                                   start=(k == 0 and n == 0), stop=(k == KD - 1 and n == 2))
                    act.wait(pe.done(ins), gt_free[i % 2], signs_read)
                    bank_free[b] = gt_ready[i] = act.done(nc.scalar.activation(
                        GT[:, i % 2, m, :], psum[b][:, :], ACT.Gelu, bias=BP1[:, m:m + 1]))
                pt_free[i % 2] = pe.last()

            def score(i):
                s, c = steps[i]
                pe.wait(gt_ready[i])
                b = take_bank()
                for k in range(KD):
                    ins = nc.tensor.matmul(psum[b][0:H, :], WP2[:, k, :], GT[:, i % 2, k, :],
                                           start=(k == 0), stop=(k == KD - 1))
                gt_free[i % 2] = pe.done(ins)
                dve.wait(pe.last(), z_free)
                bank_free[b] = dve.done(nc.vector.tensor_scalar(Z[:, s, c * BANK:(c + 1) * BANK], psum[b][0:H, :],
                                                                BP2[:, 0:1], None, ALU.add))
                dve.wait(bank_free[b])
                z_ready[s] = dve.done(nc.vector.bn_stats(ZST[:, s, c, :], Z[:, s, c * BANK:(c + 1) * BANK]))

            u_free, v_made = [[None], [None]], {}

            def values(g):
                r = g % 2
                dve.wait(u_free[r], signs_read)
                for half in range(2):
                    b = take_bank()
                    for i in range(2):
                        t = 4 * g + 2 * half + i
                        for k in range(KD):
                            ins = nc.tensor.matmul(psum[b][:, i * D:(i + 1) * D], XT[:, k, t * P:(t + 1) * P], WATT["wv"][:, k, :],
                                                   start=(k == 0), stop=(k == KD - 1))
                    dve.wait(pe.done(ins))
                    for i in range(2):
                        two = 4 * g + 2 * half + i not in ACT_KT
                        v_made[g] = bank_free[b] = dve.done(nc.vector.scalar_tensor_tensor(
                            out=U[:, r, 2 * half + i, :, 0:DH],
                            in0=psum[b][:, i * D:(i + 1) * D].rearrange("p (h d) -> p h d", h=H),
                            scalar=2.0 if two else 1.0,
                            in1=ROW[:, int(two), :].rearrange("p (h d) -> p h d", h=H),
                            op0=ALU.mult, op1=ALU.add))

            signs_read = pe.last()
            pe.wait(xt)
            project(0)
            b = take_bank()
            pe.wait(mb)
            for k in range(KD):
                ins = nc.tensor.matmul(psum[b][:, 0:D], MB[:, k, :], WATT["wv"][:, k, :], start=(k == 0), stop=(k == KD - 1))
            dve.wait(pe.done(ins))
            bank_free[b] = dve.done(nc.vector.tensor_tensor(ROW[:, 1, :], psum[b][:, 0:D], BVB, ALU.add))
            dve.wait(bank_free[b])
            dve.wait(dve.done(nc.vector.tensor_tensor(ROW[:, 0, :], BVB, ROW[:, 1, :], ALU.subtract)))
            dve.wait(dve.done(nc.vector.tensor_scalar(ROW[:, 1, :], ROW[:, 0, :], 2.0, None, ALU.mult)))
            row_ready = dve.last()
            project(1)
            for i in range(len(steps) + 2):
                if i < len(steps):
                    turn_rows(i)
                if i < len(steps):
                    take_rows(i)
                if 0 <= i - 1 < len(steps):
                    hidden(i - 1)
                if 0 <= i - 2 < len(steps):
                    score(i - 2)
            rows_read = pe.last()
            dve.wait(z_ready[0], z_ready[1])
            for s in range(2):
                mv = dve.done(nc.vector.bn_aggr(ZMV[:, s, :], ZST[:, s, :, :].rearrange("p c x -> p (c x)")))
            dve.wait(mv)
            if batch == 0:
                following = list(range(TB, NT))
                next_turned["ready"] = scales(following, statistics(following))
            both = dve.done(nc.vector.tensor_tensor(ZS[:, 0:1], ZMV[:, 0, 1:2], ZMV[:, 1, 1:2], ALU.add))
            act.wait(both)
            root = act.done(nc.scalar.activation(ZS[:, 1:2], ZS[:, 0:1], ACT.Sqrt, bias=EPS[0:H, 1:2], scale=0.5))
            dve.wait(root)
            dve.wait(dve.done(nc.vector.reciprocal(ZS[:, 2:3], ZS[:, 1:2])))
            for s in range(2):
                scaled = dve.done(nc.vector.tensor_scalar(Z[:, s, :], Z[:, s, :], ZMV[:, s, 0:1], ZS[:, 2:3],
                                                          ALU.subtract, ALU.mult))
                if s == 0:
                    q_stored = store(zq_rows[batch * H:(batch + 1) * H, :], Z[:, 0, :], scaled, loads.all())
            dve.wait(row_ready)
            values(0)
            values(1)
            pe.wait(scaled)
            for s, M in ((0, QTM), (1, KTM)):
                b = take_bank()
                for t in range(TB):
                    ins = nc.tensor.transpose(psum[b][:, t * H:(t + 1) * H], Z[:, s, t * P:(t + 1) * P], IDENT[0:H, 0:H])
                dve.wait(pe.done(ins), pool.last())
                bank_free[b] = dve.done(nc.vector.tensor_copy(M.rearrange("p t h -> p (t h)"), psum[b][:, 0:TB * H]))
            dve.wait(bank_free[b])
            nkt = dve.done(nc.vector.tensor_scalar(NKT.rearrange("p t h -> p (t h)"), KTM.rearrange("p t h -> p (t h)"),
                                                   -1.0, None, ALU.mult))
            z_read = [pe.last(), q_stored]
            tot = 7
            pe.wait(bank_free[tot])
            parts_done = []
            for g in range(TB // 4):
                r = g % 2
                tt = slice(4 * g, 4 * g + 4)
                pool.wait(v_made[g], nkt)
                nc.gpsimd.tensor_tensor(U[:, r, :, :, DH:2 * DH], U[:, r, :, :, 0:DH],
                                        KTM[:, tt, :].unsqueeze(3).broadcast_to([P, 4, H, DH]), ALU.mult)
                nc.gpsimd.tensor_copy(U[:, r, :, :, 2 * DH], SCH[:, tt, :])
                whole = pool.done(nc.gpsimd.tensor_tensor(U[:, r, :, :, 2 * DH + 1], KTM[:, tt, :], SCH[:, tt, :], ALU.mult))
                pe.wait(whole)
                for i in range(4):
                    t = 4 * g + i
                    weight = ONESF[:, 0:1] if t in ACT_KT else HALF[:, :]
                    ins = nc.tensor.matmul(psum[tot][0:1, :], weight, U[:, r, i, :, 0:2 * DH],
                                           start=(t == 0), stop=(t == TB - 1))
                summed = pe.done(ins)
                u = [U[:, r, 2 * n:2 * n + 2, :, :].rearrange("p t h c -> p (t h) c") for n in range(2)]
                rows = lambda n, m: VOP[:, 4 * g + 2 * n:4 * g + 2 * n + 2, :, m * VC:(m + 1) * VC].rearrange("p t h c -> p (t h) c")
                act.wait(whole, rows_read)
                hi = [act.done(nc.scalar.activation(rows(n, 0), u[n], ACT.Copy)) for n in range(2)]
                rest, mid, u_free[r] = [], [], []
                for n in range(2):
                    dve.wait(hi[n], summed)
                    rest.append(dve.done(nc.vector.tensor_tensor(u[n], u[n], rows(n, 0), ALU.subtract)))
                for n in range(2):
                    act.wait(rest[n])
                    mid.append(act.done(nc.scalar.activation(rows(n, 1), u[n], ACT.Copy)))
                for n in range(2):
                    dve.wait(mid[n])
                    u_free[r].append(dve.done(nc.vector.tensor_tensor(rows(n, 2), u[n], rows(n, 1), ALU.subtract)))
                parts_done += mid + u_free[r]
                if g + 2 < TB // 4:
                    values(g + 2)
            next_turned["xt_free"] = [pe.last(), mb]
            dve.wait(summed)
            bank_free[tot] = dve.done(nc.vector.tensor_copy(TOT, psum[tot][0:1, :]))
            b = take_bank()
            pe.wait(bank_free[tot])
            for h in range(H):
                ins = nc.tensor.matmul(psum[b][0:2 * DH, h:h + 1], TOT[:, h * 2 * DH:(h + 1) * 2 * DH], ONESF[0:1, 0:1],
                                       start=True, stop=True)
            dve.wait(pe.done(ins), cb_zero, act.last())
            bank_free[b] = dve.done(nc.vector.tensor_copy(CB[0:2 * DH, :], psum[b][0:2 * DH, 0:H]))
            return dict(q_stored=q_stored, z_read=z_read, nkt=nkt, parts=parts_done, cb=bank_free[b])

        def spread_q(hh, info):
            last = [sign_made[k] for k in sign_made if hh - 2 >= 0 and k // TB == hh - 2]
            act_dve = last + (info["z_read"] if hh % H < 2 else [])
            qb_ready[hh] = load(QB[:, hh % 2, :], zq_rows[hh, :].partition_broadcast(P), info["q_stored"], act_dve)

        def sign_tile(hh, kt, info):
            g = hh * TB + kt
            h = hh % H
            after = [qb_ready[hh], pe_tile.get(g - RING)]
            if kt in ACT_KT:
                act.wait(after, info["nkt"], info["parts"])
                sign_made[g] = act.done(nc.scalar.activation(SG[:, g % RING, :], QB[:, hh % 2, :], ACT.Sign,
                                                             bias=NKT[:, kt, h:h + 1]))
            else:
                dve.wait(after, info["nkt"], info["parts"])
                sign_made[g] = dve.done(nc.vector.tensor_scalar(SG[:, g % RING, :], QB[:, hh % 2, :], KTM[:, kt, h:h + 1],
                                                                0.5, ALU.is_gt, ALU.subtract))

        def accumulate(hh, kt, chunks, info):
            g = hh * TB + kt
            pe.wait(sign_made[g], info["parts"])
            for c in chunks:
                b = bank_of(hh, c)
                if kt == 0:
                    pe.wait(bank_free[b])
                ins = nc.tensor.matmul(psum[b][0:VP, :], VOP[:, kt, hh % H, :], SG[:, g % RING, c * BANK:(c + 1) * BANK],
                                       start=(kt == 0), stop=(kt == TB - 1))
            if chunks[-1] == 3:
                pe_tile[g] = pe.done(ins)

        def evacuate(hh, info):
            for c in range(4):
                b = bank_of(hh, c)
                act.wait(pe_tile[hh * TB + TB - 1], os_free[0], info["cb"])
                evac[hh, c] = bank_free[b] = act.done(nc.scalar.activation(
                    OS[0:VP, c * BANK:(c + 1) * BANK], psum[b][0:VP, :], ACT.Identity, bias=CB[:, hh % H:hh % H + 1]))

        turned, summed = {}, {}

        def turn_back(hh, c):
            b = 6 + c % 2
            pe.wait(evac[hh, c], bank_free[b])
            for i in range(4):
                ins = nc.tensor.transpose(psum[b][:, i * VP:(i + 1) * VP], OS[0:VP, (4 * c + i) * P:(4 * c + i + 1) * P],
                                          IDENT[0:VP, 0:VP])
            turned[hh, c] = pe.done(ins)
            if c == 3:
                os_free[0] = turned[hh, c]

        def sum_parts(hh, c):
            b = 6 + c % 2
            dve.wait(turned[hh, c], a_free[hh % 2])
            summed[hh, c] = bank_free[b] = dve.done(nc.vector.tensor_reduce(
                A[:, hh % 2, 4 * c:4 * c + 4, :],
                psum[b][:, 0:4 * VP].rearrange("p (i n c) -> p i c n", i=4, n=3), AX_X, ALU.add))

        norm = {}

        def norm_first(hh):
            r = hh % 2
            pool.wait(summed[hh, 3])
            q = QTM[:, :, hh % H]
            pool.wait(pool.done(nc.gpsimd.tensor_tensor(N1[:, r, :], A[:, r, :, 2 * DH], q, ALU.mult)))
            norm[hh] = pool.done(nc.gpsimd.tensor_tensor(N2[:, r, :], N1[:, r, :], A[:, r, :, 2 * DH + 1], ALU.subtract))
            pool.wait(pool.done(nc.gpsimd.tensor_tensor(CT, A[:, r, :, 0:DH], q.unsqueeze(2).broadcast_to([P, TB, DH]),
                                                        ALU.mult)))
            pool.wait(pool.done(nc.gpsimd.tensor_tensor(CT, CT, A[:, r, :, DH:2 * DH], ALU.subtract)))

        def norm_second(hh):
            r = hh % 2
            dve.wait(norm[hh])
            dve.wait(dve.done(nc.vector.tensor_scalar(N2[:, r, :], N2[:, r, :], NORM_MIN, None, ALU.max)))
            norm[hh] = dve.done(nc.vector.reciprocal(N1[:, r, :], N2[:, r, :]))

        def add_context(hh):
            r, batch, h = hh % 2, hh // H, hh % H
            pool.wait(norm[hh])
            pool.wait(pool.done(nc.gpsimd.tensor_tensor(CT, CT, N1[:, r, :].unsqueeze(2).broadcast_to([P, TB, DH]), ALU.mult)))
            x = X[:, batch * TB:(batch + 1) * TB, h * DH:(h + 1) * DH]
            a_free[r] = [pool.done(nc.gpsimd.tensor_tensor(x, x, CT, ALU.add))]
            pool.wait(a_free[r])

        def after_head(hh, kt):
            if kt in (6, 8, 10, 12):
                turn_back(hh, (kt - 6) // 2)
            if kt in (7, 9, 11, 13):
                sum_parts(hh, (kt - 7) // 2)
            if kt == 13:
                norm_first(hh)
            if kt == 15:
                norm_second(hh)
                add_context(hh)

        for batch in range(B):
            info = prepare(batch)
            if batch == 0 and "moe0" in PHASES[PHASES.index("attn"):]:
                empty_slots()
            heads = range(batch * H, (batch + 1) * H)
            spread_q(heads[0], info)
            for hh in heads:
                for kt in range(AHEAD):
                    sign_tile(hh, kt, info)
                if hh > heads[0]:
                    evacuate(hh - 1, info)
                if hh + 1 in heads:
                    spread_q(hh + 1, info)
                for chunks in ((0, 1), (2, 3)):
                    for kt in range(3):
                        accumulate(hh, kt, chunks, info)
                for kt in range(3, TB):
                    if kt - 3 + AHEAD < TB:
                        sign_tile(hh, kt - 3 + AHEAD, info)
                    accumulate(hh, kt, (0, 1, 2, 3), info)
                    if hh > heads[0]:
                        after_head(hh - 1, kt)
                    if kt in (3, 5):
                        turn_next((kt - 3) // 2, hh)
            evacuate(heads[-1], info)
            for kt in range(TB):
                after_head(heads[-1], kt)
            for t in range(batch * TB, (batch + 1) * TB):
                x_ready[t] = pool.last()
        st["xn_free"] = [pe.last(), act.last()]

    def mixer():
        part = renew(STAGE_FLOATS - KEPT)
        r2 = 2
        tc = BANK // P
        n_chunks, per_batch = T // BANK, S // BANK
        ring = lambda n: part(r2 * KD * n).rearrange("p (r k n) -> p r k n", r=r2, k=KD)
        XT = ring(BANK + 1)
        OLD, INP, HT, STATE = ring(BANK), ring(BANK), ring(BANK), ring(BANK)
        WIN = part(KD * D).rearrange("p (k n) -> p k n", k=KD)
        WOUT = part(KD * D).rearrange("p (k n) -> p k n", k=KD)
        BIN = part(KD)
        BOUT = part(D)
        SCAL = part(3)
        TMPO = part(2 * 2 * D).rearrange("p (r i d) -> p r i d", r=2, i=2)
        free = st["arena_free"]
        wt = [load(WIN, a["win_t"].rearrange("(k p) n -> p k n", p=P), free),
              load(WOUT, a["wout_t"].rearrange("(k p) n -> p k n", p=P), free),
              load(BIN, a["bin"], free),
              load(BOUT, a["bout"].partition_broadcast(P), free),
              load(SCAL[:, 0:1], a["decay"].partition_broadcast(P), free),
              load(SCAL[:, 1:2], a["mix"].partition_broadcast(P), free)]
        pool.wait(wt)
        scal = pool.done(nc.gpsimd.tensor_scalar(SCAL[:, 2:3], SCAL[:, 1:2], -1.0, 1.0, ALU.mult, ALU.add))
        xt_free, old_free, inp_free, ht_free, state_free = ([None] * r2 for _ in range(5))
        tmp_free = [None] * 2
        turned, xt_ready, state_ready, edge = {}, {}, {}, {}

        def dest(t):
            act.wait(st["xtr_free"][t // 2 % 3])
            return LNR[:, t // 2 % 3, t % 2, :]

        normed = layernorm(list(range(NT)), dest)

        def turn(c):
            for pair in range(c * tc // 2, (c + 1) * tc // 2):
                for _ in range(2):
                    _, tick = next(normed)
                b = take_bank(range(8))
                pe.wait(tick, consts)
                for i in range(2):
                    for k in range(KD):
                        ins = nc.tensor.transpose(psum[b][:, (2 * k + i) * P:(2 * k + i + 1) * P],
                                                  LNR[:, pair % 3, i, k * P:(k + 1) * P], IDENT[:, :])
                st["xtr_free"][pair % 3] = pe.done(ins)
                turned[pair] = b, pe.last()

        def take_turned(c):
            r = c % r2
            act.wait(xt_free[r], free)
            if c % per_batch:
                act.wait(xt_ready[c - 1])
                edge[c] = act.done(nc.scalar.activation(XT[:, r, :, 0], XT[:, 1 - r, :, BANK], ACT.Copy))
            else:
                pool.wait(xt_free[r])
                edge[c] = pool.done(nc.gpsimd.memset(XT[:, r, :, 0], 0.0))
            for n in range(tc // 2):
                b, tick = turned[c * tc // 2 + n]
                act.wait(tick)
                xt_ready[c] = bank_free[b] = act.done(nc.scalar.activation(
                    XT[:, r, :, 1 + 2 * n * P:1 + 2 * (n + 1) * P], psum[b][:, :].rearrange("p (k c) -> p k c", k=KD), ACT.Copy))

        def mix(c):
            r = c % r2
            act.wait(old_free[r], scal, edge[c], xt_ready[c])
            old = act.done(nc.scalar.activation(OLD[:, r, :, :], XT[:, r, :, 0:BANK], ACT.Copy, scale=SCAL[:, 2:3]))
            dve.wait(old, inp_free[r])
            old_free[r] = dve.done(nc.vector.scalar_tensor_tensor(
                out=INP[:, r, :, :], in0=XT[:, r, :, 1:BANK + 1], scalar=SCAL[:, 1:2], in1=OLD[:, r, :, :],
                op0=ALU.mult, op1=ALU.add))
            xt_free[r] = [old_free[r], old, edge.get(c + 1)]

        def scan(c):
            r = c % r2
            pe.wait(old_free[r], wt)
            scanned = []
            for m in range(KD):
                b = take_bank(range(8))
                for k in range(KD):
                    ins = nc.tensor.matmul(psum[b][:, :], WIN[:, k, m * P:(m + 1) * P], INP[:, r, k, :],
                                           start=(k == 0), stop=(k == KD - 1))
                act.wait(pe.done(ins), ht_free[r])
                bank_free[b] = act.done(nc.scalar.activation(HT[:, r, m, :], psum[b][:, :], ACT.Relu, bias=BIN[:, m:m + 1]))
                before = STATE[:, 1 - r, m, BANK - 1:BANK] if c % per_batch else 0.0
                dve.wait(bank_free[b], state_free[r], state_ready.get(c - 1))
                scanned.append(dve.done(nc.vector.tensor_tensor_scan(
                    STATE[:, r, m, :], SCAL[:, 0:1].broadcast_to([P, BANK]), HT[:, r, m, :], before, ALU.mult, ALU.add)))
            inp_free[r] = pe.last()
            ht_free[r] = state_ready[c] = scanned[-1]

        def put(c):
            r = c % r2
            pe.wait(state_ready[c])
            for n in range(tc // 2):
                b = take_bank(range(8))
                for i in range(2):
                    for k in range(KD):
                        ins = nc.tensor.matmul(psum[b][:, i * D:(i + 1) * D], STATE[:, r, k, (2 * n + i) * P:(2 * n + i + 1) * P],
                                               WOUT[:, k, :], start=(k == 0), stop=(k == KD - 1))
                t = c * tc + 2 * n
                o = t // 2 % 2
                dve.wait(pe.done(ins), tmp_free[o])
                bank_free[b] = dve.done(nc.vector.tensor_tensor(
                    TMPO[:, o, :, :], psum[b][:, :].rearrange("p (i d) -> p i d", i=2),
                    BOUT.unsqueeze(1).broadcast_to([P, 2, D]), ALU.add))
                pool.wait(bank_free[b])
                tmp_free[o] = pool.done(nc.gpsimd.tensor_tensor(X[:, t:t + 2, :], X[:, t:t + 2, :], TMPO[:, o, :, :], ALU.add))
                x_ready[t] = x_ready[t + 1] = tmp_free[o]
            state_free[r] = pe.last()

        for c in range(n_chunks + 2):
            if c < n_chunks:
                turn(c)
                take_turned(c)
            if 0 <= c - 1 < n_chunks:
                scan(c - 1)
            if c < n_chunks:
                mix(c)
            if 0 <= c - 2:
                put(c - 2)
        st["xn_free"] = [x for x in x_ready]

    for n, phase in enumerate(PHASES):
        if phase == "moe0":
            before_moe1 = PHASES[n + 1] == "moe1"
            if before_moe1:
                keep_weights1()
            moe0(before_moe1)
        elif phase == "moe1":
            moe1(n == len(PHASES) - 1)
        else:
            {"attn": attention, "mixer": mixer}[phase]()
        st["arena_free"] = everything()

    sp.wait(stores.all(), loads.all())
    pool.wait(scatters.all(), gathers.all())


def kernel(**inputs):
    import concourse.bacc as bacc
    from concourse.bass_utils import run_bass_kernel_spmd

    given = {n: np.asarray(v) for n, v in inputs.items()}
    column = lambda v: np.ascontiguousarray(v.reshape(KD, P).T)
    arrays = {
        "x": given["L0_attn_hidden_states"].reshape(T, D),
        "wg0": given["L0_ffn_wg"], "w0t": np.ascontiguousarray(given["L0_ffn_W"].transpose(0, 2, 1)),
        "b0": given["L0_ffn_b"],
        "wq": given["L0_attn_Wq"], "wk": given["L0_attn_Wk"], "wv": given["L0_attn_Wv"], "wp1": given["L0_attn_W1"],
        "wp2": given["L0_attn_W2"], "bq": given["L0_attn_bq"], "bk": given["L0_attn_bk"],
        "bp1": column(given["L0_attn_b1"]), "bp2": given["L0_attn_b2"].reshape(H, 1), "bv": given["L0_attn_bv"],
        "wg1": given["L1_ffn_Wg"], "bg1": given["L1_ffn_bg"], "w1": given["L1_ffn_W1"], "w2": given["L1_ffn_W2"],
        "b1": given["L1_ffn_b1"].reshape(1, E * D), "b2": given["L1_ffn_b2"].reshape(1, E * D),
        "win_t": np.ascontiguousarray(given["L1_attn_W_in"].T), "bin": column(given["L1_attn_b_in"]),
        "wout_t": np.ascontiguousarray(given["L1_attn_W_out"].T), "bout": given["L1_attn_b_out"],
        "decay": given["L1_attn_decay"].reshape(1), "mix": given["L1_attn_mix"].reshape(1),
    }
    nc = bacc.Bacc("TRN2", target_bir_lowering=False, num_devices=1)
    arrays = {n: np.ascontiguousarray(v) for n, v in arrays.items()}
    aps = {n: nc.dram_tensor("in_" + n, v.shape, mybir.dt.from_np(v.dtype), kind="ExternalInput").ap()
           for n, v in arrays.items()}
    out = nc.dram_tensor("out_tokens", [T + NJ1 * P, D], F32, kind="ExternalOutput").ap()
    program(nc, aps, out)
    r = run_bass_kernel_spmd(nc, [{"in_" + n: v for n, v in arrays.items()}], core_ids=[0])
    return r.results[0]["out_tokens"][:T].reshape(B, S, D)
```
